# Optimizing a Trainium2 kernel written in Bass

```python
import numpy as np
import jax
import jax.numpy as jnp

def _softmax(x, axis=-1):
    return jax.nn.softmax(x, axis=axis)

def _gelu(x):
    return jax.nn.gelu(x, approximate=True)

def _silu(x):
    return jax.nn.silu(x)

def _sigmoid(x):
    return jax.nn.sigmoid(x)

def _layernorm(x, axis=-1, eps=1e-05):
    m = jnp.mean(x, axis=axis, keepdims=True)
    v = jnp.var(x, axis=axis, keepdims=True)
    return (x - m) / jnp.sqrt(v + eps)

def _scatter_add(tgt, idx, src, axis=0):
    return tgt.at[idx].add(src)

def _segment_sum(src, seg, n):
    return jax.ops.segment_sum(src, seg, n)
kernel_name = 'mk_early_fusion_d1_tok_img1024_r4_3ef7e2'

def setup_inputs(seed: int=0):
    np.random.seed(seed)
    _w = jnp.asarray

    def _rec_inputs():
        import jax
        import jax.numpy as jnp
        _rk = jax.random.key(seed)
        x = 7.22013e-05 + 1.00017 * jax.random.normal(jax.random.fold_in(_rk, 1), (4, 1, 512, 256), jnp.float32)
        txt = 1.55315e-05 + 0.0209517 * jax.random.normal(jax.random.fold_in(_rk, 2), (4, 32, 256), jnp.float32)
        return (x, txt)
    x, txt = _rec_inputs()

    def _L0_tok_setup():
        import jax, jax.numpy as jnp
        import numpy as np
        import math
        EMBED_DIM = 256
        NUM_HEADS = 16
        HEAD_DIM = EMBED_DIM // NUM_HEADS
        INPUT_DIM = 256
        key = jax.random.key(seed)
        k_x, k_wqkv, k_wout = jax.random.split(key, 3)
        x = jax.random.normal(k_x, (4, 1, 512, INPUT_DIM), dtype=jnp.float32)

        def xavier(k, shape):
            fan_out, fan_in = shape
            bound = math.sqrt(6.0 / (fan_in + fan_out))
            return jax.random.uniform(k, shape, jnp.float32, -bound, bound)
        w_qkv = xavier(k_wqkv, (3 * EMBED_DIM, INPUT_DIM))
        b_qkv = jnp.zeros((3 * EMBED_DIM,), jnp.float32)
        w_out = xavier(k_wout, (EMBED_DIM, EMBED_DIM))
        b_out = jnp.zeros((EMBED_DIM,), jnp.float32)
        return {'x': x, 'w_qkv': w_qkv, 'b_qkv': b_qkv, 'w_out': w_out, 'b_out': b_out}
    _L0_tok_all = _L0_tok_setup()
    _L0_tok_in = {k: v for k, v in _L0_tok_all.items() if k in ('w_qkv', 'b_qkv', 'w_out', 'b_out')}
    del _L0_tok_all

    def _L0_attn_setup():
        import jax, jax.numpy as jnp
        import numpy as np
        EMBED_DIM = 256
        NUM_HEAD = 16
        NEG_BIG = 10000000000.0
        key = jax.random.key(seed)
        k_x, k_w1, k_b1, k_w2, k_b2 = jax.random.split(key, 5)
        B, S, E = (4, 512, EMBED_DIM)
        std = 1.0 / np.sqrt(E)
        return {'x': jax.random.normal(k_x, (B, S, E), dtype=jnp.float32), 'W1': jax.random.uniform(k_w1, (E, 3 * E), dtype=jnp.float32, minval=-std, maxval=std), 'b1': jax.random.uniform(k_b1, (3 * E,), dtype=jnp.float32, minval=-std, maxval=std), 'W2': jax.random.uniform(k_w2, (E, E), dtype=jnp.float32, minval=-std, maxval=std), 'b2': jax.random.uniform(k_b2, (E,), dtype=jnp.float32, minval=-std, maxval=std)}
    _L0_attn_all = _L0_attn_setup()
    _L0_attn_in = {k: v for k, v in _L0_attn_all.items() if k in ('W1', 'b1', 'W2', 'b2')}
    del _L0_attn_all

    def _L0_ffn_setup():
        import jax, jax.numpy as jnp
        import numpy as np
        E, K, H, I, SI = (32, 8, 256, 128, 512)
        CAP = 512
        LIMIT = 7.0
        SCALE = 2.5
        B, S = (2, 512)
        key = jax.random.key(seed)
        ks = jax.random.split(key, 8)
        s = 0.02
        return {'hidden_states': jax.random.normal(ks[0], (B, S, H), jnp.float32), 'router_weight': jax.random.normal(ks[1], (E, H), jnp.float32) * s, 'e_score_correction_bias': jnp.zeros((E,), jnp.float32), 'gate_up_proj': jax.random.normal(ks[2], (E, 2 * I, H), jnp.float32) * s, 'down_proj': jax.random.normal(ks[3], (E, H, I), jnp.float32) * s, 'shared_gate': jax.random.normal(ks[4], (SI, H), jnp.float32) * s, 'shared_up': jax.random.normal(ks[5], (SI, H), jnp.float32) * s, 'shared_down': jax.random.normal(ks[6], (H, SI), jnp.float32) * s}
    _L0_ffn_all = _L0_ffn_setup()
    _L0_ffn_in = {k: v for k, v in _L0_ffn_all.items() if k in ('router_weight', 'e_score_correction_bias', 'gate_up_proj', 'down_proj', 'shared_gate', 'shared_up', 'shared_down')}
    del _L0_ffn_all
    return {'x': x, 'txt': txt, 'L0_tok_w_qkv': _L0_tok_in['w_qkv'], 'L0_tok_b_qkv': _L0_tok_in['b_qkv'], 'L0_tok_w_out': _L0_tok_in['w_out'], 'L0_tok_b_out': _L0_tok_in['b_out'], 'L0_attn_W1': _L0_attn_in['W1'], 'L0_attn_b1': _L0_attn_in['b1'], 'L0_attn_W2': _L0_attn_in['W2'], 'L0_attn_b2': _L0_attn_in['b2'], 'L0_ffn_router_weight': _L0_ffn_in['router_weight'], 'L0_ffn_e_score_correction_bias': _L0_ffn_in['e_score_correction_bias'], 'L0_ffn_gate_up_proj': _L0_ffn_in['gate_up_proj'], 'L0_ffn_down_proj': _L0_ffn_in['down_proj'], 'L0_ffn_shared_gate': _L0_ffn_in['shared_gate'], 'L0_ffn_shared_up': _L0_ffn_in['shared_up'], 'L0_ffn_shared_down': _L0_ffn_in['shared_down']}

def reference(x, txt, L0_tok_w_qkv, L0_tok_b_qkv, L0_tok_w_out, L0_tok_b_out, L0_attn_W1, L0_attn_b1, L0_attn_W2, L0_attn_b2, L0_ffn_router_weight, L0_ffn_e_score_correction_bias, L0_ffn_gate_up_proj, L0_ffn_down_proj, L0_ffn_shared_gate, L0_ffn_shared_up, L0_ffn_shared_down):
    import jax
    import jax.numpy as jnp

    def _L0_tok_ref(x, w_qkv, b_qkv, w_out, b_out):
        import jax, jax.numpy as jnp
        import numpy as np
        import math
        EMBED_DIM = 256
        NUM_HEADS = 16
        HEAD_DIM = EMBED_DIM // NUM_HEADS
        INPUT_DIM = 256
        B, y, S, _ = x.shape
        qkv = jnp.einsum('bysd,ed->byse', x, w_qkv) + b_qkv
        qkv = qkv.reshape(B, S, NUM_HEADS, 3 * HEAD_DIM).transpose(0, 2, 1, 3)
        q, k, v = jnp.split(qkv, 3, axis=-1)
        logits = jnp.einsum('bhqd,bhkd->bhqk', q, k) / math.sqrt(HEAD_DIM)
        attn = jax.nn.softmax(logits, axis=-1)
        vals = jnp.einsum('bhqk,bhkd->bhqd', attn, v)
        vals = vals.transpose(0, 2, 1, 3).reshape(B, S, EMBED_DIM)
        return jnp.einsum('bse,oe->bso', vals, w_out) + b_out

    def _L0_attn_ref(x, W1, b1, W2, b2):
        import jax, jax.numpy as jnp
        import numpy as np
        EMBED_DIM = 256
        NUM_HEAD = 16
        NEG_BIG = 10000000000.0
        B, S, E = x.shape
        H = NUM_HEAD
        y = jnp.einsum('bse,ef->bsf', x, W1) + b1
        y = y.reshape(B, S, H, -1).transpose(0, 2, 1, 3)
        q, k, v = jnp.split(y, 3, axis=-1)
        dk = jnp.asarray(v.shape[-1], x.dtype) ** 0.5
        w = jnp.einsum('bhqd,bhkd->bhqk', q, k) / dk
        mask = jnp.tril(jnp.ones((S, S), dtype=x.dtype))
        w = w * mask - NEG_BIG * (1.0 - mask)
        w = jax.nn.softmax(w, axis=-1)
        attn = jnp.einsum('bhqk,bhkd->bhqd', w, v)
        attn = attn.transpose(0, 2, 1, 3).reshape(B, S, E)
        return jnp.einsum('bse,ef->bsf', attn, W2) + b2

    def _L0_ffn_ref(hidden_states, router_weight, e_score_correction_bias, gate_up_proj, down_proj, shared_gate, shared_up, shared_down):
        import jax, jax.numpy as jnp
        import numpy as np
        E, K, H, I, SI = (32, 8, 256, 128, 512)
        CAP = 512
        LIMIT = 7.0
        SCALE = 2.5
        B, S = (2, 512)
        b, s, _ = hidden_states.shape
        T = b * s
        x = hidden_states.reshape(T, H)
        logits = x.astype(jnp.float32) @ router_weight.astype(jnp.float32).T
        scores = jax.nn.sigmoid(logits)
        _, idx = jax.lax.top_k(scores + e_score_correction_bias, K)
        w = jnp.take_along_axis(scores, idx, axis=1)
        w = w / (w.sum(-1, keepdims=True) + 1e-20) * SCALE
        e_flat = idx.reshape(-1)
        onehot = jax.nn.one_hot(e_flat, E, dtype=jnp.int32)
        pos = jnp.cumsum(onehot, axis=0) - onehot
        pos = jnp.take_along_axis(pos, e_flat[:, None], axis=1)[:, 0]
        keep = pos < CAP
        slot = jnp.where(keep, e_flat * CAP + pos, E * CAP)
        tok = jnp.arange(T * K) // K
        buf = jnp.zeros((E * CAP + 1, H), x.dtype).at[slot].set(x[tok])
        xe = buf[:E * CAP].reshape(E, CAP, H)
        gu = jnp.einsum('ech,eoh->eco', xe, gate_up_proj)
        g, u = (gu[..., :I], gu[..., I:])
        g = jnp.minimum(g, LIMIT)
        u = jnp.clip(u, -LIMIT, LIMIT)
        h = jax.nn.silu(g) * u
        ye = jnp.einsum('eci,ehi->ech', h, down_proj)
        yp = ye.reshape(E * CAP, H)[jnp.minimum(slot, E * CAP - 1)]
        yp = jnp.where(keep[:, None], yp, 0.0) * w.reshape(-1)[:, None]
        routed = jax.ops.segment_sum(yp, tok, num_segments=T).reshape(b, s, H)
        shared = jax.nn.silu(hidden_states @ shared_gate.T) * (hidden_states @ shared_up.T) @ shared_down.T
        return routed + shared
    h = _L0_tok_ref(x, L0_tok_w_qkv, L0_tok_b_qkv, L0_tok_w_out, L0_tok_b_out)
    h = jnp.concatenate([h, txt], axis=1)
    h = h + _L0_attn_ref(_layernorm(h, axis=-1), L0_attn_W1, L0_attn_b1, L0_attn_W2, L0_attn_b2)
    h = h + _L0_ffn_ref(_layernorm(h, axis=-1), L0_ffn_router_weight, L0_ffn_e_score_correction_bias, L0_ffn_gate_up_proj, L0_ffn_down_proj, L0_ffn_shared_gate, L0_ffn_shared_up, L0_ffn_shared_down)
    return h

_drawn_inputs = setup_inputs


def setup_inputs(seed=0):
    import zlib

    import numpy as np

    out = dict(_drawn_inputs(seed))
    spreads = {'L0_tok_b_qkv': (0.0, 0.1),
     'L0_tok_b_out': (0.0, 0.1),
     'L0_ffn_e_score_correction_bias': (0.0, 0.559)}
    factors = {'txt': 3.6,
     'L0_ffn_router_weight': 4.057,
     'L0_ffn_gate_up_proj': 3.313,
     'L0_ffn_down_proj': 3.445}
    for name, (base, spread) in spreads.items():
        noise = np.random.default_rng([zlib.crc32(name.encode()), seed]).standard_normal(out[name].shape)
        drawn = base * np.exp(spread * noise) if base else spread * noise
        out[name] = jnp.asarray(drawn.astype(out[name].dtype))
    for name, factor in factors.items():
        out[name] = (out[name] * factor).astype(out[name].dtype)
    return out
```

```python
from contextlib import ExitStack

import concourse.bass as bass
from concourse import mybir

ALU = mybir.AluOpType
ACT = mybir.ActivationFunctionType
AX = mybir.AxisListType
F32 = mybir.dt.float32
BF16 = mybir.dt.bfloat16
I32 = mybir.dt.int32
U32 = mybir.dt.uint32

P = 128
NB, S_IMG, S_TXT, D = 4, 512, 32, 256
S_ALL = S_IMG + S_TXT
T_ALL = NB * S_ALL
NT = T_ALL // P
HEADS, HD = 16, 16
GROUPS, GH = 4, 4
KC = D // P
PARTS = 3
STACK = 6 * HD
E, TOPK, INTER, SHARED, CAP = 32, 8, 128, 512, 512
LIMIT, ROUTE_SCALE, LN_EPS = 7.0, 2.5, 1e-5
CT = CAP // P
SCALE = HD ** -0.5


class Turns:

    def __init__(self, names, first=0):
        self.at = {n: i for i, n in enumerate(names)}
        self.per = len(names)
        self.first = first

    def after(self, b, name):
        return b * self.per + (self.first + self.at[name] + 1)


def attention_layer(nc, tag, causal, xT, w_qk, b_qk, w_v, b_v, w_o, b_o, consts, qk_dram, residual, y_dram):
    S = S_ALL if causal else S_IMG
    TAIL = S - S_IMG
    KT = S_IMG // P
    ctx = ExitStack()
    with ctx:
        def sb(name, shape, dt):
            return ctx.enter_context(nc.sbuf_tensor(f"{tag}_{name}", shape, dt))

        def ps(name, shape, dt):
            return ctx.enter_context(nc.psum_tensor(f"{tag}_{name}", shape, dt))

        def sem(name):
            return ctx.enter_context(nc.semaphore(f"{tag}_{name}"))

        wqk = sb("wqk", [P, KC, 2 * D], F32)
        bqk = sb("bqk", [P, 4], F32)
        wv = sb("wv", [P, KC, D], F32)
        bv = sb("bv", [P, D], F32)
        wo = sb("wo", [P, GROUPS, D], F32)
        bo = sb("bo", [P, D], F32)
        ident_bf = sb("ident_bf", [P, P], BF16)
        sel = sb("sel", [P, P], F32)
        mask_q = sb("mask_q", [P, P], BF16)
        mask_k = sb("mask_k", [P, P], BF16)
        mask_qt = sb("mask_qt", [P, S_TXT], BF16)
        xb = sb("xb", [P, KC, S], F32)
        q_stack = sb("q_stack", [P, GROUPS, GH, S], BF16)
        k_stack = sb("k_stack", [P, GROUPS, GH, S], BF16)
        qk_full = sb("qk_full", [P, 4, S], F32)
        qk_rest = sb("qk_rest", [P, 4, S], F32)
        qk_part = sb("qk_part", [P, 4, PARTS, S], BF16)
        VT = KT + (1 if causal else 0)
        v_ones = sb("v_ones", [P, VT, GROUPS, GH, 32], F32)
        probs = sb("probs", [P, 4, 2 * S_IMG], F32)
        probs_t = sb("probs_t", [P, 5 * P], F32)
        neg_max = sb("neg_max", [P, 2, KT, GH], F32)
        max_part = sb("max_part", [P, 2, KT, 2, GH], BF16)
        neg_max_t = sb("neg_max_t", [P, 2, 3], F32)
        max_part_t = sb("max_part_t", [P, 2, 2], BF16)
        max_rows = sb("max_rows", [2 * GH, 2, S_IMG], BF16)
        max_rows_t = sb("max_rows_t", [2, 2, P], BF16)
        o_raw = sb("o_raw", [P, 2, S], F32)
        o_inv = sb("o_inv", [P, 2, S], F32)
        o_all = sb("o_all", [P, GROUPS, NB * S], F32)
        o_tile = sb("o_tile", [P, 2, GROUPS, P], F32)
        res = sb("res", [P, 2, D], F32)
        y_tile = sb("y_tile", [P, 2, D], F32)

        mx = [ps(f"mx{i}", [P, 512], F32) for i in range(2)]
        sc = [ps(f"sc{i}", [P, 2, 512], F32) for i in range(2)]
        ob = ps("ob", [P, 512], F32)
        ms = ps("ms", [P, 512], F32)
        ms_bf = ms[:, :].bitcast(BF16)

        if causal:
            max_units = [(0, (0, 1, 2, 3)), (1, (0, 1)), (1, (2, 3))] + \
                [(i, (h,)) for i in (2, 3) for h in range(GH)] + [("t", 0), ("t", 1)]
            score_units = [(0, (0, 1)), (0, (2, 3)), (1, (0, 1)), (1, (2, 3)), (2, (0, 1, 2, 3)),
                           (3, (0, 1, 2, 3)), ("t", ())]
        else:
            max_units = [(i, (h,)) for i in range(KT) for h in range(GH)]
            score_units = [(j, hs) for j in range(KT) for hs in ((0, 1), (2, 3))]
        MU, SU = len(max_units), len(score_units)
        NAV = SU - (1 if TAIL else 0)

        def proj_turns():
            return (["qt"] if TAIL else []) + [("qk", m) for m in range(4)]

        v_turns = [("v", t) for t in range(VT)]
        order = []
        for step in (("tr", 0), ("tr", 1), ("ot", 0), ("tr", 2), ("se", 0), ("ot", 1), "QK", ("tr", 3),
                     ("se", 1), ("ot", 2), ("se", 2), ("ot", 3), ("se", 3), "V"):
            if step == "QK":
                order += proj_turns()
            elif step == "V":
                order += v_turns
            elif step[0] == "ot":
                order += [step] if TAIL else []
            elif step[0] == "se":
                order += [step] + ([("st", step[1])] if TAIL else [])
            else:
                order.append(step)
        first = proj_turns() + v_turns
        MS0 = Turns(first)
        MS = Turns(order, first=len(first))
        MSL = Turns([x for x in order if x not in first], first=len(first) + (NB - 1) * len(order))

        def ms_turn(b, name, last):
            return MSL.after(0, name) if last else MS.after(b, name)

        s_const = sem("constants_loaded")
        s_preset = sem("presets_done")
        s_xb = sem("x_loaded")
        s_stack = [sem(f"stack{g}_loaded") for g in range(GROUPS)]
        s_mrow = [sem(f"max_rows{g}_loaded") for g in range(GROUPS)]
        s_qk_stored = sem("qk_stored")
        s_mx_ready = sem("max_scores_ready")
        s_mx_free = sem("max_banks_free")
        s_sc_ready = sem("scores_ready")
        s_exp = sem("exps_done")
        s_av_done = sem("probs_used")
        s_o_read = sem("o_read")
        s_ms_ready = sem("misc_bank_ready")
        s_ms_free = sem("misc_bank_free")
        s_negmax = sem("neg_max_done")
        s_negt = sem("neg_max_tail_done")
        s_mhigh = sem("max_high_done")
        s_mpart = sem("max_parts_done")
        s_full = sem("qk_full_ready")
        s_high = sem("qk_high_ready")
        s_rest = sem("qk_rest_ready")
        s_mid = sem("qk_mid_ready")
        s_low = sem("qk_low_ready")
        s_norm = sem("o_normalized")
        s_tile_in = sem("o_tile_ready")
        s_y_bank = sem("y_bank_ready")
        s_y = sem("y_ready")
        s_sum = sem("y_summed")
        s_res = [sem(f"residual_loaded{i}") for i in range(2)]
        s_out = [sem(f"rows_stored{i}") for i in range(2)]

        block = ctx.enter_context(nc.Block())

        def batches(eng, body):
            with eng.Fori(0, NB - 1) as b:
                body(b, False)
            body(NB - 1, True)

        @block.sync
        def _(sp):
            n = 0
            for dst, src in ((wqk, w_qk), (bqk, b_qk), (wv, w_v), (bv, b_v), (wo, w_o), (bo, b_o),
                             (ident_bf, consts["ident_bf"]), (sel, consts["sel"]), (mask_q, consts["mask_q"]),
                             (mask_k, consts["mask_k"]), (mask_qt, consts["mask_qt"])):
                sp.dma_start(dst[:], src).then_inc(s_const, 16)
                n += 1
            assert n == 11

            def load_x(b):
                sp.dma_start(xb[:], xT.rearrange("(c p) t -> p c t", p=P)[:, :, bass.ds(b * S, S)]).then_inc(s_xb, 16)

            def store_parts(b):
                for m in range(4):
                    sp.wait_ge(s_low, b * 4 + m + 1)
                    for half in range(2):
                        g = 2 * (m % 2) + half
                        sp.dma_start(qk_dram[m // 2, b, g].rearrange("c p t -> p c t"),
                                     qk_part[64 * half:64 * half + 64, m, :, :]).then_inc(s_qk_stored, 16)

            def load_stack(b, g):
                q = qk_dram[0, b, g].rearrange("c (h d) t -> c d h t", h=GH)
                k = qk_dram[1, b, g].rearrange("c (h d) t -> c d h t", h=GH)
                for j, (qp, kp) in enumerate(((0, 0), (1, 0), (2, 0), (0, 1), (1, 1), (0, 2))):
                    r = slice(HD * j, HD * j + HD)
                    sp.dma_start(q_stack[r, g], q[qp]).then_inc(s_stack[g], 16)
                    sp.dma_start(k_stack[r, g], k[kp]).then_inc(s_stack[g], 16)

            load_x(0)
            store_parts(0)
            sp.wait_ge(s_qk_stored, 16 * 8)
            for g in range(GROUPS):
                load_stack(0, g)

            def body(b, last):
                def rows(g):
                    sp.wait_ge(s_ms_free, ms_turn(b, ("tr", g), last) + 1)
                    for part in range(2):
                        sp.dma_start(q_stack[STACK + part:STACK + part + 1, g, :, 0:S_IMG],
                                     max_rows[GH * part:GH * part + GH, g % 2, :]).then_inc(s_mrow[g], 16)
                        if TAIL:
                            sp.dma_start(q_stack[STACK + part:STACK + part + 1, g, :, S_IMG:S],
                                         max_rows_t[part:part + 1, g % 2, :].rearrange("p (h q) -> p h q", h=GH)
                                         ).then_inc(s_mrow[g], 16)
                if not last:
                    sp.wait_ge(s_ms_ready, MS.after(b - 1, ("v", VT - 1)))
                    load_x(b + 1)
                for g in range(3):
                    rows(g)
                if not last:
                    store_parts(b + 1)
                rows(3)
                if not last:
                    sp.wait_ge(s_qk_stored, (b + 2) * (16 * 8))
                    for g in range(GROUPS):
                        sp.wait_ge(s_sc_ready, b * (GROUPS * SU) + (g + 1) * SU)
                        load_stack(b + 1, g)

            batches(sp, body)

            def load_residual(b, t):
                sp.wait_ge(s_sum, 4 * b + (t + 1))
                sp.dma_start(res[:, t % 2, :], residual[bass.ds(b * (4 * P) + t * P, P), :]).then_inc(s_res[t % 2], 16)

            def store(b, t):
                if residual is None:
                    sp.wait_ge(s_y, 4 * b + (t + 3))
                    sp.dma_start(y_dram[bass.ds(b * S_ALL + t * P, P), :], y_tile[:, t % 2, :]).then_inc(s_out[t % 2], 16)
                else:
                    sp.wait_ge(s_sum, 4 * b + (t + 3))
                    sp.dma_start(y_dram[bass.ds(b * (4 * P) + t * P, P), :],
                                 y_tile[:, t % 2, :]).then_inc(s_out[t % 2], 16)

            def rows_of(b):
                for t in range(4):
                    if residual is not None:
                        load_residual(b, t)
                    if t % 2 == 1:
                        store(b, t - 1)
                        store(b, t)

            with sp.Fori(0, NB) as b:
                rows_of(b)
            if residual is not None:
                load_residual(NB, 0)
                store(NB, 0)
            for i in range(2):
                sp.wait_ge(s_out[i], 16 * (9 + (1 if residual is not None and i == 0 else 0)))

        @block.tensor
        def _(pe):
            pe.wait_ge(s_const, 16 * 11)
            pe.wait_ge(s_preset, 2)

            def misc(b, name, last, prologue=False):
                n = MS0.after(0, name) if prologue else ms_turn(b, name, last)
                pe.wait_ge(s_ms_free, n)
                return n

            def project_qk(b, last, prologue=False):
                pe.wait_ge(s_xb, 16 * (b + 1))
                if TAIL:
                    misc(b - 1, "qt", last, prologue)
                    for m in range(4):
                        for c in range(KC):
                            mm = pe.matmul(ms[:, S_TXT * m:S_TXT * m + S_TXT], wqk[:, c, P * m:P * m + P],
                                           xb[:, c, S_IMG:S], start=(c == 0), stop=(c == KC - 1))
                    mm.then_inc(s_ms_ready, 1)
                for m in range(4):
                    misc(b - 1, ("qk", m), last, prologue)
                    for c in range(KC):
                        mm = pe.matmul(ms[:, :], wqk[:, c, P * m:P * m + P], xb[:, c, 0:S_IMG],
                                       start=(c == 0), stop=(c == KC - 1))
                    mm.then_inc(s_ms_ready, 1)

            def project_v(b, last, prologue=False):
                for t in range(VT):
                    misc(b - 1, ("v", t), last, prologue)
                    w = P if t < KT else TAIL
                    for c in range(KC):
                        mm = pe.matmul(ms[0:w, 0:D], xb[:, c, P * t:P * t + w], wv[:, c, :],
                                       start=(c == 0), stop=(c == KC - 1))
                    mm.then_inc(s_ms_ready, 1)

            def max_pass(b, g):
                pe.wait_ge(s_stack[g], 16 * 12 * (b + 1))
                for u, (i, hs) in enumerate(max_units):
                    pe.wait_ge(s_mx_free, b * (GROUPS * MU) + (g * MU + u + 1))
                    bank = mx[(g * MU + u) % 2]
                    if i == "t":
                        lo, w = (0, S_IMG) if hs == 0 else (S_IMG, TAIL)
                        for h in range(GH):
                            r = slice(32 * h, 32 * h + 32)
                            mm = pe.matmul(bank[r, 0:w], q_stack[0:STACK, g, h, S_IMG:S],
                                           k_stack[0:STACK, g, h, lo:lo + w], start=True, stop=(hs == 0))
                            if hs == 1:
                                mm = pe.matmul(bank[r, 0:w], ident_bf[:, 0:32], mask_qt[:, :], start=False, stop=True)
                    else:
                        w = P * (i + 1) if causal else S_IMG
                        for n, h in enumerate(hs):
                            mm = pe.matmul(bank[:, n * w:n * w + w], q_stack[0:STACK, g, h, P * i:P * i + P],
                                           k_stack[0:STACK, g, h, 0:w], start=True, stop=not causal)
                            if causal:
                                mm = pe.matmul(bank[:, n * w + w - P:n * w + w], ident_bf[:, :], mask_q[:, :],
                                               start=False, stop=True)
                    mm.then_inc(s_mx_ready, 1)

            def turn_max(b, g, last):
                misc(b, ("tr", g), last)
                pe.wait_ge(s_mpart, b * GROUPS + g + 1)
                for i in range(KT):
                    mm = pe.transpose(ms_bf[0:2 * GH, P * i:P * i + P],
                                      max_part[:, g % 2, i, :, :].rearrange("p a h -> p (a h)"), ident_bf[:, :])
                if TAIL:
                    mm = pe.transpose(ms_bf[0:2, 512:640], max_part_t[:, g % 2, :], ident_bf[:, :])
                mm.then_inc(s_ms_ready, 1)

            def score_pass(b, g, last):
                pe.wait_ge(s_mrow[g], 16 + (16 * (4 if TAIL else 2)) * (b + 1))
                R = STACK + 2

                def score(u):
                    j, hs = score_units[u]
                    pe.wait_ge(s_exp, b * (GROUPS * SU) + (g * SU + u + 1))
                    bank = sc[(g * SU + u) % 2]
                    if j == "t":
                        for jj in range(KT):
                            for h in range(GH):
                                o = P * jj + 32 * h
                                pe.matmul(bank[:, 0, o:o + 32], k_stack[0:R, g, h, P * jj:P * jj + P],
                                          q_stack[0:R, g, h, S_IMG:S], start=True, stop=True)
                        for h in range(GH):
                            o = 32 * h
                            pe.matmul(bank[0:32, 1, o:o + 32], k_stack[0:R, g, h, S_IMG:S],
                                      q_stack[0:R, g, h, S_IMG:S], start=True, stop=False)
                            mm = pe.matmul(bank[0:32, 1, o:o + 32], ident_bf[:, 0:32], mask_k[:, 0:32],
                                           start=False, stop=True)
                    else:
                        lo = P * j if causal else 0
                        w = S_IMG - lo
                        per = len(hs) // 2
                        for n, h in enumerate(hs):
                            o = (n % per) * w
                            half = n // per
                            mm = pe.matmul(bank[:, half, o:o + w], k_stack[0:R, g, h, P * j:P * j + P],
                                           q_stack[0:R, g, h, lo:S_IMG], start=True, stop=not causal)
                            if causal:
                                mm = pe.matmul(bank[:, half, o:o + P], ident_bf[:, :], mask_k[:, :],
                                               start=False, stop=True)
                    mm.then_inc(s_sc_ready, 1)

                def values(us):
                    pe.wait_ge(s_exp, b * (GROUPS * SU) + (g * SU + us[-1] + 3))
                    j = score_units[us[0]][0]
                    if j == 0:
                        pe.wait_ge(s_o_read, b * GROUPS + g + 1)
                    for u in us:
                        jj, hs = score_units[u]
                        lo = P * j if causal else 0
                        w = S_IMG - lo
                        per = len(hs) // 2
                        for n, h in enumerate(hs):
                            o = 512 * (n // per) + (n % per) * w
                            mm = pe.matmul(ob[32 * h:32 * h + 32, lo:S_IMG], v_ones[:, j, g, h, :],
                                           probs[:, (g * NAV + u) % 4, o:o + w], start=(j == 0), stop=(j == KT - 1),
                                           skip_group_check=True)
                        if u != us[-1]:
                            mm.then_inc(s_av_done, 1)
                    mm.then_inc(s_av_done, 1)
                    return mm

                if g == 0:
                    pe.wait_ge(s_ms_free, MS.after(b - 1, ("v", VT - 1)) + 1)
                units = []
                for u, (j, hs) in enumerate(score_units):
                    if j == "t":
                        continue
                    if units and score_units[units[-1][0]][0] == j:
                        units[-1].append(u)
                    else:
                        units.append([u])
                score(0)
                score(1)
                done = 2
                for n, us in enumerate(units):
                    while done < SU and done < us[-1] + 3:
                        score(done)
                        done += 1
                    values(us)
                if TAIL:
                    while done < SU:
                        score(done)
                        done += 1
                    u = SU - 1
                    pe.wait_ge(s_exp, b * (GROUPS * SU) + (g * SU + u + 3))
                    misc(b, ("ot", g), last)
                    for jj in range(KT + 1):
                        for h in range(GH):
                            w = P if jj < KT else TAIL
                            mm = pe.matmul(ms[32 * h:32 * h + 32, 0:32], v_ones[0:w, jj, g, h, :],
                                           probs_t[0:w, P * jj + 32 * h:P * jj + 32 * h + 32], start=(jj == 0),
                                           stop=(jj == KT), skip_group_check=True)
                    mm.then_inc(s_ms_ready, 1)

            def spread_sum(b, g, last):
                pe.wait_ge(s_o_read, b * GROUPS + (g + 2))
                misc(b, ("se", g), last)
                pe.matmul(ms[:, :], sel[:, :], o_raw[:, g % 2, 0:S_IMG], start=True, stop=True).then_inc(s_ms_ready, 1)
                if TAIL:
                    misc(b, ("st", g), last)
                    pe.matmul(ms[:, 0:TAIL], sel[:, :], o_raw[:, g % 2, S_IMG:S], start=True,
                              stop=True).then_inc(s_ms_ready, 1)

            project_qk(0, False, True)
            project_v(0, False, True)

            def body(b, last):
                max_pass(b, 0)
                max_pass(b, 1)
                turn_max(b, 0, last)
                max_pass(b, 2)
                turn_max(b, 1, last)
                score_pass(b, 0, last)
                max_pass(b, 3)
                turn_max(b, 2, last)
                spread_sum(b, 0, last)
                score_pass(b, 1, last)
                if not last:
                    project_qk(b + 1, last)
                turn_max(b, 3, last)
                spread_sum(b, 1, last)
                score_pass(b, 2, last)
                spread_sum(b, 2, last)
                score_pass(b, 3, last)
                spread_sum(b, 3, last)
                if not last:
                    project_v(b + 1, last)

            batches(pe, body)

            def project_out(b, t):
                pe.wait_ge(s_tile_in, 4 * b + (t + 1))
                pe.wait_ge(s_y, 4 * b + (t + 1))
                for g in range(GROUPS):
                    mm = pe.matmul(mx[t % 2][:, 0:D], o_tile[:, t % 2, g, :], wo[:, g, :], start=(g == 0),
                                   stop=(g == GROUPS - 1))
                mm.then_inc(s_y_bank, 1)

            with pe.Fori(0, NB) as b:
                for t in range(4):
                    project_out(b, t)
            if residual is not None:
                project_out(NB, 0)

        @block.scalar
        def _(act):
            act.wait_ge(s_const, 16 * 11)

            def split_high(b, last, prologue=False):
                def turn(name):
                    return MS0.after(0, name) if prologue else ms_turn(b - 1, name, last)
                if not prologue:
                    act.wait_ge(s_qk_stored, (16 * 8) * b)
                if TAIL:
                    act.wait_ge(s_ms_ready, turn("qt"))
                    for m in range(4):
                        i = nc.scalar.activation(qk_full[:, m, S_IMG:S], ms[:, S_TXT * m:S_TXT * m + S_TXT],
                                                 ACT.Identity, bias=bqk[:, m:m + 1])
                        if m < 3:
                            i.then_inc(s_full, 1)
                        else:
                            i.then_inc(s_ms_free, 1)
                for m in range(4):
                    act.wait_ge(s_ms_ready, turn(("qk", m)))
                    nc.scalar.activation(qk_full[:, m, 0:S_IMG], ms[:, :], ACT.Identity,
                                         bias=bqk[:, m:m + 1]).then_inc(s_ms_free, 1)
                    act.wait_ge(s_ms_free, turn(("qk", m)) + 1)
                    nc.scalar.activation(qk_part[:, m, 0, :], qk_full[:, m, :], ACT.Copy).then_inc(s_high, 1)

            def exps(b, g, last):
                for u, (j, hs) in enumerate(score_units):
                    act.wait_ge(s_sc_ready, b * (GROUPS * SU) + (g * SU + u + 1))
                    bank = sc[(g * SU + u) % 2]
                    if j == "t":
                        nc.scalar.activation(probs_t[:, 0:512], bank[:, 0, :], ACT.Exp, scale=SCALE)
                        nc.scalar.activation(probs_t[0:32, 512:640], bank[0:32, 1, 0:P], ACT.Exp,
                                             scale=SCALE).then_inc(s_exp, 1)
                    else:
                        act.wait_ge(s_av_done, b * (GROUPS * NAV) + (g * NAV + u + 1))
                        w = (len(hs) // 2) * (S_IMG - (P * j if causal else 0))
                        nc.scalar.activation(
                            probs[:, (g * NAV + u) % 4, :].rearrange("p (a w) -> p a w", a=2)[:, :, 0:w],
                            bank[:, :, 0:w], ACT.Exp, scale=SCALE).then_inc(s_exp, 1)

            def read_o(b, g, last):
                act.wait_ge(s_av_done, b * (GROUPS * NAV) + ((g + 1) * NAV + 4))
                act.wait_ge(s_norm, b * GROUPS + (g + 1))
                if TAIL:
                    act.wait_ge(s_ms_ready, ms_turn(b, ("ot", g), last))
                    nc.scalar.copy(o_raw[:, g % 2, S_IMG:S], ms[:, 0:TAIL]).then_inc(s_ms_free, 1)
                nc.scalar.copy(o_raw[:, g % 2, 0:S_IMG], ob[:, :]).then_inc(s_o_read, 1)

            split_high(0, False, True)

            def body(b, last):
                exps(b, 0, last)
                read_o(b, 0, last)
                exps(b, 1, last)
                read_o(b, 1, last)
                if not last:
                    split_high(b + 1, last)
                exps(b, 2, last)
                read_o(b, 2, last)
                exps(b, 3, last)
                read_o(b, 3, last)

            batches(act, body)
            act.wait_ge(s_norm, 2 + NB * GROUPS)

            def take_tile(b, t):
                act.wait_ge(s_y_bank, 4 * b + (t + 1))
                nc.scalar.copy(o_tile[:, t % 2, :, :], o_all[:, :, bass.ds(b * (4 * P) + t * P, P)]
                               ).then_inc(s_tile_in, 1)

            with act.Fori(0, NB) as b:
                for t in range(4):
                    take_tile(b, t)
            if residual is not None:
                take_tile(NB, 0)

        @block.gpsimd
        def _(pool):
            pool.memset(v_ones[:], 1.0).then_inc(s_preset, 1)
            pool.sem_inc(s_ms_free, 1)
            pool.sem_inc(s_mx_free, 2)
            pool.sem_inc(s_exp, 2)
            pool.sem_inc(s_av_done, 4)
            pool.sem_inc(s_o_read, 1)
            pool.sem_inc(s_norm, 2)
            pool.sem_inc(s_y, 2)
            pool.sem_inc(s_y_bank, 2)
            pool.sem_inc(s_sum, 2)
            for q in (*s_mrow, *s_out):
                pool.sem_inc(q, 16)

        @block.vector
        def _(dve):
            nc.vector.memset(k_stack[STACK:STACK + 2], 1.0).then_inc(s_preset, 1)
            dve.wait_ge(s_const, 16 * 11)
            dve.wait_ge(s_preset, 2)

            def split_low(b):
                for m in range(4):
                    dve.wait_ge(s_high, b * 4 + m + 1)
                    nc.vector.tensor_tensor(qk_rest[:, m, :], qk_full[:, m, :], qk_part[:, m, 0, :],
                                            ALU.subtract).then_inc(s_rest, 1)
                for m in range(4):
                    dve.wait_ge(s_rest, b * 4 + m + 1)
                    nc.vector.tensor_copy(qk_part[:, m, 1, :], qk_rest[:, m, :]).then_inc(s_mid, 1)
                for m in range(4):
                    dve.wait_ge(s_mid, b * 4 + m + 1)
                    nc.vector.tensor_tensor(qk_part[:, m, 2, :], qk_rest[:, m, :], qk_part[:, m, 1, :],
                                            ALU.subtract).then_inc(s_low, 1)

            def read_v(b, last, prologue=False):
                for t in range(VT):
                    n = MS0.after(0, ("v", t)) if prologue else ms_turn(b - 1, ("v", t), last)
                    dve.wait_ge(s_ms_ready, n)
                    if not prologue and t == 0:
                        dve.wait_ge(s_o_read, b * GROUPS + 1)
                    w = P if t < KT else TAIL
                    nc.vector.tensor_tensor(
                        v_ones[0:w, t, :, :, 0:HD], ms[0:w, 0:D].rearrange("p (g h d) -> p g h d", g=GROUPS, h=GH),
                        bv[0:w, :].rearrange("p (g h d) -> p g h d", g=GROUPS, h=GH), ALU.add).then_inc(s_ms_free, 1)

            def row_max(b, g):
                for u, (i, hs) in enumerate(max_units):
                    n = b * (GROUPS * MU) + (g * MU + u + 1)
                    dve.wait_ge(s_mx_ready, n)
                    bank = mx[(g * MU + u) % 2]
                    if i == "t":
                        w = S_IMG if hs == 0 else TAIL
                        nc.vector.tensor_reduce(neg_max_t[:, g % 2, hs:hs + 1], bank[:, 0:w], AX.X, ALU.max,
                                                negate=True).then_inc(s_mx_free, 1)
                    else:
                        w = P * (i + 1) if causal else S_IMG
                        h0 = hs[0]
                        nc.vector.tensor_reduce(
                            neg_max[:, g % 2, i, h0:h0 + len(hs)],
                            bank[:, 0:w * len(hs)].rearrange("p (h k) -> p h k", h=len(hs)), AX.X, ALU.max,
                            negate=True).then_inc(s_mx_free, 1)
                dve.wait_ge(s_mx_free, 2 + b * (GROUPS * MU) + (g + 1) * MU)
                nc.vector.tensor_copy(max_part[:, g % 2, :, 0, :], neg_max[:, g % 2]).then_inc(s_mhigh, 1)
                if TAIL:
                    nc.vector.tensor_tensor(neg_max_t[:, g % 2, 2:3], neg_max_t[:, g % 2, 0:1],
                                            neg_max_t[:, g % 2, 1:2], ALU.min).then_inc(s_negt, 1)
                    dve.wait_ge(s_negt, b * GROUPS + (g + 1))
                    nc.vector.tensor_copy(max_part_t[:, g % 2, 0:1], neg_max_t[:, g % 2, 2:3]).then_inc(s_mhigh, 1)
                k = 2 if TAIL else 1
                dve.wait_ge(s_mhigh, b * (GROUPS * k) + (g + 1) * k)
                if TAIL:
                    nc.vector.tensor_tensor(max_part_t[:, g % 2, 1:2], neg_max_t[:, g % 2, 2:3],
                                            max_part_t[:, g % 2, 0:1], ALU.subtract)
                nc.vector.tensor_tensor(max_part[:, g % 2, :, 1, :], neg_max[:, g % 2], max_part[:, g % 2, :, 0, :],
                                        ALU.subtract).then_inc(s_mpart, 1)

            def read_rows(b, g, last):
                dve.wait_ge(s_ms_ready, ms_turn(b, ("tr", g), last))
                dve.wait_ge(s_mrow[(g + 2) % GROUPS], 16 + (16 * (4 if TAIL else 2)) * (b + 1 if g >= 2 else b))
                if TAIL:
                    nc.vector.tensor_copy(max_rows_t[:, g % 2, :], ms_bf[0:2, 512:640])
                nc.vector.tensor_copy(max_rows[:, g % 2, :], ms_bf[0:2 * GH, 0:512]).then_inc(s_ms_free, 1)

            def normalize(b, g, last):
                dve.wait_ge(s_ms_ready, ms_turn(b, ("se", g), last))
                nc.vector.reciprocal(o_inv[:, g % 2, 0:S_IMG], ms[:, :]).then_inc(s_ms_free, 1)
                if TAIL:
                    dve.wait_ge(s_ms_ready, ms_turn(b, ("st", g), last))
                    nc.vector.reciprocal(o_inv[:, g % 2, S_IMG:S], ms[:, 0:TAIL]).then_inc(s_ms_free, 1)
                dve.wait_ge(s_ms_free, ms_turn(b, ("st" if TAIL else "se", g), last) + 1)
                nc.vector.tensor_tensor(o_all[:, g, bass.ds(b * S, S)], o_raw[:, g % 2, :], o_inv[:, g % 2, :],
                                        ALU.mult).then_inc(s_norm, 1)

            split_low(0)
            read_v(0, False, True)

            def body(b, last):
                row_max(b, 0)
                row_max(b, 1)
                read_rows(b, 0, last)
                row_max(b, 2)
                read_rows(b, 1, last)
                row_max(b, 3)
                read_rows(b, 2, last)
                normalize(b, 0, last)
                if not last:
                    split_low(b + 1)
                read_rows(b, 3, last)
                normalize(b, 1, last)
                normalize(b, 2, last)
                normalize(b, 3, last)
                if not last:
                    read_v(b + 1, last)

            batches(dve, body)

            def finish_tile(b, t):
                dve.wait_ge(s_y_bank, 4 * b + (t + 3))
                dve.wait_ge(s_out[t % 2], 32 * b + 16 * (t // 2 + 1))
                nc.vector.tensor_tensor(y_tile[:, t % 2, :], mx[t % 2][:, 0:D], bo[:, :], ALU.add).then_inc(s_y, 1)
                if residual is not None:
                    dve.wait_ge(s_y, 4 * b + (t + 3))
                    dve.wait_ge(s_res[t % 2], 32 * b + 16 * (t // 2 + 1))
                    nc.vector.tensor_tensor(y_tile[:, t % 2, :], y_tile[:, t % 2, :], res[:, t % 2, :],
                                            ALU.add).then_inc(s_sum, 1)

            with dve.Fori(0, NB) as b:
                for t in range(4):
                    finish_tile(b, t)
            if residual is not None:
                finish_tile(NB, 0)


def layer_norm(nc, tag, h_dram, xT_dram, ident):
    ctx = ExitStack()
    with ctx:
        def sb(name, shape, dt):
            return ctx.enter_context(nc.sbuf_tensor(f"{tag}_{name}", shape, dt))

        def sem(name):
            return ctx.enter_context(nc.semaphore(f"{tag}_{name}"))

        h = sb("h", [P, NT, D], F32)
        xn = sb("xn", [P, NT, D], F32)
        xT = sb("xT", [P, KC, T_ALL], F32)
        idf = sb("ident", [P, P], F32)
        stats = sb("stats", [P, NT, 6], F32)
        mean_var = sb("mean_var", [P, NT, 2], F32)
        exponent = sb("exponent", [P, NT], F32)
        shifted = sb("shifted", [P, NT], F32)
        rstd = sb("rstd", [P, NT], F32)
        bank = [ctx.enter_context(nc.psum_tensor(f"{tag}_t{i}", [P, 512], F32)) for i in range(4)]
        s_in, s_stats, s_mv, s_shift, s_rstd, s_xn, s_t, s_x, s_out, s_id, s_exp = [
            sem(n) for n in ("h_loaded", "stats_done", "mean_var_done", "shifted", "rstd_ready", "xn_ready",
                             "turned", "xT_ready", "stored", "identity_loaded", "exponent_set")]
        block = ctx.enter_context(nc.Block())

        @block.sync
        def _(sp):
            sp.dma_start(h[:], h_dram.rearrange("(n p) d -> p n d", p=P)).then_inc(s_in, 16)
            sp.dma_start(idf[:], ident).then_inc(s_id, 16)
            sp.wait_ge(s_x, 2 * NT)
            sp.dma_start(xT_dram.rearrange("(c p) t -> p c t", p=P), xT[:]).then_inc(s_out, 16)
            sp.wait_ge(s_out, 16)

        @block.vector
        def _(dve):
            normalize_rows(nc, dve, h, xn, stats, mean_var, rstd, s_in, 16, s_stats, s_mv, s_rstd, s_xn)

        @block.gpsimd
        def _(pool):
            inverse_deviation(nc, pool, mean_var, shifted, exponent, rstd, s_mv, s_shift, s_exp, s_rstd)

        @block.tensor
        def _(pe):
            pe.wait_ge(s_id, 16)
            turn_rows(pe, xn, idf, bank, s_xn, s_x, s_t)

        @block.scalar
        def _(act):
            take_turned(nc, act, bank, xT, s_t, s_x)


def normalize_rows(nc, dve, h, xn, stats, mean_var, rstd, s_in, loaded, s_stats, s_mv, s_rstd, s_xn):
    dve.wait_ge(s_in, loaded)
    for t in range(NT):
        nc.vector.bn_stats(stats[:, t, :], h[:, t, :]).then_inc(s_stats, 1)
    for t in range(NT):
        dve.wait_ge(s_stats, t + 1)
        nc.vector.bn_aggr(mean_var[:, t, :], stats[:, t, :]).then_inc(s_mv, 1)
    dve.wait_ge(s_rstd, 1)
    for t in range(NT):
        nc.vector.tensor_scalar(xn[:, t, :], h[:, t, :], mean_var[:, t, 0:1], rstd[:, t:t + 1], ALU.subtract,
                                ALU.mult).then_inc(s_xn, 1)


def inverse_deviation(nc, pool, mean_var, shifted, exponent, rstd, s_mv, s_shift, s_exp, s_rstd):
    pool.memset(exponent[:], -0.5).then_inc(s_exp, 1)
    pool.wait_ge(s_mv, NT)
    nc.gpsimd.tensor_scalar(shifted[:], mean_var[:, :, 1], LN_EPS, 0.0, ALU.add, ALU.add).then_inc(s_shift, 1)
    pool.wait_ge(s_shift, 1)
    pool.wait_ge(s_exp, 1)
    nc.gpsimd.tensor_tensor(rstd[:], shifted[:], exponent[:], ALU.pow).then_inc(s_rstd, 1)


def turn_rows(pe, xn, idf, bank, s_xn, s_x, s_t):
    for t in range(NT):
        pe.wait_ge(s_xn, t + 1)
        if t >= 4:
            pe.wait_ge(s_x, 2 * (t - 3))
        for c in range(KC):
            mm = pe.transpose(bank[t % 4][:, P * c:P * c + P], xn[:, t, P * c:P * c + P], idf[:, :])
        mm.then_inc(s_t, 1)


def take_turned(nc, act, bank, xT, s_t, s_x):
    for t in range(NT):
        act.wait_ge(s_t, t + 1)
        nc.scalar.copy(xT[:, :, P * t:P * t + P], bank[t % 4][:, 0:KC * P].rearrange("p (c t) -> p c t", c=KC)
                       ).then_inc(s_x, 2)


def copy_text(nc, txt, h_dram):
    with ExitStack() as ctx:
        s_txt = ctx.enter_context(nc.semaphore("text_stored"))
        block = ctx.enter_context(nc.Block())

        @block.sync
        def _(sp):
            sp.dma_start(h_dram.rearrange("(b s) d -> b s d", b=NB)[:, S_IMG:S_ALL, :], txt).then_inc(s_txt, 16)
            sp.wait_ge(s_txt, 16)


INPUTS = ["xT", "txt", "t_wqk", "t_bqk", "t_wv", "t_bv", "t_wo", "t_bo", "a_wqk", "a_bqk", "a_wv", "a_bv", "a_wo",
          "a_bo", "ident_f", "ident_bf", "sel", "mask_q", "mask_k", "mask_qt"]


def attention_inputs(w_cols, b_cols, w_rows, b_out):
    import numpy as np
    w = w_cols.reshape(D, HEADS, 3, HD)
    b = b_cols.reshape(HEADS, 3, HD)
    out = {"wqk": w[:, :, 0:2].transpose(0, 2, 1, 3).reshape(KC, P, 2 * D).transpose(1, 0, 2),
           "bqk": b[:, 0:2].transpose(1, 0, 2).reshape(4, P).T,
           "wv": w[:, :, 2].reshape(KC, P, D).transpose(1, 0, 2),
           "bv": np.broadcast_to(b[:, 2].reshape(1, D), (P, D))}
    wo = np.zeros((GROUPS, GH, 32, D), np.float32)
    wo[:, :, 0:HD] = w_rows.reshape(GROUPS, GH, HD, D)
    out["wo"] = wo.reshape(GROUPS, P, D).transpose(1, 0, 2)
    out["bo"] = np.broadcast_to(b_out.reshape(1, D), (P, D))
    return out


def constants():
    import numpy as np
    f, bf = np.float32, mybir.dt.np(BF16)
    i = np.arange(P)
    c = {"ident_f": np.eye(P, dtype=f), "ident_bf": np.eye(P, dtype=f).astype(bf)}
    c["sel"] = ((i[:, None] % 32 == HD) & (i[:, None] // 32 == i[None, :] // 32)).astype(f)
    later = np.where(i[None, :] > i[:, None], f(-1e30), f(0))
    c["mask_q"] = later.astype(bf)
    c["mask_k"] = later.T.astype(bf)
    qt = np.zeros((P, S_TXT), f)
    qt[0:S_TXT] = later[0:S_TXT, 0:S_TXT]
    c["mask_qt"] = qt.astype(bf)
    return c


def experts_layer(nc, h_dram, xn_dram, slots_dram, y_dram, w, out):
    NC2 = 2 * P
    CHUNKS = T_ALL // NC2
    ctx = ExitStack()
    with ctx:
        def sb(name, shape, dt, where=ctx):
            return where.enter_context(nc.sbuf_tensor(f"e_{name}", shape, dt))

        def sem(name):
            return ctx.enter_context(nc.semaphore(f"e_{name}"))

        h = sb("h", [P, NT, D], F32)
        xT = sb("xT", [P, KC, T_ALL], F32)
        idf = sb("ident", [P, P], F32)
        slot_of = sb("slot_of", [P, NT, TOPK], U32)
        weight_of = sb("weight_of", [P, NT, TOPK], F32)
        token_of = sb("token_of", [P, E * CT], U32)

        with ExitStack() as early:
            def se(name, shape, dt):
                return sb(name, shape, dt, early)

            xn = se("xn", [P, NT, D], F32)
            stats = se("stats", [P, NT, 6], F32)
            mean_var = se("mean_var", [P, NT, 2], F32)
            exponent = se("exponent", [P, NT], F32)
            shifted = se("shifted", [P, NT], F32)
            rstd = se("rstd", [P, NT], F32)
            router = se("router", [P, KC, E], F32)
            bias = se("bias", [P, E], F32)
            before = se("before", [P, P], BF16)
            ones = se("ones", [P, P], BF16)
            iota_e = se("iota_e", [P, E], F32)
            iota_bf = se("iota_bf", [P, 32], BF16)
            token = se("token", [P, 1], F32)
            scores = se("scores", [P, NT, E], F32)
            ranked = se("ranked", [P, NT, E], F32)
            top = se("top", [P, NT, TOPK], F32)
            struck = se("struck", [P, NT, E], F32)
            choice = se("choice", [P, NT, TOPK], U32)
            choice_f = se("choice_f", [P, NT, TOPK], F32)
            chosen = se("chosen", [P, NT, E], F32)
            chosen_bf = se("chosen_bf", [P, NT, E], BF16)
            count = se("count", [P, NT, E], BF16)
            pos = se("pos", [P, NT, E], F32)
            pos_in = se("pos_in", [P, NT, E], F32)
            total = se("total", [P, NT], F32)
            gain = se("gain", [P, NT, E], F32)
            pos_i = se("pos_i", [P, NT, E], I32)
            hi_i = se("hi_i", [P, NT, E], I32)
            lo_i = se("lo_i", [P, NT, E], I32)
            hi = se("hi", [P, NT, E], BF16)
            lo = se("lo", [P, NT, E], BF16)
            one_hi = se("one_hi", [P, NT, E, 32], BF16)
            one_lo = se("one_lo", [P, NT, E, 2, 16], BF16)
            pick = se("pick", [P, NT, TOPK, E], F32)
            picked = se("picked", [P, NT, TOPK, E], F32)
            slot_f = se("slot_f", [P, NT, TOPK], F32)
            parts = se("parts", [P, 8, 4, 2, 16], F32)
            table = se("table", [P, 8, 16], F32)
            rows = se("rows", [P, P], F32)
            bank = [early.enter_context(nc.psum_tensor(f"e_t{i}", [P, 512], F32)) for i in range(4)]
            pr = early.enter_context(nc.psum_tensor("e_pr", [P, 2, 512], F32))
            pt = early.enter_context(nc.psum_tensor("e_pt", [P, 2, 512], F32))
            (s_in, s_stats, s_mv, s_shift, s_rstd, s_xn, s_t, s_x, s_xn_out, s_exp, s_const, s_logits, s_sig, s_v,
             s_count, s_pos, s_onehot, s_table, s_rows_out, s_rows_in, s_rows_turned, s_tab) = [
                sem(n) for n in (
                    "h_loaded", "stats_done", "mean_var_done", "shifted", "rstd_ready", "xn_ready", "turned",
                    "xT_ready", "xn_stored", "exponent_set", "router_constants", "logits_ready", "exp_ready",
                    "vector_steps", "count_ready", "pos_ready", "onehot_ready", "table_ready", "table_stored",
                    "table_loaded", "table_turned", "table_rows_ready")]
            block = early.enter_context(nc.Block())

            @block.sync
            def _(sp):
                sp.dma_start(h[:], h_dram.rearrange("(n p) d -> p n d", p=P)).then_inc(s_in, 16)
                for dst, src in ((idf, w["ident_f"]), (router, w["router"]), (bias, w["e_bias"]),
                                 (before, w["before"]), (ones, w["ones_bf"]), (iota_e, w["iota_e"]),
                                 (iota_bf, w["iota_bf"]), (token, w["token"])):
                    sp.dma_start(dst[:], src).then_inc(s_const, 16)
                sp.wait_ge(s_xn, NT)
                sp.dma_start(xn_dram.rearrange("(n p) d -> p n d", p=P), xn[:]).then_inc(s_xn_out, 16)
                sp.wait_ge(s_tab, 4)
                sp.dma_start(slots_dram.rearrange("(g p l) -> p g l", p=P, l=16), table[:]).then_inc(s_rows_out, 16)
                sp.wait_ge(s_rows_out, 16)
                sp.dma_start(rows[:], slots_dram.rearrange("(r s) -> r s", s=P)).then_inc(s_rows_in, 16)
                sp.wait_ge(s_xn_out, 16)

            @block.gpsimd
            def _(pool):
                inverse_deviation(nc, pool, mean_var, shifted, exponent, rstd, s_mv, s_shift, s_exp, s_rstd)

            @block.scalar
            def _(act):
                take_turned(nc, act, bank, xT, s_t, s_x)
                act.wait_ge(s_logits, 1)
                nc.scalar.activation(scores[:, 0:16, :], pr[:, 0, :].rearrange("p (t e) -> p t e", e=E), ACT.Exp,
                                     scale=-1.0)
                nc.scalar.activation(scores[:, 16, :], pr[:, 1, 0:E], ACT.Exp, scale=-1.0).then_inc(s_sig, 1)

            @block.tensor
            def _(pe):
                pe.wait_ge(s_const, 16 * 8)
                turn_rows(pe, xn, idf, bank, s_xn, s_x, s_t)
                pe.wait_ge(s_x, 2 * NT)
                for t in range(NT):
                    for c in range(KC):
                        mm = pe.matmul(pr[:, t // 16, E * (t % 16):E * (t % 16) + E], xT[:, c, P * t:P * t + P],
                                       router[:, c, :], start=(c == 0), stop=(c == KC - 1))
                mm.then_inc(s_logits, 1)
                pe.wait_ge(s_count, NT)
                for t in range(NT):
                    o = pr[:, t // 16, E * (t % 16):E * (t % 16) + E]
                    mm = pe.matmul(o, before[:, :], chosen_bf[:, t, :], start=True, stop=False)
                    mm = pe.matmul(o, ones[:, :], count[:, t, :], start=False, stop=True)
                mm.then_inc(s_pos, 1)
                pe.wait_ge(s_onehot, 1)
                for g in range(8):
                    for t in range(NT):
                        mm = pe.matmul(pt[:, g // 4, P * (g % 4):P * (g % 4) + P],
                                       one_hi[:, t, 4 * g:4 * g + 4, :].rearrange("p e a -> p (e a)"),
                                       one_lo[:, t, 4 * g:4 * g + 4, :, :].rearrange("p e k b -> p (e k b)"),
                                       start=(t == 0), stop=(t == NT - 1))
                mm.then_inc(s_table, 1)
                pe.wait_ge(s_rows_in, 16)
                pe.transpose(bank[0][:, 0:P], rows[:, :], idf[:, :]).then_inc(s_rows_turned, 1)

            @block.vector
            def _(dve):
                normalize_rows(nc, dve, h, xn, stats, mean_var, rstd, s_in, 16, s_stats, s_mv, s_rstd, s_xn)
                steps = [0]

                def then(i):
                    steps[0] += 1
                    i.then_inc(s_v, 1)
                    dve.wait_ge(s_v, steps[0])

                v = nc.vector
                dve.wait_ge(s_const, 16 * 8)
                dve.wait_ge(s_sig, 1)
                then(v.tensor_scalar(scores[:], scores[:], 1.0, None, ALU.add))
                then(v.reciprocal(scores[:], scores[:]))
                then(v.tensor_tensor(ranked[:], scores[:], bias[:, None, :].to_broadcast([P, NT, E]), ALU.add))
                for t in range(NT):
                    i = v.max(top[:, t, :], ranked[:, t, :])
                then(i)
                for t in range(NT):
                    v.max_index(choice[:, t, :], top[:, t, :], ranked[:, t, :])
                for t in range(NT):
                    i = v.match_replace(struck[:, t, :], top[:, t, :], ranked[:, t, :], -3e38)
                then(i)
                then(v.tensor_tensor(chosen[:], struck[:], ranked[:], ALU.not_equal))
                v.memset(count[:, 0, :], 0.0).then_inc(s_count, 1)
                then(v.tensor_copy(chosen_bf[:], chosen[:]))
                for t in range(1, NT):
                    dve.wait_ge(s_count, t)
                    v.tensor_tensor(count[:, t, :], count[:, t - 1, :], chosen_bf[:, t - 1, :],
                                    ALU.add).then_inc(s_count, 1)
                then(v.tensor_tensor(gain[:], scores[:], chosen[:], ALU.mult))
                then(v.tensor_reduce(total[:], gain[:], AX.X, ALU.add))
                then(v.tensor_scalar(total[:], total[:], 1e-20, None, ALU.add))
                then(v.reciprocal(total[:], total[:]))
                then(v.tensor_tensor(gain[:], gain[:], total[:, :, None].to_broadcast([P, NT, E]), ALU.mult))
                then(v.tensor_scalar(gain[:], gain[:], ROUTE_SCALE, None, ALU.mult))
                then(v.tensor_copy(choice_f[:], choice[:]))
                dve.wait_ge(s_pos, 1)
                v.tensor_copy(pos[:, 0:16, :], pr[:, 0, :].rearrange("p (t e) -> p t e", e=E))
                then(v.tensor_copy(pos[:, 16, :], pr[:, 1, 0:E]))
                then(v.tensor_scalar(pos_in[:], chosen[:], -4096.0, 4096.0, ALU.mult, ALU.add))
                then(v.tensor_tensor(pos_in[:], pos_in[:], pos[:], ALU.add))
                then(v.tensor_copy(pos_i[:], pos_in[:]))
                v.tensor_scalar(hi_i[:], pos_i[:], 4, None, ALU.logical_shift_right)
                then(v.tensor_scalar(lo_i[:], pos_i[:], 15, None, ALU.bitwise_and))
                v.tensor_copy(hi[:], hi_i[:])
                then(v.tensor_copy(lo[:], lo_i[:]))
                for t in range(NT):
                    v.tensor_tensor(one_hi[:, t], hi[:, t, :, None].to_broadcast([P, E, 32]),
                                    iota_bf[:, None, :].to_broadcast([P, E, 32]), ALU.is_equal)
                    i = v.tensor_tensor(one_lo[:, t, :, 1, :], lo[:, t, :, None].to_broadcast([P, E, 16]),
                                        iota_bf[:, None, 0:16].to_broadcast([P, E, 16]), ALU.is_equal)
                then(i)
                for t in range(NT):
                    i = v.tensor_scalar(one_lo[:, t, :, 0, :], one_lo[:, t, :, 1, :], token[:, 0:1], None, ALU.mult)
                then(i)
                for t in range(NT):
                    i = v.tensor_scalar(one_lo[:, t, :, 1, :], one_lo[:, t, :, 1, :], float(t), None, ALU.mult)
                i.then_inc(s_onehot, 1)
                then(v.tensor_scalar(pos_in[:], pos[:], float(CAP), None, ALU.is_lt))
                then(v.tensor_tensor(gain[:], gain[:], pos_in[:], ALU.mult))
                then(v.tensor_scalar(pos[:], pos[:], float(CAP - 1), None, ALU.min))
                for t in range(NT):
                    i = v.tensor_tensor(pick[:, t], choice_f[:, t, :, None].to_broadcast([P, TOPK, E]),
                                        iota_e[:, None, :].to_broadcast([P, TOPK, E]), ALU.is_equal)
                then(i)
                for t in range(NT):
                    i = v.tensor_tensor(picked[:, t], pick[:, t], gain[:, t, None, :].to_broadcast([P, TOPK, E]),
                                        ALU.mult)
                then(i)
                then(v.tensor_reduce(weight_of[:], picked[:], AX.X, ALU.add))
                for t in range(NT):
                    i = v.tensor_tensor(picked[:, t], pick[:, t], pos[:, t, None, :].to_broadcast([P, TOPK, E]),
                                        ALU.mult)
                then(i)
                then(v.tensor_reduce(slot_f[:], picked[:], AX.X, ALU.add))
                then(v.tensor_scalar(choice_f[:], choice_f[:], float(CAP), None, ALU.mult))
                then(v.tensor_tensor(slot_f[:], slot_f[:], choice_f[:], ALU.add))
                then(v.tensor_copy(slot_of[:], slot_f[:]))
                dve.wait_ge(s_table, 1)
                v.tensor_copy(parts[:, 0:4], pt[:, 0, :].rearrange("p (g e k b) -> p g e k b", g=4, e=4, k=2))
                then(v.tensor_copy(parts[:, 4:8], pt[:, 1, :].rearrange("p (g e k b) -> p g e k b", g=4, e=4, k=2)))
                for e in range(4):
                    r = slice(32 * e, 32 * e + 32)
                    v.scalar_tensor_tensor(table[r], parts[r, :, e, 1, :], float(P), parts[r, :, e, 0, :], ALU.mult,
                                           ALU.add).then_inc(s_tab, 1)
                dve.wait_ge(s_rows_turned, 1)
                v.tensor_copy(token_of[:], bank[0][:, 0:P])

        gate_up = sb("gate_up", [P, 2, KC, 2 * INTER], F32)
        down = sb("down", [P, 2, D], F32)
        now = sb("now", [P, 2, CT], U32)
        xg = [[sb(f"xg{i}{c}", [P, D], F32) for c in range(CT)] for i in range(2)]
        xgT = sb("xgT", [P, 2, KC, CAP], F32)
        g_lim = sb("g_lim", [P, 2, CAP], F32)
        u_lim = sb("u_lim", [P, 2, CAP], F32)
        sg = sb("sg", [P, 2, CAP], F32)
        hid = sb("hid", [P, 2, CAP], F32)
        y = sb("y", [P, 2, CT, D], F32)
        pick_now = sb("pick_now", [P, 2, TOPK], U32)
        yg = [[sb(f"yg{i}{c}", [P, D], F32) for c in range(TOPK)] for i in range(2)]
        s_gu = sb("s_gu", [P, KC, 2 * SHARED], F32)
        s_down = sb("s_down", [P, SHARED // P, D], F32)
        s_g = sb("s_g", [P, 4, NC2], F32)
        s_e = sb("s_e", [P, 4, NC2], F32)
        s_h = sb("s_h", [P, 4, NC2], F32)
        acc = sb("acc", [P, 2, D], F32)
        res = sb("res", [P, 2, D], F32)
        tp = ctx.enter_context(nc.psum_tensor("e_tp", [P, KC, 512], F32))
        gu = ctx.enter_context(nc.psum_tensor("e_gu", [P, 2, 512], F32))
        yp = ctx.enter_context(nc.psum_tensor("e_yp", [P, 2, 512], F32))
        (q_w0, q_w1, q_now, q_g0, q_g1, q_free, q_tr, q_xT, q_gu, q_gl, q_ul, q_sig, q_s1, q_s2, q_hid, q_y, q_yr,
         q_st0, q_st1, q_sw, q_pick, q_c0, q_c1, q_cfree, q_sp, q_se, q_s3, q_s4, q_sh, q_sy, q_acc, q_out0, q_out1,
         q_res) = [
            sem(n) for n in (
                "weights0_loaded", "weights1_loaded", "indices_ready", "rows0_gathered", "rows1_gathered",
                "rows_turned", "turned_ready", "xT_taken", "gate_up_ready", "gate_limited", "up_limited",
                "gate_exp", "gate_denominator", "gate_inverse", "hidden_ready", "y_ready", "y_read", "y0_stored",
                "y1_stored", "shared_weights", "slots_ready", "results0_gathered", "results1_gathered",
                "results_summed", "shared_gate_up", "shared_exp", "shared_denominator", "shared_inverse",
                "shared_hidden", "shared_y", "sum_steps", "out0_stored", "out1_stored", "residual_added")]
        q_w, q_g, q_st, q_c, q_out = (q_w0, q_w1), (q_g0, q_g1), (q_st0, q_st1), (q_c0, q_c1), (q_out0, q_out1)
        block = ctx.enter_context(nc.Block())
        TAKE = SHARED // P

        @block.sync
        def _(sp):
            sp.dma_start(s_gu[:], w["s_gu"]).then_inc(q_sw, 16)
            sp.dma_start(s_down[:], w["s_down"]).then_inc(q_sw, 16)

            def load(i, k):
                sp.wait_ge(q_y, 2 * i + (k + 1))
                sp.dma_start(gate_up[:, k], w["gate_up"][bass.ds(2 * i + k, 1)].rearrange("e p c o -> p (e c) o")
                             ).then_inc(q_w[k], 16)
                sp.dma_start(down[:, k], w["down"][bass.ds(2 * i + k, 1)].rearrange("e p o -> p (e o)")
                             ).then_inc(q_w[k], 16)

            def store(i, k):
                sp.wait_ge(q_yr, 2 * i + (k + 3))
                sp.dma_start(y_dram[bass.ds((2 * i + k) * CAP, CAP), :].rearrange("(c p) d -> p c d", p=P),
                             y[:, k]).then_inc(q_st[k], 16)

            load(0, 0)
            load(0, 1)
            with sp.Fori(0, E // 2 - 1) as i:
                for k in range(2):
                    store(i, k)
                    load(i + 1, k)
            for k in range(2):
                store(E // 2 - 1, k)

            def store_out(i, k):
                sp.wait_ge(q_res, 2 * i + (k + 1))
                sp.dma_start(out[bass.ds((2 * i + k) * P, P), :], acc[:, k]).then_inc(q_out[k], 16)

            with sp.Fori(0, NT // 2) as i:
                for k in range(2):
                    store_out(i, k)
            store_out(NT // 2, 0)
            sp.wait_ge(q_out[0], 16 * (NT // 2 + 2))
            sp.wait_ge(q_out[1], 16 * (NT // 2 + 1))

        @block.gpsimd
        def _(pool):
            pool.sem_inc(q_y, 2)
            pool.sem_inc(q_free, 2)
            pool.sem_inc(q_yr, 2)
            pool.sem_inc(q_cfree, 2)
            for q in (q_xT, q_ul, q_sh, q_acc):
                pool.sem_inc(q, 1)
            for q in (*q_st, *q_out):
                pool.sem_inc(q, 16)

            def gather(i, k):
                pool.wait_ge(q_free, 2 * i + (k + 1))
                nc.gpsimd.tensor_copy(now[:, k, :], token_of[:, bass.ds((2 * i + k) * CT, CT)]).then_inc(q_now, 1)
                pool.drain()
                for c in range(CT):
                    pool.indirect_dma_start(xg[k][c][:, :], None, xn_dram,
                                            bass.IndirectOffsetOnAxis(now[:, k, c:c + 1], 0)).then_inc(q_g[k], 16)

            with pool.Fori(0, E // 2) as i:
                for k in range(2):
                    gather(i, k)
            for k in range(2):
                pool.wait_ge(q_st[k], 16 * (E // 2 + 1))

            def collect(i, k):
                pool.wait_ge(q_cfree, 2 * i + (k + 1))
                nc.gpsimd.tensor_copy(pick_now[:, k, :], slot_of[:, bass.ds(2 * i + k, 1), :].rearrange(
                    "p n c -> p (n c)")).then_inc(q_pick, 1)
                pool.drain()
                for c in range(TOPK):
                    pool.indirect_dma_start(yg[k][c][:, :], None, y_dram,
                                            bass.IndirectOffsetOnAxis(pick_now[:, k, c:c + 1], 0)
                                            ).then_inc(q_c[k], 16)

            with pool.Fori(0, NT // 2) as i:
                for k in range(2):
                    collect(i, k)
            collect(NT // 2, 0)

        @block.tensor
        def _(pe):
            def turn(i, k):
                pe.wait_ge(q_g[k], 16 * CT * (i + 1))
                pe.wait_ge(q_xT, 2 * (2 * i + k) + 1)
                for ch in range(KC):
                    for c in range(CT):
                        mm = pe.transpose(tp[:, ch, P * c:P * c + P], xg[k][c][:, P * ch:P * ch + P], idf[:, :])
                mm.then_inc(q_free, 1)

            def compute(i, k):
                pe.wait_ge(q_w[k], 32 * (i + 1))
                pe.wait_ge(q_xT, 2 * (2 * i + k) + 3)
                pe.wait_ge(q_ul, 2 * i + (k + 1))
                for half in range(2):
                    for ch in range(KC):
                        mm = pe.matmul(gu[:, half, :], gate_up[:, k, ch, INTER * half:INTER * half + INTER],
                                       xgT[:, k, ch, :], start=(ch == 0), stop=(ch == KC - 1))
                    mm.then_inc(q_gu, 1)

            def finish(i, k):
                pe.wait_ge(q_hid, 2 * i + (k + 1))
                pe.wait_ge(q_yr, 2 * i + (k + 2))
                for c in range(CT):
                    mm = pe.matmul(yp[:, c // 2, D * (c % 2):D * (c % 2) + D], hid[:, k, P * c:P * c + P], down[:, k, :],
                                   start=True, stop=True)
                mm.then_inc(q_y, 1)

            turn(0, 0)
            with pe.Fori(0, E // 2 - 1) as i:
                compute(i, 0)
                turn(i, 1)
                finish(i, 0)
                compute(i, 1)
                turn(i + 1, 0)
                finish(i, 1)
            n = E // 2 - 1
            compute(n, 0)
            turn(n, 1)
            finish(n, 0)
            compute(n, 1)
            finish(n, 1)
            pe.wait_ge(q_sw, 32)
            pe.wait_ge(q_yr, 2 + E)
            pe.wait_ge(q_ul, E + 1)

            def shared(i, wd, tiles):
                pe.wait_ge(q_sh, i + 1)
                for half, banks in ((0, tp), (1, gu)):
                    for f in range(TAKE):
                        for ch in range(KC):
                            mm = pe.matmul(banks[:, f // 2, NC2 * (f % 2):NC2 * (f % 2) + wd],
                                           s_gu[:, ch, SHARED * half + P * f:SHARED * half + P * f + P],
                                           xT[:, ch, bass.ds(i * NC2, wd)], start=(ch == 0), stop=(ch == KC - 1))
                mm.then_inc(q_sp, 1)
                pe.wait_ge(q_sh, i + 2)
                for t in range(tiles):
                    pe.wait_ge(q_acc, (2 * 9) * i + (9 * t + 1))
                    for f in range(TAKE):
                        mm = pe.matmul(yp[:, t, 0:D], s_h[:, f, P * t:P * t + P], s_down[:, f, :], start=(f == 0),
                                       stop=(f == TAKE - 1))
                    mm.then_inc(q_sy, 1)

            with pe.Fori(0, CHUNKS) as i:
                shared(i, NC2, 2)
            shared(CHUNKS, P, 1)

        @block.scalar
        def _(act):
            def take(i, k):
                act.wait_ge(q_free, 2 * i + (k + 3))
                for ch in range(KC):
                    nc.scalar.copy(xgT[:, k, ch, :], tp[:, ch, :]).then_inc(q_xT, 1)

            def sigmoid(i, k):
                act.wait_ge(q_gl, 2 * i + (k + 1))
                nc.scalar.activation(sg[:, k, :], g_lim[:, k, :], ACT.Exp, scale=-1.0).then_inc(q_sig, 1)

            def result(i, k):
                act.wait_ge(q_y, 2 * i + (k + 3))
                act.wait_ge(q_st[k], 16 * (i + 1))
                nc.scalar.copy(y[:, k].rearrange("p (a c) d -> p a (c d)", a=2), yp[:, :, :]).then_inc(q_yr, 1)

            take(0, 0)
            with act.Fori(0, E // 2 - 1) as i:
                sigmoid(i, 0)
                take(i, 1)
                result(i, 0)
                sigmoid(i, 1)
                take(i + 1, 0)
                result(i, 1)
            n = E // 2 - 1
            sigmoid(n, 0)
            take(n, 1)
            result(n, 0)
            sigmoid(n, 1)
            result(n, 1)

            def shared_exp(i, wd):
                act.wait_ge(q_sp, i + 1)
                act.wait_ge(q_sh, i + 1)
                nc.scalar.activation(s_e[:, :, 0:wd].rearrange("p (a b) t -> p a b t", a=2),
                                     tp[:, :, :].rearrange("p a (b t) -> p a b t", b=2)[:, :, :, 0:wd], ACT.Exp,
                                     scale=-1.0).then_inc(q_se, 1)

            with act.Fori(0, CHUNKS) as i:
                shared_exp(i, NC2)
            shared_exp(CHUNKS, P)

        @block.vector
        def _(dve):
            v = nc.vector

            def hidden(i, k):
                n = 2 * i + k
                dve.wait_ge(q_gu, 2 * n + 1)
                v.tensor_scalar(g_lim[:, k, :], gu[:, 0, :], LIMIT, None, ALU.min).then_inc(q_gl, 1)
                dve.wait_ge(q_gu, 2 * n + 2)
                v.tensor_scalar(u_lim[:, k, :], gu[:, 1, :], LIMIT, -LIMIT, ALU.min, ALU.max).then_inc(q_ul, 1)
                dve.wait_ge(q_sig, n + 1)
                v.tensor_scalar(sg[:, k, :], sg[:, k, :], 1.0, None, ALU.add).then_inc(q_s1, 1)
                dve.wait_ge(q_ul, n + 2)
                v.tensor_tensor(u_lim[:, k, :], u_lim[:, k, :], g_lim[:, k, :], ALU.mult)
                dve.wait_ge(q_s1, n + 1)
                v.reciprocal(sg[:, k, :], sg[:, k, :]).then_inc(q_s2, 1)
                dve.wait_ge(q_s2, n + 1)
                v.tensor_tensor(hid[:, k, :], u_lim[:, k, :], sg[:, k, :], ALU.mult).then_inc(q_hid, 1)

            with dve.Fori(0, E // 2) as i:
                for k in range(2):
                    hidden(i, k)

            def shared_hidden(i, wd):
                dve.wait_ge(q_se, i + 1)
                four = [P, 2, 2, wd]
                e4 = s_e[:, :, 0:wd].rearrange("p (a b) t -> p a b t", a=2)
                g4 = s_g[:, :, 0:wd].rearrange("p (a b) t -> p a b t", a=2)
                v.tensor_scalar(s_e[:, :, 0:wd], s_e[:, :, 0:wd], 1.0, None, ALU.add).then_inc(q_s3, 1)
                dve.wait_ge(q_s3, 3 * i + 1)
                v.reciprocal(s_e[:, :, 0:wd], s_e[:, :, 0:wd]).then_inc(q_s3, 1)
                dve.wait_ge(q_s3, 3 * i + 2)
                v.tensor_tensor(g4, tp[:, :, :].rearrange("p a (b t) -> p a b t", b=2)[:, :, :, 0:wd], e4,
                                ALU.mult).then_inc(q_s3, 1)
                dve.wait_ge(q_s3, 3 * i + 3)
                v.tensor_tensor(s_h[:, :, 0:wd].rearrange("p (a b) t -> p a b t", a=2),
                                gu[:, :, :].rearrange("p a (b t) -> p a b t", b=2)[:, :, :, 0:wd], g4,
                                ALU.mult).then_inc(q_sh, 1)

            def combine(i, k):
                dve.wait_ge(q_c[k], 16 * TOPK * (i + 1))
                dve.wait_ge(q_out[k], 16 * (i + 1))
                base = 18 * i + (9 * k + 1)
                wt = weight_of[:, bass.ds(2 * i + k, 1), :].rearrange("p n c -> p (n c)")
                v.tensor_scalar(acc[:, k], yg[k][0][:, :], wt[:, 0:1], None, ALU.mult).then_inc(q_acc, 1)
                for c in range(1, TOPK):
                    dve.wait_ge(q_acc, base + c)
                    v.scalar_tensor_tensor(acc[:, k], yg[k][c][:, :], wt[:, c:c + 1], acc[:, k], ALU.mult,
                                           ALU.add).then_inc(q_acc, 1)
                dve.wait_ge(q_acc, base + TOPK)
                dve.wait_ge(q_sy, 2 * i + (k + 1))
                v.tensor_tensor(acc[:, k], acc[:, k], yp[:, k, 0:D], ALU.add).then_inc(q_acc, 1)
                dve.wait_ge(q_acc, base + 9)
                v.tensor_tensor(acc[:, k], acc[:, k], h[:, bass.ds(2 * i + k, 1), :].rearrange("p n d -> p (n d)"),
                                ALU.add).then_inc(q_res, 1)
                dve.wait_ge(q_res, 2 * i + (k + 1))
                dve.sem_inc(q_cfree, 1)

            with dve.Fori(0, CHUNKS) as i:
                shared_hidden(i, NC2)
                combine(i, 0)
                combine(i, 1)
            shared_hidden(CHUNKS, P)
            combine(CHUNKS, 0)


def expert_inputs(router_weight, e_bias, gate_up, down, shared_gate, shared_up, shared_down):
    import numpy as np
    return {
        "router": router_weight.T.reshape(KC, P, E).transpose(1, 0, 2),
        "e_bias": np.broadcast_to(e_bias.reshape(1, E), (P, E)),
        "gate_up": gate_up.transpose(0, 2, 1).reshape(E, KC, P, 2 * INTER).transpose(0, 2, 1, 3),
        "down": down.transpose(0, 2, 1),
        "s_gu": np.concatenate([shared_gate, shared_up], 0).T.reshape(KC, P, 2 * SHARED).transpose(1, 0, 2),
        "s_down": shared_down.T.reshape(SHARED // P, P, D).transpose(1, 0, 2),
    }


def routing_constants():
    import numpy as np
    f, bf = np.float32, mybir.dt.np(BF16)
    i = np.arange(P)
    return {
        "before": (i[:, None] < i[None, :]).astype(bf),
        "ones_bf": np.ones((P, P), bf),
        "iota_e": np.broadcast_to(np.arange(E, dtype=f), (P, E)),
        "iota_bf": np.broadcast_to(np.arange(32, dtype=f).astype(bf), (P, 32)),
        "token": i.astype(f).reshape(P, 1),
    }


ATTENTION = ("wqk", "bqk", "wv", "bv", "wo", "bo")


def early_fusion(nc, a, out):
    def scratch(name, shape, dt):
        return nc.dram_tensor(name, shape, dt, kind="Internal").ap()

    h1 = scratch("h1", [T_ALL, D], F32)
    h2 = scratch("h2", [T_ALL, D], F32)
    xn1T = scratch("xn1T", [D, T_ALL], F32)
    xn2 = scratch("xn2", [T_ALL, D], F32)
    slots = scratch("slots", [E * CAP], F32)
    y = scratch("y", [E * CAP, D], F32)
    qk_t = scratch("qk_t", [2, NB, GROUPS, PARTS, GH * HD, S_IMG], BF16)
    qk_a = scratch("qk_a", [2, NB, GROUPS, PARTS, GH * HD, S_ALL], BF16)
    copy_text(nc, a["txt"], h1)
    attention_layer(nc, "t", False, a["xT"], *(a["t_" + n] for n in ATTENTION), a, qk_t, None, h1)
    layer_norm(nc, "n", h1, xn1T, a["ident_f"])
    attention_layer(nc, "a", True, xn1T, *(a["a_" + n] for n in ATTENTION), a, qk_a, h1, h2)
    experts_layer(nc, h2, xn2, slots, y, a, out)


def kernel(x, txt, L0_tok_w_qkv, L0_tok_b_qkv, L0_tok_w_out, L0_tok_b_out, L0_attn_W1, L0_attn_b1, L0_attn_W2,
           L0_attn_b2, L0_ffn_router_weight, L0_ffn_e_score_correction_bias, L0_ffn_gate_up_proj, L0_ffn_down_proj,
           L0_ffn_shared_gate, L0_ffn_shared_up, L0_ffn_shared_down):
    import numpy as np
    import concourse.bacc as bacc
    from concourse.bass_utils import run_bass_kernel_spmd

    n = np.asarray
    arrays = {"xT": n(x).reshape(NB * S_IMG, D).T, "txt": n(txt)}
    arrays.update({"t_" + k: v for k, v in attention_inputs(
        n(L0_tok_w_qkv).T, n(L0_tok_b_qkv), n(L0_tok_w_out).T, n(L0_tok_b_out)).items()})
    arrays.update({"a_" + k: v for k, v in attention_inputs(
        n(L0_attn_W1), n(L0_attn_b1), n(L0_attn_W2), n(L0_attn_b2)).items()})
    arrays.update(expert_inputs(n(L0_ffn_router_weight), n(L0_ffn_e_score_correction_bias), n(L0_ffn_gate_up_proj),
                                n(L0_ffn_down_proj), n(L0_ffn_shared_gate), n(L0_ffn_shared_up),
                                n(L0_ffn_shared_down)))
    arrays.update(constants())
    arrays.update(routing_constants())
    arrays = {k: np.ascontiguousarray(v) for k, v in arrays.items()}

    nc = bacc.Bacc("TRN2", target_bir_lowering=False, num_devices=1)
    aps = {k: nc.dram_tensor("in_" + k, v.shape, mybir.dt.from_np(v.dtype), kind="ExternalInput").ap()
           for k, v in arrays.items()}
    out = nc.dram_tensor("out", [T_ALL, D], F32, kind="ExternalOutput").ap()
    early_fusion(nc, aps, out)
    r = run_bass_kernel_spmd(nc, [{"in_" + k: v for k, v in arrays.items()}], core_ids=[0])
    return r.results[0]["out"].reshape(NB, S_ALL, D)
```

```python
from contextlib import ExitStack

import concourse.bass as bass
from concourse import mybir

ALU = mybir.AluOpType
ACT = mybir.ActivationFunctionType
AX = mybir.AxisListType
F32 = mybir.dt.float32
BF16 = mybir.dt.bfloat16
I32 = mybir.dt.int32
U32 = mybir.dt.uint32

P = 128
NB, S_IMG, S_TXT, D = 4, 512, 32, 256
S_ALL = S_IMG + S_TXT
T_ALL = NB * S_ALL
NT = T_ALL // P
HEADS, HD = 16, 16
GROUPS, GH = 4, 4
KC = D // P
PARTS = 3
STACK = 6 * HD
E, TOPK, INTER, SHARED, CAP = 32, 8, 128, 512, 512
LIMIT, ROUTE_SCALE, LN_EPS = 7.0, 2.5, 1e-5
CT = CAP // P
SCALE = HD ** -0.5


class Turns:

    def __init__(self, banks, segments):
        self.place, self.per = {}, {}
        before = [0] * banks
        for segment, names in segments:
            count = [0] * banks
            for i, name in enumerate(names):
                bank = i % banks
                count[bank] += 1
                self.place[segment, name] = (bank, before[bank] + count[bank])
            self.per[segment] = count
            times = NB - 2 if segment == "middle" else 1
            before = [x + times * y for x, y in zip(before, count)]

    def of(self, segment, b, name):
        bank, n = self.place[segment, name]
        if segment == "middle":
            return bank, (b * self.per[segment][bank]) + (n - self.per[segment][bank])
        return bank, n


def attention_layer(nc, tag, causal, xT, w_qk, b_qk, w_v, b_v, w_o, b_o, consts, qk_dram, residual, y_dram):
    S = S_ALL if causal else S_IMG
    TAIL = S - S_IMG
    KT = S_IMG // P
    VT = KT + (1 if causal else 0)
    R = STACK + 2
    G = GROUPS

    if causal:
        max_units = [(0, (0, 1, 2, 3)), (1, (0, 1)), (1, (2, 3))] + \
            [(i, (h,)) for i in (2, 3) for h in range(GH)] + [("tail", 0), ("tail", 1)]
    else:
        max_units = [(i, (h,)) for i in range(KT) for h in range(GH)]
    if causal:
        score_units = [(0, (h,)) for h in range(GH)] + [(1, (h,)) for h in range(GH)] + \
            [(2, (0, 1)), (2, (2, 3)), (3, (0, 1, 2, 3)), ("tail", 0), ("tail", 1)]
    else:
        score_units = [(j, (h,)) for j in range(KT) for h in range(GH)]
    MU, SU = len(max_units), len(score_units)
    units_of = [[u for u, (j, _) in enumerate(score_units) if j == jj] for jj in range(KT)]
    NPROB = sum(len(us) for us in units_of)
    v_pairs = [(t, min(t + 2, VT)) for t in range(0, VT, 2)]

    def score_steps(g):
        out, at = [], 0
        for j in range(KT):
            ahead = min(SU, units_of[j][-1] + 3)
            out += [("s", g, u) for u in range(at, ahead)] + [("av", g, j)]
            at = max(at, ahead)
        out += [("s", g, u) for u in range(at, SU)]
        return out + ([("ot", g)] if TAIL else [])

    def output_steps():
        c = [("ct", i) for i in range(len(v_pairs))]
        p = [("cp", i) for i in range(len(v_pairs))]
        return [c[0], c[1], p[0]] + ([c[2], p[1], p[2]] if len(c) > 2 else [p[1]])

    def project_steps():
        return ([("qt",)] if TAIL else []) + [("qk", m) for m in range(4)]

    def turned(db, g):
        return [("on", db, g)] + ([("nt", db, g)] if TAIL else [])

    def body_steps(first, last):
        out = []
        for k in range(G):
            score = score_steps(k)
            at = [((i + 0.5) / len(score), x) for i, x in enumerate(score)]
            if k < 2 or not last:
                at += [((i + 0.5) / MU, ("mx", k // 2, (k + 2) % G, u)) for i, u in enumerate(range(MU))]

            def put(lo, hi, steps):
                at.extend((lo + (hi - lo) * (i + 0.5) / len(steps), x) for i, x in enumerate(steps))

            if k == 0:
                put(0, 0.01, ([("load_x",)] if not last else []) + ([("load", 0, 3)] if not first else []) +
                    ([("load_res",)] if residual is not None and not first else []))
                put(0.01, 0.15, [("v", i) for i in range(len(v_pairs))])
                put(0.1, 0.3, [("tr", 0, 1)] + (turned(-1, 3) if not first else []))
                if not first:
                    put(0.3, 0.7, output_steps())
                if not last:
                    put(0.6, 1.0, project_steps())
            else:
                if k < 3 or not last:
                    put(0.05, 0.15, [("tr", (k + 1) // G, (k + 1) % G)])
                put(0.15, 0.3, turned(0, k - 1))
                if not last:
                    put(0.3 if k == 1 else 0.0, 0.4 if k == 1 else 0.01, [("load", 1, k - 1)])
                    if k == 1:
                        put(0.0, 0.01, [("load_xv",)])
            out += [x for _, x in sorted(at, key=lambda y: y[0])]
        return out

    prologue = [("load_x",), ("load_xv",)] + project_steps() + [("load", 1, g) for g in range(G)] + \
        [("mx", 1, 0, u) for u in range(MU)] + [("mx", 1, 1, u) for u in range(MU // 2)] + [("tr", 1, 0)] + \
        [("mx", 1, 1, u) for u in range(MU // 2, MU)]
    segments = [("prologue", prologue), ("first", body_steps(True, False)), ("middle", body_steps(False, False)),
                ("last", body_steps(False, True)),
                ("epilogue", ([("load_res",)] if residual is not None else []) + turned(-1, 3) + output_steps())]
    MISC_KINDS = ("tr", "ot", "on", "nt", "qt", "qk", "v", "ct", "cp")
    misc = Turns(2, [(n, [x for x in xs if x[0] in MISC_KINDS]) for n, xs in segments])
    scores = Turns(3, [(n, [x for x in xs if x[0] == "s"]) for n, xs in segments])

    ctx = ExitStack()
    with ctx:
        def sb(name, shape, dt):
            return ctx.enter_context(nc.sbuf_tensor(f"{tag}_{name}", shape, dt))

        def ps(name, shape, dt):
            return ctx.enter_context(nc.psum_tensor(f"{tag}_{name}", shape, dt))

        def sem(name):
            return ctx.enter_context(nc.semaphore(f"{tag}_{name}"))

        wqk = sb("wqk", [P, KC, 2 * D], F32)
        bqk = sb("bqk", [P, 4], F32)
        wv = sb("wv", [P, KC, D], F32)
        bv = sb("bv", [P, D], F32)
        wo = sb("wo", [P, KC, D], F32)
        bo = sb("bo", [P, D], F32)
        ident_bf = sb("ident_bf", [P, P], BF16)
        ident_f = sb("ident_f", [P, P], F32)
        mask_q = sb("mask_q", [P, P], BF16)
        mask_k = sb("mask_k", [P, P], BF16)
        mask_qt = sb("mask_qt", [P, S_TXT], BF16)
        xb = sb("xb", [P, KC, S], F32)
        xv = sb("xv", [P, KC, S], F32)
        q_stack = sb("q_stack", [P, G, GH, S], BF16)
        k_stack = sb("k_stack", [P, G, GH, S], BF16)
        qk_full = sb("qk_full", [P, 4, S], F32)
        qk_rest = sb("qk_rest", [P, 4, S], F32)
        qk_part = sb("qk_part", [P, 4, PARTS, S], BF16)
        v_ones = sb("v_ones", [P, VT, G, GH, 32], F32)
        probs = sb("probs", [P, NPROB, S_IMG], F32)
        probs_t = sb("probs_t", [P, 5 * P], F32)
        neg_max = sb("neg_max", [P, 2, KT, GH], F32)
        max_part = sb("max_part", [P, 2, KT, 2, GH], BF16)
        neg_max_t = sb("neg_max_t", [P, 2, 3], F32)
        max_part_t = sb("max_part_t", [P, 2, 2], BF16)
        max_rows = sb("max_rows", [2 * GH, 2, S_IMG], BF16)
        max_rows_t = sb("max_rows_t", [2, 2, P], BF16)
        o_raw = sb("o_raw", [P, 2, S], F32)
        o_inv = sb("o_inv", [P, G, VT, GH], F32)
        o_rows = sb("o_rows", [P, VT, D], F32)
        oT = sb("oT", [P, VT, KC, P], F32)
        res = sb("res", [P, VT, D], F32)
        base = sb("base", [P, VT, D], F32)
        y_rows = sb("y_rows", [P, VT, D], F32)

        mx = [ps(f"mx{i}", [P, 512], F32) for i in range(2)]
        sc = [ps(f"sc{i}", [P, 512], F32) for i in range(3)]
        ob = ps("ob", [P, 512], F32)
        ms = [ps(f"ms{i}", [P, 512], F32) for i in range(2)]

        s_const = sem("constants_loaded")
        s_preset = sem("presets_done")
        s_xb = sem("x_loaded")
        s_xv = sem("x_for_v_loaded")
        s_stack = [sem(f"stack{g}_loaded") for g in range(G)]
        s_mrow = [sem(f"max_rows{g}_loaded") for g in range(G)]
        s_qk_stored = sem("qk_stored")
        s_mx_ready = sem("max_scores_ready")
        s_mx_free = sem("max_banks_free")
        s_sc_ready = [sem(f"scores{i}_ready") for i in range(3)]
        s_exp = [sem(f"scores{i}_exp_done") for i in range(3)]
        s_av_done = sem("probs_used")
        s_o_read = sem("o_read")
        s_ms_ready = [sem(f"misc{i}_ready") for i in range(2)]
        s_ms_read = [sem(f"misc{i}_read") for i in range(2)]
        s_negt = sem("neg_max_tail_done")
        s_mhigh = sem("max_high_done")
        s_mpart = sem("max_parts_done")
        s_high = sem("qk_high_ready")
        s_rest = sem("qk_rest_ready")
        s_mid = sem("qk_mid_ready")
        s_low = sem("qk_low_ready")
        s_inv = sem("o_inverse_ready")
        s_res = sem("residual_loaded")
        s_base = sem("base_ready")
        s_out = sem("rows_stored")
        MROW = 16 * (4 if TAIL else 2)
        NP_ = len(v_pairs)

        block = ctx.enter_context(nc.Block())

        def run(eng, handle):
            for segment, steps in segments:
                if segment == "middle":
                    with eng.Fori(1, NB - 1) as b:
                        for x in steps:
                            handle(segment, b, x)
                else:
                    b = {"prologue": -1, "first": 0, "last": NB - 1, "epilogue": NB}[segment]
                    for x in steps:
                        handle(segment, b, x)

        def width(j):
            return S_IMG - (P * j if causal else 0)

        @block.sync
        def _(sp):
            for dst, src in ((wqk, w_qk), (bqk, b_qk), (wv, w_v), (bv, b_v), (wo, w_o), (bo, b_o),
                             (ident_bf, consts["ident_bf"]), (ident_f, consts["ident_f"]),
                             (mask_q, consts["mask_q"]), (mask_k, consts["mask_k"]), (mask_qt, consts["mask_qt"])):
                sp.dma_start(dst[:], src).then_inc(s_const, 16)
            x_dram = xT.rearrange("(c p) t -> p c t", p=P)

            def handle(segment, b, x):
                if x[0] == "load_x":
                    if segment != "prologue":
                        sp.wait_ge(s_high, b * 4 + 4)
                    sp.dma_start(xb[:], x_dram[:, :, bass.ds(b * S + S, S)]).then_inc(s_xb, 16)
                elif x[0] == "load_xv":
                    if segment != "prologue":
                        bank, n = misc.of(segment, b, ("v", NP_ - 1))
                        sp.wait_ge(s_ms_ready[bank], n)
                    sp.dma_start(xv[:], x_dram[:, :, bass.ds(b * S + S, S)]).then_inc(s_xv, 16)
                elif x[0] == "load_res":
                    sp.wait_ge(s_base, b)
                    rows = residual[bass.ds(b * S_ALL - S_ALL, S_ALL), :]
                    sp.dma_start(res[:, 0:KT, :], rows[0:S_IMG, :].rearrange("(t p) d -> p t d", p=P)
                                 ).then_inc(s_res, 16)
                    sp.dma_start(res[0:TAIL, KT, :], rows[S_IMG:S, :]).then_inc(s_res, 16)
                elif x[0] == "qk":
                    m = x[1]
                    sp.wait_ge(s_low, b * 4 + (m + 5))
                    for half in range(2):
                        dst = qk_dram[m // 2, bass.ds(b + 1, 1), 2 * (m % 2) + half]
                        sp.dma_start(dst.rearrange("b c p t -> p (b c) t"),
                                     qk_part[64 * half:64 * half + 64, m, :, :]).then_inc(s_qk_stored, 16)
                elif x[0] == "load":
                    _, db, g = x
                    if segment != "prologue":
                        sp.wait_ge(s_av_done, b * (G * KT) + (KT + (g + 1) * KT * db))
                    if db == 1 and g == 0:
                        sp.wait_ge(s_qk_stored, b * (16 * 8) + 2 * (16 * 8))
                    q = qk_dram[0, bass.ds(b + db, 1), g].rearrange("b c (h d) t -> (b c) d h t", h=GH)
                    k = qk_dram[1, bass.ds(b + db, 1), g].rearrange("b c (h d) t -> (b c) d h t", h=GH)
                    for j, (qp, kp) in enumerate(((0, 0), (1, 0), (2, 0), (0, 1), (1, 1), (0, 2))):
                        r = slice(HD * j, HD * j + HD)
                        sp.dma_start(q_stack[r, g], q[qp]).then_inc(s_stack[g], 16)
                        sp.dma_start(k_stack[r, g], k[kp]).then_inc(s_stack[g], 16)
                elif x[0] == "tr":
                    g = x[2]
                    bank, n = misc.of(segment, b, x)
                    sp.wait_ge(s_ms_read[bank], n + 1)
                    for part in range(2):
                        sp.dma_start(q_stack[STACK + part:STACK + part + 1, g, :, 0:S_IMG],
                                     max_rows[GH * part:GH * part + GH, g % 2, :]).then_inc(s_mrow[g], 16)
                        if TAIL:
                            sp.dma_start(q_stack[STACK + part:STACK + part + 1, g, :, S_IMG:S],
                                         max_rows_t[part:part + 1, g % 2, :].rearrange("p (h q) -> p h q", h=GH)
                                         ).then_inc(s_mrow[g], 16)
                elif x[0] == "cp":
                    lo, hi = v_pairs[x[1]]
                    bank, n = misc.of(segment, b, x)
                    sp.wait_ge(s_ms_read[bank], n + 1)
                    full = min(hi, KT)
                    y_b = y_dram[bass.ds(b * S_ALL - S_ALL, S_ALL), :]
                    if full > lo:
                        sp.dma_start(y_b[P * lo:P * full, :].rearrange("(t p) d -> p t d", p=P),
                                     y_rows[:, lo:full, :]).then_inc(s_out, 16)
                    else:
                        sp.dma_start(y_b[S_IMG:S, :], y_rows[0:TAIL, KT, :]).then_inc(s_out, 16)

            run(sp, handle)
            sp.wait_ge(s_out, 16 + 16 * NP_ * NB)

        @block.tensor
        def _(pe):
            pe.wait_ge(s_const, 16 * 11)
            pe.wait_ge(s_preset, 3)

            def handle(segment, b, x):
                kind = x[0]
                if kind in MISC_KINDS:
                    bank, n = misc.of(segment, b, x)
                    pe.wait_ge(s_ms_read[bank], n)
                    m_, done = ms[bank], s_ms_ready[bank]
                    m_bf = m_[:, :].bitcast(BF16)
                if kind == "mx":
                    _, db, g, u = x
                    i, hs = max_units[u]
                    if u == 0:
                        pe.wait_ge(s_stack[g], b * (16 * 12) + (db + 1) * (16 * 12))
                    pe.wait_ge(s_mx_free, b * (G * MU) + ((db * G + g) * MU + u + 1))
                    out = mx[(g * MU + u) % 2]
                    if i == "tail":
                        lo, w = (0, S_IMG) if hs == 0 else (S_IMG, TAIL)
                        for h in range(GH):
                            r = slice(32 * h, 32 * h + 32)
                            mm = pe.matmul(out[r, 0:w], q_stack[0:STACK, g, h, S_IMG:S],
                                           k_stack[0:STACK, g, h, lo:lo + w], start=True, stop=(hs == 0))
                            if hs == 1:
                                mm = pe.matmul(out[r, 0:w], ident_bf[:, 0:32], mask_qt[:, :], start=False, stop=True)
                    else:
                        w = P * (i + 1) if causal else S_IMG
                        for n_, h in enumerate(hs):
                            mm = pe.matmul(out[:, n_ * w:n_ * w + w], q_stack[0:STACK, g, h, P * i:P * i + P],
                                           k_stack[0:STACK, g, h, 0:w], start=True, stop=not causal)
                            if causal:
                                mm = pe.matmul(out[:, n_ * w + w - P:n_ * w + w], ident_bf[:, :], mask_q[:, :],
                                               start=False, stop=True)
                    mm.then_inc(s_mx_ready, 1)
                elif kind == "tr":
                    _, db, g = x
                    pe.wait_ge(s_mpart, b * G + (db * G + g + 1))
                    for i in range(KT):
                        mm = pe.transpose(m_bf[0:2 * GH, P * i:P * i + P],
                                          max_part[:, g % 2, i, :, :].rearrange("p a h -> p (a h)"), ident_bf[:, :])
                    if TAIL:
                        mm = pe.transpose(m_bf[0:2, 512:640], max_part_t[:, g % 2, :], ident_bf[:, :])
                    mm.then_inc(done, 1)
                elif kind == "s":
                    _, g, u = x
                    j, hs = score_units[u]
                    if u == 0:
                        pe.wait_ge(s_mrow[g], b * MROW + (16 + MROW))
                    bank, n = scores.of(segment, b, x)
                    pe.wait_ge(s_exp[bank], n)
                    out = sc[bank]
                    if (j, hs) == ("tail", 0):
                        for jj in range(KT):
                            for h in range(GH):
                                o = P * jj + 32 * h
                                mm = pe.matmul(out[:, o:o + 32], k_stack[0:R, g, h, P * jj:P * jj + P],
                                               q_stack[0:R, g, h, S_IMG:S], start=True, stop=True)
                    elif j == "tail":
                        for h in range(GH):
                            o = 32 * h
                            pe.matmul(out[0:32, o:o + 32], k_stack[0:R, g, h, S_IMG:S],
                                      q_stack[0:R, g, h, S_IMG:S], start=True, stop=False)
                            mm = pe.matmul(out[0:32, o:o + 32], ident_bf[:, 0:32], mask_k[:, 0:32],
                                           start=False, stop=True)
                    else:
                        w = width(j)
                        for n_, h in enumerate(hs):
                            o = n_ * w
                            mm = pe.matmul(out[:, o:o + w], k_stack[0:R, g, h, P * j:P * j + P],
                                           q_stack[0:R, g, h, S_IMG - w:S_IMG], start=True, stop=not causal)
                            if causal:
                                mm = pe.matmul(out[:, o:o + P], ident_bf[:, :], mask_k[:, :], start=False, stop=True)
                    mm.then_inc(s_sc_ready[bank], 1)
                elif kind == "av":
                    _, g, j = x
                    for u in units_of[j]:
                        bank, n = scores.of(segment, b, ("s", g, u))
                        pe.wait_ge(s_exp[bank], n + 1)
                    if j == 0:
                        pe.wait_ge(s_o_read, b * G + (g + 1))
                        if g == 0:
                            for i in range(NP_):
                                bank, n = misc.of(segment, b, ("v", i))
                                pe.wait_ge(s_ms_read[bank], n + 1)
                    w = width(j)
                    for u in units_of[j]:
                        for n_, h in enumerate(score_units[u][1]):
                            mm = pe.matmul(ob[32 * h:32 * h + 32, S_IMG - w:S_IMG], v_ones[:, j, g, h, :],
                                           probs[:, u, n_ * w:n_ * w + w], start=(j == 0), stop=(j == KT - 1),
                                           skip_group_check=True)
                    mm.then_inc(s_av_done, 1)
                elif kind == "ot":
                    g = x[1]
                    for u in (SU - 2, SU - 1):
                        bank, n = scores.of(segment, b, ("s", g, u))
                        pe.wait_ge(s_exp[bank], n + 1)
                    for jj in range(KT + 1):
                        for h in range(GH):
                            w = P if jj < KT else TAIL
                            mm = pe.matmul(m_[32 * h:32 * h + 32, 0:32], v_ones[0:w, jj, g, h, :],
                                           probs_t[0:w, P * jj + 32 * h:P * jj + 32 * h + 32], start=(jj == 0),
                                           stop=(jj == KT), skip_group_check=True)
                    mm.then_inc(done, 1)
                elif kind == "on":
                    _, db, g = x
                    pe.wait_ge(s_o_read, b * G + (db * G + g + 2))
                    for t in range(KT):
                        mm = pe.transpose(m_[:, P * t:P * t + P], o_raw[:, g % 2, P * t:P * t + P], ident_f[:, :])
                    mm.then_inc(done, 1)
                elif kind == "nt":
                    g = x[2]
                    pe.transpose(m_[0:TAIL, 0:P], o_raw[:, g % 2, S_IMG:S], ident_f[:, :]).then_inc(done, 1)
                elif kind in ("qt", "qk"):
                    if x in (project_steps()[0],):
                        pe.wait_ge(s_xb, b * 16 + 32)
                    for m in (range(4) if kind == "qt" else (x[1],)):
                        lo, w = (S_IMG, TAIL) if kind == "qt" else (0, S_IMG)
                        o = S_TXT * m if kind == "qt" else 0
                        for c in range(KC):
                            mm = pe.matmul(m_[:, o:o + w], wqk[:, c, P * m:P * m + P], xb[:, c, lo:lo + w],
                                           start=(c == 0), stop=(c == KC - 1))
                    mm.then_inc(done, 1)
                elif kind == "v":
                    lo, hi = v_pairs[x[1]]
                    if lo == 0:
                        pe.wait_ge(s_xv, b * 16 + 16)
                    for t in range(lo, hi):
                        w = P if t < KT else TAIL
                        o = D * (t - lo)
                        for c in range(KC):
                            mm = pe.matmul(m_[0:w, o:o + D], xv[:, c, P * t:P * t + w], wv[:, c, :],
                                           start=(c == 0), stop=(c == KC - 1))
                    mm.then_inc(done, 1)
                elif kind == "ct":
                    lo, hi = v_pairs[x[1]]
                    if lo == 0:
                        for y in turned(-1, 3):
                            bank2, n2 = misc.of(segment, b, y)
                            pe.wait_ge(s_ms_read[bank2], n2 + 1)
                    for t in range(lo, hi):
                        for c in range(KC):
                            o = D * (t - lo) + P * c
                            mm = pe.transpose(m_[:, o:o + P], o_rows[:, t, P * c:P * c + P], ident_f[:, :])
                    mm.then_inc(done, 1)
                elif kind == "cp":
                    lo, hi = v_pairs[x[1]]
                    bank2, n2 = misc.of(segment, b, ("ct", x[1]))
                    pe.wait_ge(s_ms_read[bank2], n2 + 1)
                    for t in range(lo, hi):
                        w = P if t < KT else TAIL
                        o = D * (t - lo)
                        for c in range(KC):
                            mm = pe.matmul(m_[0:w, o:o + D], oT[:, t, c, 0:w], wo[:, c, :], start=(c == 0),
                                           stop=(c == KC - 1))
                    mm.then_inc(done, 1)

            run(pe, handle)

        @block.scalar
        def _(act):
            act.wait_ge(s_const, 16 * 11)

            def handle(segment, b, x):
                kind = x[0]
                if kind in MISC_KINDS:
                    bank, n = misc.of(segment, b, x)
                    m_, read = ms[bank], s_ms_read[bank]
                if kind == "qt":
                    if segment != "prologue":
                        act.wait_ge(s_qk_stored, b * (16 * 8) + (16 * 8))
                    act.wait_ge(s_ms_ready[bank], n)
                    for m in range(4):
                        i = nc.scalar.activation(qk_full[:, m, S_IMG:S], m_[:, S_TXT * m:S_TXT * m + S_TXT],
                                                 ACT.Identity, bias=bqk[:, m:m + 1])
                    i.then_inc(read, 1)
                elif kind == "qk":
                    m = x[1]
                    if segment != "prologue":
                        act.wait_ge(s_qk_stored, b * (16 * 8) + (16 * 8))
                    act.wait_ge(s_ms_ready[bank], n)
                    nc.scalar.activation(qk_full[:, m, 0:S_IMG], m_[:, :], ACT.Identity,
                                         bias=bqk[:, m:m + 1]).then_inc(read, 1)
                    act.wait_ge(read, n + 1)
                    nc.scalar.activation(qk_part[:, m, 0, :], qk_full[:, m, :], ACT.Copy).then_inc(s_high, 1)
                    for mm in ((m - 1,) if m < 3 else (2, 3)):
                        if mm >= 0:
                            act.wait_ge(s_rest, b * 4 + (mm + 5))
                            nc.scalar.activation(qk_part[:, mm, 1, :], qk_rest[:, mm, :], ACT.Copy).then_inc(s_mid, 1)
                elif kind == "tr":
                    _, db, g = x
                    act.wait_ge(s_ms_ready[bank], n)
                    act.wait_ge(s_mrow[(g + 2) % G], b * MROW + (16 + MROW * (db + (1 if g >= 2 else 0))))
                    if TAIL:
                        nc.scalar.copy(max_rows_t[:, g % 2, :], m_[:, :].bitcast(BF16)[0:2, 512:640])
                    nc.scalar.copy(max_rows[:, g % 2, :], m_[:, :].bitcast(BF16)[0:2 * GH, 0:512]).then_inc(read, 1)
                elif kind == "s":
                    _, g, u = x
                    j, hs = score_units[u]
                    bank, n = scores.of(segment, b, x)
                    act.wait_ge(s_sc_ready[bank], n)
                    if (j, hs) == ("tail", 0):
                        nc.scalar.activation(probs_t[:, 0:512], sc[bank][:, :], ACT.Exp, scale=SCALE
                                             ).then_inc(s_exp[bank], 1)
                    elif j == "tail":
                        nc.scalar.activation(probs_t[0:32, 512:640], sc[bank][0:32, 0:P], ACT.Exp, scale=SCALE
                                             ).then_inc(s_exp[bank], 1)
                    else:
                        act.wait_ge(s_av_done, b * (G * KT) + (g * KT + j + 1))
                        w = width(j) * len(hs)
                        nc.scalar.activation(probs[:, u, 0:w], sc[bank][:, 0:w], ACT.Exp, scale=SCALE
                                             ).then_inc(s_exp[bank], 1)
                elif kind == "av" and x[2] == KT - 1:
                    g = x[1]
                    act.wait_ge(s_av_done, b * (G * KT) + ((g + 1) * KT + KT))
                    nc.scalar.copy(o_raw[:, g % 2, 0:S_IMG], ob[:, :]).then_inc(s_o_read, 1)
                elif kind == "ot":
                    g = x[1]
                    act.wait_ge(s_ms_ready[bank], n)
                    nc.scalar.copy(o_raw[:, g % 2, S_IMG:S], m_[:, 0:TAIL]).then_inc(read, 1)
                elif kind == "ct":
                    lo, hi = v_pairs[x[1]]
                    act.wait_ge(s_ms_ready[bank], n)
                    w = P if hi <= KT else TAIL
                    nc.scalar.copy(oT[:, lo:hi, :, 0:w], m_[:, 0:D * (hi - lo)].rearrange(
                        "p (t c q) -> p t c q", c=KC, q=P)[:, :, :, 0:w]).then_inc(read, 1)

            run(act, handle)

        @block.gpsimd
        def _(pool):
            pool.memset(v_ones[:], 1.0).then_inc(s_preset, 1)
            for q in (*s_exp, s_o_read, *s_ms_read, s_base):
                pool.sem_inc(q, 1)
            pool.sem_inc(s_mx_free, 2)
            pool.sem_inc(s_av_done, KT)
            for q in (*s_mrow, s_out):
                pool.sem_inc(q, 16)
            pool.wait_ge(s_const, 16 * 11)

            def handle(segment, b, x):
                if x[0] == "qk":
                    m = x[1]
                    pool.wait_ge(s_high, b * 4 + (m + 5))
                    nc.gpsimd.tensor_tensor(qk_rest[:, m, :], qk_full[:, m, :], qk_part[:, m, 0, :],
                                            ALU.subtract).then_inc(s_rest, 1)
                    for mm in ((m - 1,) if m < 3 else (2, 3)):
                        if mm >= 0:
                            pool.wait_ge(s_mid, b * 4 + (mm + 5))
                            nc.gpsimd.tensor_tensor(qk_part[:, mm, 2, :], qk_rest[:, mm, :], qk_part[:, mm, 1, :],
                                                    ALU.subtract).then_inc(s_low, 1)
                elif x[0] == "load_res":
                    pool.wait_ge(s_out, (b - 1) * (16 * NP_) + 16)
                    pool.wait_ge(s_res, b * 32)
                    nc.gpsimd.tensor_tensor(base[:, 0:KT, :], res[:, 0:KT, :],
                                            bo[:, None, :].to_broadcast([P, KT, D]), ALU.add)
                    nc.gpsimd.tensor_tensor(base[0:TAIL, KT, :], res[0:TAIL, KT, :], bo[0:TAIL, :],
                                            ALU.add).then_inc(s_base, 1)

            run(pool, handle)

        @block.vector
        def _(dve):
            nc.vector.memset(k_stack[STACK:R], 1.0).then_inc(s_preset, 1)
            nc.vector.memset(o_rows[:], 0.0).then_inc(s_preset, 1)
            dve.wait_ge(s_const, 16 * 11)
            dve.wait_ge(s_preset, 3)

            def handle(segment, b, x):
                kind = x[0]
                if kind in MISC_KINDS:
                    bank, n = misc.of(segment, b, x)
                    m_, read = ms[bank], s_ms_read[bank]
                if kind == "mx":
                    _, db, g, u = x
                    i, hs = max_units[u]
                    dve.wait_ge(s_mx_ready, b * (G * MU) + ((db * G + g) * MU + u + 1))
                    src = mx[(g * MU + u) % 2]
                    if i == "tail":
                        w = S_IMG if hs == 0 else TAIL
                        nc.vector.tensor_reduce(neg_max_t[:, g % 2, hs:hs + 1], src[:, 0:w], AX.X, ALU.max,
                                                negate=True).then_inc(s_mx_free, 1)
                    else:
                        w = P * (i + 1) if causal else S_IMG
                        nc.vector.tensor_reduce(
                            neg_max[:, g % 2, i, hs[0]:hs[0] + len(hs)],
                            src[:, 0:w * len(hs)].rearrange("p (h k) -> p h k", h=len(hs)), AX.X, ALU.max,
                            negate=True).then_inc(s_mx_free, 1)
                    if u == MU - 1:
                        dve.wait_ge(s_mx_free, b * (G * MU) + (2 + (db * G + g + 1) * MU))
                        nc.vector.tensor_copy(max_part[:, g % 2, :, 0, :], neg_max[:, g % 2]).then_inc(s_mhigh, 1)
                        k = 2 if TAIL else 1
                        if TAIL:
                            nc.vector.tensor_tensor(neg_max_t[:, g % 2, 2:3], neg_max_t[:, g % 2, 0:1],
                                                    neg_max_t[:, g % 2, 1:2], ALU.min).then_inc(s_negt, 1)
                            dve.wait_ge(s_negt, b * G + (db * G + g + 1))
                            nc.vector.tensor_copy(max_part_t[:, g % 2, 0:1], neg_max_t[:, g % 2, 2:3]
                                                  ).then_inc(s_mhigh, 1)
                        dve.wait_ge(s_mhigh, b * (G * k) + (db * G + g + 1) * k)
                        if TAIL:
                            nc.vector.tensor_tensor(max_part_t[:, g % 2, 1:2], neg_max_t[:, g % 2, 2:3],
                                                    max_part_t[:, g % 2, 0:1], ALU.subtract)
                        nc.vector.tensor_tensor(max_part[:, g % 2, :, 1, :], neg_max[:, g % 2],
                                                max_part[:, g % 2, :, 0, :], ALU.subtract).then_inc(s_mpart, 1)
                elif kind in ("on", "nt"):
                    _, db, g = x
                    k = 2 if TAIL else 1
                    count = (db * G + g) * k + (1 if kind == "on" else 2)
                    r, lo, hi = (slice(0, P), 0, KT) if kind == "on" else (slice(0, TAIL), KT, VT)
                    o = m_[r, 0:P * (hi - lo)].rearrange("p (t h d) -> p t h d", h=GH, d=32)
                    dve.wait_ge(s_ms_ready[bank], n)
                    nc.vector.reciprocal(o_inv[r, g, lo:hi, :], o[:, :, :, HD]).then_inc(s_inv, 1)
                    dve.wait_ge(s_inv, b * (G * k) + count)
                    nc.vector.tensor_tensor(
                        o_rows[r, lo:hi, 64 * g:64 * g + 64].rearrange("p t (h d) -> p t h d", h=GH), o[:, :, :, 0:HD],
                        o_inv[r, g, lo:hi, :, None].to_broadcast([r.stop, hi - lo, GH, HD]), ALU.mult).then_inc(read, 1)
                elif kind == "v":
                    lo, hi = v_pairs[x[1]]
                    dve.wait_ge(s_ms_ready[bank], n)
                    for t in range(lo, hi):
                        w = P if t < KT else TAIL
                        o = D * (t - lo)
                        i = nc.vector.tensor_tensor(
                            v_ones[0:w, t, :, :, 0:HD],
                            m_[0:w, o:o + D].rearrange("p (g h d) -> p g h d", g=G, h=GH),
                            bv[0:w, :].rearrange("p (g h d) -> p g h d", g=G, h=GH), ALU.add)
                    i.then_inc(read, 1)
                elif kind == "cp":
                    lo, hi = v_pairs[x[1]]
                    dve.wait_ge(s_ms_ready[bank], n)
                    if lo == 0:
                        dve.wait_ge(s_out, (b - 1) * (16 * NP_) + 16)
                        if residual is not None:
                            dve.wait_ge(s_base, b + 1)
                    for t in range(lo, hi):
                        w = P if t < KT else TAIL
                        o = D * (t - lo)
                        i = nc.vector.tensor_tensor(y_rows[0:w, t, :], m_[0:w, o:o + D],
                                                    bo[0:w, :] if residual is None else base[0:w, t, :], ALU.add)
                    i.then_inc(read, 1)

            run(dve, handle)


def layer_norm(nc, tag, h_dram, xT_dram, ident):
    ctx = ExitStack()
    with ctx:
        def sb(name, shape, dt):
            return ctx.enter_context(nc.sbuf_tensor(f"{tag}_{name}", shape, dt))

        def sem(name):
            return ctx.enter_context(nc.semaphore(f"{tag}_{name}"))

        h = sb("h", [P, NT, D], F32)
        xn = sb("xn", [P, NT, D], F32)
        xT = sb("xT", [P, KC, T_ALL], F32)
        idf = sb("ident", [P, P], F32)
        stats = sb("stats", [P, NT, 6], F32)
        mean_var = sb("mean_var", [P, NT, 2], F32)
        exponent = sb("exponent", [P, NT], F32)
        shifted = sb("shifted", [P, NT], F32)
        rstd = sb("rstd", [P, NT], F32)
        bank = [ctx.enter_context(nc.psum_tensor(f"{tag}_t{i}", [P, 512], F32)) for i in range(4)]
        s_in, s_stats, s_mv, s_shift, s_rstd, s_xn, s_t, s_x, s_out, s_id, s_exp = [
            sem(n) for n in ("h_loaded", "stats_done", "mean_var_done", "shifted", "rstd_ready", "xn_ready",
                             "turned", "xT_ready", "stored", "identity_loaded", "exponent_set")]
        block = ctx.enter_context(nc.Block())

        @block.sync
        def _(sp):
            sp.dma_start(h[:], h_dram.rearrange("(n p) d -> p n d", p=P)).then_inc(s_in, 16)
            sp.dma_start(idf[:], ident).then_inc(s_id, 16)
            sp.wait_ge(s_x, 2 * NT)
            sp.dma_start(xT_dram.rearrange("(c p) t -> p c t", p=P), xT[:]).then_inc(s_out, 16)
            sp.wait_ge(s_out, 16)

        @block.vector
        def _(dve):
            normalize_rows(nc, dve, h, xn, stats, mean_var, rstd, s_in, 16, s_stats, s_mv, s_rstd, s_xn)

        @block.gpsimd
        def _(pool):
            inverse_deviation(nc, pool, mean_var, shifted, exponent, rstd, s_mv, s_shift, s_exp, s_rstd)

        @block.tensor
        def _(pe):
            pe.wait_ge(s_id, 16)
            turn_rows(pe, xn, idf, bank, s_xn, s_x, s_t)

        @block.scalar
        def _(act):
            take_turned(nc, act, bank, xT, s_t, s_x)


def normalize_rows(nc, dve, h, xn, stats, mean_var, rstd, s_in, loaded, s_stats, s_mv, s_rstd, s_xn):
    dve.wait_ge(s_in, loaded)
    for t in range(NT):
        nc.vector.bn_stats(stats[:, t, :], h[:, t, :]).then_inc(s_stats, 1)
    for t in range(NT):
        dve.wait_ge(s_stats, t + 1)
        nc.vector.bn_aggr(mean_var[:, t, :], stats[:, t, :]).then_inc(s_mv, 1)
    dve.wait_ge(s_rstd, 1)
    for t in range(NT):
        nc.vector.tensor_scalar(xn[:, t, :], h[:, t, :], mean_var[:, t, 0:1], rstd[:, t:t + 1], ALU.subtract,
                                ALU.mult).then_inc(s_xn, 1)


def inverse_deviation(nc, pool, mean_var, shifted, exponent, rstd, s_mv, s_shift, s_exp, s_rstd):
    pool.memset(exponent[:], -0.5).then_inc(s_exp, 1)
    pool.wait_ge(s_mv, NT)
    nc.gpsimd.tensor_scalar(shifted[:], mean_var[:, :, 1], LN_EPS, 0.0, ALU.add, ALU.add).then_inc(s_shift, 1)
    pool.wait_ge(s_shift, 1)
    pool.wait_ge(s_exp, 1)
    nc.gpsimd.tensor_tensor(rstd[:], shifted[:], exponent[:], ALU.pow).then_inc(s_rstd, 1)


def turn_rows(pe, xn, idf, bank, s_xn, s_x, s_t):
    for t in range(NT):
        pe.wait_ge(s_xn, t + 1)
        if t >= 4:
            pe.wait_ge(s_x, 2 * (t - 3))
        for c in range(KC):
            mm = pe.transpose(bank[t % 4][:, P * c:P * c + P], xn[:, t, P * c:P * c + P], idf[:, :])
        mm.then_inc(s_t, 1)


def take_turned(nc, act, bank, xT, s_t, s_x):
    for t in range(NT):
        act.wait_ge(s_t, t + 1)
        nc.scalar.copy(xT[:, :, P * t:P * t + P], bank[t % 4][:, 0:KC * P].rearrange("p (c t) -> p c t", c=KC)
                       ).then_inc(s_x, 2)


def copy_text(nc, txt, h_dram):
    with ExitStack() as ctx:
        s_txt = ctx.enter_context(nc.semaphore("text_stored"))
        block = ctx.enter_context(nc.Block())

        @block.sync
        def _(sp):
            sp.dma_start(h_dram.rearrange("(b s) d -> b s d", b=NB)[:, S_IMG:S_ALL, :], txt).then_inc(s_txt, 16)
            sp.wait_ge(s_txt, 16)


def attention_inputs(w_cols, b_cols, w_rows, b_out):
    import numpy as np
    w = w_cols.reshape(D, HEADS, 3, HD)
    b = b_cols.reshape(HEADS, 3, HD)
    out = {"wqk": w[:, :, 0:2].transpose(0, 2, 1, 3).reshape(KC, P, 2 * D).transpose(1, 0, 2),
           "bqk": b[:, 0:2].transpose(1, 0, 2).reshape(4, P).T,
           "wv": w[:, :, 2].reshape(KC, P, D).transpose(1, 0, 2),
           "bv": np.broadcast_to(b[:, 2].reshape(1, D), (P, D))}
    out["wo"] = w_rows.reshape(KC, P, D).transpose(1, 0, 2)
    out["bo"] = np.broadcast_to(b_out.reshape(1, D), (P, D))
    return out


def constants():
    import numpy as np
    f, bf = np.float32, mybir.dt.np(BF16)
    i = np.arange(P)
    c = {"ident_f": np.eye(P, dtype=f), "ident_bf": np.eye(P, dtype=f).astype(bf)}
    later = np.where(i[None, :] > i[:, None], f(-1e30), f(0))
    c["mask_q"] = later.astype(bf)
    c["mask_k"] = later.T.astype(bf)
    qt = np.zeros((P, S_TXT), f)
    qt[0:S_TXT] = later[0:S_TXT, 0:S_TXT]
    c["mask_qt"] = qt.astype(bf)
    return c


def experts_layer(nc, h_dram, xn_dram, slots_dram, y_dram, w, out):
    NC2 = 2 * P
    CHUNKS = T_ALL // NC2
    ctx = ExitStack()
    with ctx:
        def sb(name, shape, dt, where=ctx):
            return where.enter_context(nc.sbuf_tensor(f"e_{name}", shape, dt))

        def sem(name):
            return ctx.enter_context(nc.semaphore(f"e_{name}"))

        h = sb("h", [P, NT, D], F32)
        xT = sb("xT", [P, KC, T_ALL], F32)
        idf = sb("ident", [P, P], F32)
        slot_of = sb("slot_of", [P, NT, TOPK], U32)
        weight_of = sb("weight_of", [P, NT, TOPK], F32)
        token_of = sb("token_of", [P, E * CT], U32)

        with ExitStack() as early:
            def se(name, shape, dt):
                return sb(name, shape, dt, early)

            xn = se("xn", [P, NT, D], F32)
            stats = se("stats", [P, NT, 6], F32)
            mean_var = se("mean_var", [P, NT, 2], F32)
            exponent = se("exponent", [P, NT], F32)
            shifted = se("shifted", [P, NT], F32)
            rstd = se("rstd", [P, NT], F32)
            router = se("router", [P, KC, E], F32)
            bias = se("bias", [P, E], F32)
            before = se("before", [P, P], BF16)
            ones = se("ones", [P, P], BF16)
            iota_e = se("iota_e", [P, E], F32)
            iota_bf = se("iota_bf", [P, 32], BF16)
            token = se("token", [P, 1], F32)
            scores = se("scores", [P, NT, E], F32)
            ranked = se("ranked", [P, NT, E], F32)
            top = se("top", [P, NT, TOPK], F32)
            struck = se("struck", [P, NT, E], F32)
            choice = se("choice", [P, NT, TOPK], U32)
            choice_f = se("choice_f", [P, NT, TOPK], F32)
            chosen = se("chosen", [P, NT, E], F32)
            chosen_bf = se("chosen_bf", [P, NT, E], BF16)
            count = se("count", [P, NT, E], BF16)
            pos = se("pos", [P, NT, E], F32)
            pos_in = se("pos_in", [P, NT, E], F32)
            total = se("total", [P, NT], F32)
            gain = se("gain", [P, NT, E], F32)
            pos_i = se("pos_i", [P, NT, E], I32)
            hi_i = se("hi_i", [P, NT, E], I32)
            lo_i = se("lo_i", [P, NT, E], I32)
            hi = se("hi", [P, NT, E], BF16)
            lo = se("lo", [P, NT, E], BF16)
            one_hi = se("one_hi", [P, NT, E, 32], BF16)
            one_lo = se("one_lo", [P, NT, E, 2, 16], BF16)
            pick = se("pick", [P, NT, TOPK, E], F32)
            picked = se("picked", [P, NT, TOPK, E], F32)
            slot_f = se("slot_f", [P, NT, TOPK], F32)
            parts = se("parts", [P, 8, 4, 2, 16], F32)
            table = se("table", [P, 8, 16], F32)
            rows = se("rows", [P, P], F32)
            bank = [early.enter_context(nc.psum_tensor(f"e_t{i}", [P, 512], F32)) for i in range(4)]
            pr = early.enter_context(nc.psum_tensor("e_pr", [P, 2, 512], F32))
            pt = early.enter_context(nc.psum_tensor("e_pt", [P, 2, 512], F32))
            (s_in, s_stats, s_mv, s_shift, s_rstd, s_xn, s_t, s_x, s_xn_out, s_exp, s_const, s_logits, s_sig, s_v,
             s_count, s_pos, s_onehot, s_table, s_rows_out, s_rows_in, s_rows_turned, s_tab) = [
                sem(n) for n in (
                    "h_loaded", "stats_done", "mean_var_done", "shifted", "rstd_ready", "xn_ready", "turned",
                    "xT_ready", "xn_stored", "exponent_set", "router_constants", "logits_ready", "exp_ready",
                    "vector_steps", "count_ready", "pos_ready", "onehot_ready", "table_ready", "table_stored",
                    "table_loaded", "table_turned", "table_rows_ready")]
            block = early.enter_context(nc.Block())

            @block.sync
            def _(sp):
                sp.dma_start(h[:], h_dram.rearrange("(n p) d -> p n d", p=P)).then_inc(s_in, 16)
                for dst, src in ((idf, w["ident_f"]), (router, w["router"]), (bias, w["e_bias"]),
                                 (before, w["before"]), (ones, w["ones_bf"]), (iota_e, w["iota_e"]),
                                 (iota_bf, w["iota_bf"]), (token, w["token"])):
                    sp.dma_start(dst[:], src).then_inc(s_const, 16)
                sp.wait_ge(s_xn, NT)
                sp.dma_start(xn_dram.rearrange("(n p) d -> p n d", p=P), xn[:]).then_inc(s_xn_out, 16)
                sp.wait_ge(s_tab, 4)
                sp.dma_start(slots_dram.rearrange("(g p l) -> p g l", p=P, l=16), table[:]).then_inc(s_rows_out, 16)
                sp.wait_ge(s_rows_out, 16)
                sp.dma_start(rows[:], slots_dram.rearrange("(r s) -> r s", s=P)).then_inc(s_rows_in, 16)
                sp.wait_ge(s_xn_out, 16)

            @block.gpsimd
            def _(pool):
                inverse_deviation(nc, pool, mean_var, shifted, exponent, rstd, s_mv, s_shift, s_exp, s_rstd)

            @block.scalar
            def _(act):
                take_turned(nc, act, bank, xT, s_t, s_x)
                act.wait_ge(s_logits, 1)
                nc.scalar.activation(scores[:, 0:16, :], pr[:, 0, :].rearrange("p (t e) -> p t e", e=E), ACT.Exp,
                                     scale=-1.0)
                nc.scalar.activation(scores[:, 16, :], pr[:, 1, 0:E], ACT.Exp, scale=-1.0).then_inc(s_sig, 1)

            @block.tensor
            def _(pe):
                pe.wait_ge(s_const, 16 * 8)
                turn_rows(pe, xn, idf, bank, s_xn, s_x, s_t)
                pe.wait_ge(s_x, 2 * NT)
                for t in range(NT):
                    for c in range(KC):
                        mm = pe.matmul(pr[:, t // 16, E * (t % 16):E * (t % 16) + E], xT[:, c, P * t:P * t + P],
                                       router[:, c, :], start=(c == 0), stop=(c == KC - 1))
                mm.then_inc(s_logits, 1)
                pe.wait_ge(s_count, NT)
                for t in range(NT):
                    o = pr[:, t // 16, E * (t % 16):E * (t % 16) + E]
                    mm = pe.matmul(o, before[:, :], chosen_bf[:, t, :], start=True, stop=False)
                    mm = pe.matmul(o, ones[:, :], count[:, t, :], start=False, stop=True)
                mm.then_inc(s_pos, 1)
                pe.wait_ge(s_onehot, 1)
                for g in range(8):
                    for t in range(NT):
                        mm = pe.matmul(pt[:, g // 4, P * (g % 4):P * (g % 4) + P],
                                       one_hi[:, t, 4 * g:4 * g + 4, :].rearrange("p e a -> p (e a)"),
                                       one_lo[:, t, 4 * g:4 * g + 4, :, :].rearrange("p e k b -> p (e k b)"),
                                       start=(t == 0), stop=(t == NT - 1))
                mm.then_inc(s_table, 1)
                pe.wait_ge(s_rows_in, 16)
                pe.transpose(bank[0][:, 0:P], rows[:, :], idf[:, :]).then_inc(s_rows_turned, 1)

            @block.vector
            def _(dve):
                normalize_rows(nc, dve, h, xn, stats, mean_var, rstd, s_in, 16, s_stats, s_mv, s_rstd, s_xn)
                steps = [0]

                def then(i):
                    steps[0] += 1
                    i.then_inc(s_v, 1)
                    dve.wait_ge(s_v, steps[0])

                v = nc.vector
                dve.wait_ge(s_const, 16 * 8)
                dve.wait_ge(s_sig, 1)
                then(v.tensor_scalar(scores[:], scores[:], 1.0, None, ALU.add))
                then(v.reciprocal(scores[:], scores[:]))
                then(v.tensor_tensor(ranked[:], scores[:], bias[:, None, :].to_broadcast([P, NT, E]), ALU.add))
                for t in range(NT):
                    i = v.max(top[:, t, :], ranked[:, t, :])
                then(i)
                for t in range(NT):
                    v.max_index(choice[:, t, :], top[:, t, :], ranked[:, t, :])
                for t in range(NT):
                    i = v.match_replace(struck[:, t, :], top[:, t, :], ranked[:, t, :], -3e38)
                then(i)
                then(v.tensor_tensor(chosen[:], struck[:], ranked[:], ALU.not_equal))
                v.memset(count[:, 0, :], 0.0).then_inc(s_count, 1)
                then(v.tensor_copy(chosen_bf[:], chosen[:]))
                for t in range(1, NT):
                    dve.wait_ge(s_count, t)
                    v.tensor_tensor(count[:, t, :], count[:, t - 1, :], chosen_bf[:, t - 1, :],
                                    ALU.add).then_inc(s_count, 1)
                then(v.tensor_tensor(gain[:], scores[:], chosen[:], ALU.mult))
                then(v.tensor_reduce(total[:], gain[:], AX.X, ALU.add))
                then(v.tensor_scalar(total[:], total[:], 1e-20, None, ALU.add))
                then(v.reciprocal(total[:], total[:]))
                then(v.tensor_tensor(gain[:], gain[:], total[:, :, None].to_broadcast([P, NT, E]), ALU.mult))
                then(v.tensor_scalar(gain[:], gain[:], ROUTE_SCALE, None, ALU.mult))
                then(v.tensor_copy(choice_f[:], choice[:]))
                dve.wait_ge(s_pos, 1)
                v.tensor_copy(pos[:, 0:16, :], pr[:, 0, :].rearrange("p (t e) -> p t e", e=E))
                then(v.tensor_copy(pos[:, 16, :], pr[:, 1, 0:E]))
                then(v.tensor_scalar(pos_in[:], chosen[:], -4096.0, 4096.0, ALU.mult, ALU.add))
                then(v.tensor_tensor(pos_in[:], pos_in[:], pos[:], ALU.add))
                then(v.tensor_copy(pos_i[:], pos_in[:]))
                v.tensor_scalar(hi_i[:], pos_i[:], 4, None, ALU.logical_shift_right)
                then(v.tensor_scalar(lo_i[:], pos_i[:], 15, None, ALU.bitwise_and))
                v.tensor_copy(hi[:], hi_i[:])
                then(v.tensor_copy(lo[:], lo_i[:]))
                for t in range(NT):
                    v.tensor_tensor(one_hi[:, t], hi[:, t, :, None].to_broadcast([P, E, 32]),
                                    iota_bf[:, None, :].to_broadcast([P, E, 32]), ALU.is_equal)
                    i = v.tensor_tensor(one_lo[:, t, :, 1, :], lo[:, t, :, None].to_broadcast([P, E, 16]),
                                        iota_bf[:, None, 0:16].to_broadcast([P, E, 16]), ALU.is_equal)
                then(i)
                for t in range(NT):
                    i = v.tensor_scalar(one_lo[:, t, :, 0, :], one_lo[:, t, :, 1, :], token[:, 0:1], None, ALU.mult)
                then(i)
                for t in range(NT):
                    i = v.tensor_scalar(one_lo[:, t, :, 1, :], one_lo[:, t, :, 1, :], float(t), None, ALU.mult)
                i.then_inc(s_onehot, 1)
                then(v.tensor_scalar(pos_in[:], pos[:], float(CAP), None, ALU.is_lt))
                then(v.tensor_tensor(gain[:], gain[:], pos_in[:], ALU.mult))
                then(v.tensor_scalar(pos[:], pos[:], float(CAP - 1), None, ALU.min))
                for t in range(NT):
                    i = v.tensor_tensor(pick[:, t], choice_f[:, t, :, None].to_broadcast([P, TOPK, E]),
                                        iota_e[:, None, :].to_broadcast([P, TOPK, E]), ALU.is_equal)
                then(i)
                for t in range(NT):
                    i = v.tensor_tensor(picked[:, t], pick[:, t], gain[:, t, None, :].to_broadcast([P, TOPK, E]),
                                        ALU.mult)
                then(i)
                then(v.tensor_reduce(weight_of[:], picked[:], AX.X, ALU.add))
                for t in range(NT):
                    i = v.tensor_tensor(picked[:, t], pick[:, t], pos[:, t, None, :].to_broadcast([P, TOPK, E]),
                                        ALU.mult)
                then(i)
                then(v.tensor_reduce(slot_f[:], picked[:], AX.X, ALU.add))
                then(v.tensor_scalar(choice_f[:], choice_f[:], float(CAP), None, ALU.mult))
                then(v.tensor_tensor(slot_f[:], slot_f[:], choice_f[:], ALU.add))
                then(v.tensor_copy(slot_of[:], slot_f[:]))
                dve.wait_ge(s_table, 1)
                v.tensor_copy(parts[:, 0:4], pt[:, 0, :].rearrange("p (g e k b) -> p g e k b", g=4, e=4, k=2))
                then(v.tensor_copy(parts[:, 4:8], pt[:, 1, :].rearrange("p (g e k b) -> p g e k b", g=4, e=4, k=2)))
                for e in range(4):
                    r = slice(32 * e, 32 * e + 32)
                    v.scalar_tensor_tensor(table[r], parts[r, :, e, 1, :], float(P), parts[r, :, e, 0, :], ALU.mult,
                                           ALU.add).then_inc(s_tab, 1)
                dve.wait_ge(s_rows_turned, 1)
                v.tensor_copy(token_of[:], bank[0][:, 0:P])

        gate_up = sb("gate_up", [P, 2, KC, 2 * INTER], F32)
        down = sb("down", [P, 2, D], F32)
        now = sb("now", [P, 2, CT], U32)
        xg = [[sb(f"xg{i}{c}", [P, D], F32) for c in range(CT)] for i in range(2)]
        xgT = sb("xgT", [P, 2, KC, CAP], F32)
        g_lim = sb("g_lim", [P, 2, CAP], F32)
        u_lim = sb("u_lim", [P, 2, CAP], F32)
        sg = sb("sg", [P, 2, CAP], F32)
        hid = sb("hid", [P, 2, CAP], F32)
        y = sb("y", [P, 2, CT, D], F32)
        pick_now = sb("pick_now", [P, 2, TOPK], U32)
        yg = [[sb(f"yg{i}{c}", [P, D], F32) for c in range(TOPK)] for i in range(2)]
        s_gu = sb("s_gu", [P, KC, 2 * SHARED], F32)
        s_down = sb("s_down", [P, SHARED // P, D], F32)
        s_g = sb("s_g", [P, 4, NC2], F32)
        s_e = sb("s_e", [P, 4, NC2], F32)
        s_h = sb("s_h", [P, 4, NC2], F32)
        acc = sb("acc", [P, 2, D], F32)
        res = sb("res", [P, 2, D], F32)
        tp = ctx.enter_context(nc.psum_tensor("e_tp", [P, KC, 512], F32))
        gu = ctx.enter_context(nc.psum_tensor("e_gu", [P, 2, 512], F32))
        yp = ctx.enter_context(nc.psum_tensor("e_yp", [P, 2, 512], F32))
        (q_w0, q_w1, q_now, q_g0, q_g1, q_free, q_tr, q_xT, q_gu, q_gl, q_ul, q_sig, q_s1, q_s2, q_hid, q_y, q_yr,
         q_st0, q_st1, q_sw, q_pick, q_c0, q_c1, q_cfree, q_sp, q_se, q_s3, q_s4, q_sh, q_sy, q_acc, q_out0, q_out1,
         q_res) = [
            sem(n) for n in (
                "weights0_loaded", "weights1_loaded", "indices_ready", "rows0_gathered", "rows1_gathered",
                "rows_turned", "turned_ready", "xT_taken", "gate_up_ready", "gate_limited", "up_limited",
                "gate_exp", "gate_denominator", "gate_inverse", "hidden_ready", "y_ready", "y_read", "y0_stored",
                "y1_stored", "shared_weights", "slots_ready", "results0_gathered", "results1_gathered",
                "results_summed", "shared_gate_up", "shared_exp", "shared_denominator", "shared_inverse",
                "shared_hidden", "shared_y", "sum_steps", "out0_stored", "out1_stored", "residual_added")]
        q_w, q_g, q_st, q_c, q_out = (q_w0, q_w1), (q_g0, q_g1), (q_st0, q_st1), (q_c0, q_c1), (q_out0, q_out1)
        block = ctx.enter_context(nc.Block())
        TAKE = SHARED // P

        @block.sync
        def _(sp):
            sp.dma_start(s_gu[:], w["s_gu"]).then_inc(q_sw, 16)
            sp.dma_start(s_down[:], w["s_down"]).then_inc(q_sw, 16)

            def load(i, k):
                sp.wait_ge(q_y, 2 * i + (k + 1))
                sp.dma_start(gate_up[:, k], w["gate_up"][bass.ds(2 * i + k, 1)].rearrange("e p c o -> p (e c) o")
                             ).then_inc(q_w[k], 16)
                sp.dma_start(down[:, k], w["down"][bass.ds(2 * i + k, 1)].rearrange("e p o -> p (e o)")
                             ).then_inc(q_w[k], 16)

            def store(i, k):
                sp.wait_ge(q_yr, 2 * i + (k + 3))
                sp.dma_start(y_dram[bass.ds((2 * i + k) * CAP, CAP), :].rearrange("(c p) d -> p c d", p=P),
                             y[:, k]).then_inc(q_st[k], 16)

            load(0, 0)
            load(0, 1)
            with sp.Fori(0, E // 2 - 1) as i:
                for k in range(2):
                    store(i, k)
                    load(i + 1, k)
            for k in range(2):
                store(E // 2 - 1, k)

            def store_out(i, k):
                sp.wait_ge(q_res, 2 * i + (k + 1))
                sp.dma_start(out[bass.ds((2 * i + k) * P, P), :], acc[:, k]).then_inc(q_out[k], 16)

            with sp.Fori(0, NT // 2) as i:
                for k in range(2):
                    store_out(i, k)
            store_out(NT // 2, 0)
            sp.wait_ge(q_out[0], 16 * (NT // 2 + 2))
            sp.wait_ge(q_out[1], 16 * (NT // 2 + 1))

        @block.gpsimd
        def _(pool):
            pool.sem_inc(q_y, 2)
            pool.sem_inc(q_free, 2)
            pool.sem_inc(q_yr, 2)
            pool.sem_inc(q_cfree, 2)
            for q in (q_xT, q_ul, q_sh, q_acc):
                pool.sem_inc(q, 1)
            for q in (*q_st, *q_out):
                pool.sem_inc(q, 16)

            def gather(i, k):
                pool.wait_ge(q_free, 2 * i + (k + 1))
                nc.gpsimd.tensor_copy(now[:, k, :], token_of[:, bass.ds((2 * i + k) * CT, CT)]).then_inc(q_now, 1)
                pool.drain()
                for c in range(CT):
                    pool.indirect_dma_start(xg[k][c][:, :], None, xn_dram,
                                            bass.IndirectOffsetOnAxis(now[:, k, c:c + 1], 0)).then_inc(q_g[k], 16)

            with pool.Fori(0, E // 2) as i:
                for k in range(2):
                    gather(i, k)
            for k in range(2):
                pool.wait_ge(q_st[k], 16 * (E // 2 + 1))

            def collect(i, k):
                pool.wait_ge(q_cfree, 2 * i + (k + 1))
                nc.gpsimd.tensor_copy(pick_now[:, k, :], slot_of[:, bass.ds(2 * i + k, 1), :].rearrange(
                    "p n c -> p (n c)")).then_inc(q_pick, 1)
                pool.drain()
                for c in range(TOPK):
                    pool.indirect_dma_start(yg[k][c][:, :], None, y_dram,
                                            bass.IndirectOffsetOnAxis(pick_now[:, k, c:c + 1], 0)
                                            ).then_inc(q_c[k], 16)

            with pool.Fori(0, NT // 2) as i:
                for k in range(2):
                    collect(i, k)
            collect(NT // 2, 0)

        @block.tensor
        def _(pe):
            def turn(i, k):
                pe.wait_ge(q_g[k], 16 * CT * (i + 1))
                pe.wait_ge(q_xT, 2 * (2 * i + k) + 1)
                for ch in range(KC):
                    for c in range(CT):
                        mm = pe.transpose(tp[:, ch, P * c:P * c + P], xg[k][c][:, P * ch:P * ch + P], idf[:, :])
                mm.then_inc(q_free, 1)

            def compute(i, k):
                pe.wait_ge(q_w[k], 32 * (i + 1))
                pe.wait_ge(q_xT, 2 * (2 * i + k) + 3)
                pe.wait_ge(q_ul, 2 * i + (k + 1))
                for half in range(2):
                    for ch in range(KC):
                        mm = pe.matmul(gu[:, half, :], gate_up[:, k, ch, INTER * half:INTER * half + INTER],
                                       xgT[:, k, ch, :], start=(ch == 0), stop=(ch == KC - 1))
                    mm.then_inc(q_gu, 1)

            def finish(i, k):
                pe.wait_ge(q_hid, 2 * i + (k + 1))
                pe.wait_ge(q_yr, 2 * i + (k + 2))
                for c in range(CT):
                    mm = pe.matmul(yp[:, c // 2, D * (c % 2):D * (c % 2) + D], hid[:, k, P * c:P * c + P], down[:, k, :],
                                   start=True, stop=True)
                mm.then_inc(q_y, 1)

            turn(0, 0)
            with pe.Fori(0, E // 2 - 1) as i:
                compute(i, 0)
                turn(i, 1)
                finish(i, 0)
                compute(i, 1)
                turn(i + 1, 0)
                finish(i, 1)
            n = E // 2 - 1
            compute(n, 0)
            turn(n, 1)
            finish(n, 0)
            compute(n, 1)
            finish(n, 1)
            pe.wait_ge(q_sw, 32)
            pe.wait_ge(q_yr, 2 + E)
            pe.wait_ge(q_ul, E + 1)

            def shared(i, wd, tiles):
                pe.wait_ge(q_sh, i + 1)
                for half, banks in ((0, tp), (1, gu)):
                    for f in range(TAKE):
                        for ch in range(KC):
                            mm = pe.matmul(banks[:, f // 2, NC2 * (f % 2):NC2 * (f % 2) + wd],
                                           s_gu[:, ch, SHARED * half + P * f:SHARED * half + P * f + P],
                                           xT[:, ch, bass.ds(i * NC2, wd)], start=(ch == 0), stop=(ch == KC - 1))
                mm.then_inc(q_sp, 1)
                pe.wait_ge(q_sh, i + 2)
                for t in range(tiles):
                    pe.wait_ge(q_acc, (2 * 9) * i + (9 * t + 1))
                    for f in range(TAKE):
                        mm = pe.matmul(yp[:, t, 0:D], s_h[:, f, P * t:P * t + P], s_down[:, f, :], start=(f == 0),
                                       stop=(f == TAKE - 1))
                    mm.then_inc(q_sy, 1)

            with pe.Fori(0, CHUNKS) as i:
                shared(i, NC2, 2)
            shared(CHUNKS, P, 1)

        @block.scalar
        def _(act):
            def take(i, k):
                act.wait_ge(q_free, 2 * i + (k + 3))
                for ch in range(KC):
                    nc.scalar.copy(xgT[:, k, ch, :], tp[:, ch, :]).then_inc(q_xT, 1)

            def sigmoid(i, k):
                act.wait_ge(q_gl, 2 * i + (k + 1))
                nc.scalar.activation(sg[:, k, :], g_lim[:, k, :], ACT.Exp, scale=-1.0).then_inc(q_sig, 1)

            def result(i, k):
                act.wait_ge(q_y, 2 * i + (k + 3))
                act.wait_ge(q_st[k], 16 * (i + 1))
                nc.scalar.copy(y[:, k].rearrange("p (a c) d -> p a (c d)", a=2), yp[:, :, :]).then_inc(q_yr, 1)

            take(0, 0)
            with act.Fori(0, E // 2 - 1) as i:
                sigmoid(i, 0)
                take(i, 1)
                result(i, 0)
                sigmoid(i, 1)
                take(i + 1, 0)
                result(i, 1)
            n = E // 2 - 1
            sigmoid(n, 0)
            take(n, 1)
            result(n, 0)
            sigmoid(n, 1)
            result(n, 1)

            def shared_exp(i, wd):
                act.wait_ge(q_sp, i + 1)
                act.wait_ge(q_sh, i + 1)
                nc.scalar.activation(s_e[:, :, 0:wd].rearrange("p (a b) t -> p a b t", a=2),
                                     tp[:, :, :].rearrange("p a (b t) -> p a b t", b=2)[:, :, :, 0:wd], ACT.Exp,
                                     scale=-1.0).then_inc(q_se, 1)

            with act.Fori(0, CHUNKS) as i:
                shared_exp(i, NC2)
            shared_exp(CHUNKS, P)

        @block.vector
        def _(dve):
            v = nc.vector

            def hidden(i, k):
                n = 2 * i + k
                dve.wait_ge(q_gu, 2 * n + 1)
                v.tensor_scalar(g_lim[:, k, :], gu[:, 0, :], LIMIT, None, ALU.min).then_inc(q_gl, 1)
                dve.wait_ge(q_gu, 2 * n + 2)
                v.tensor_scalar(u_lim[:, k, :], gu[:, 1, :], LIMIT, -LIMIT, ALU.min, ALU.max).then_inc(q_ul, 1)
                dve.wait_ge(q_sig, n + 1)
                v.tensor_scalar(sg[:, k, :], sg[:, k, :], 1.0, None, ALU.add).then_inc(q_s1, 1)
                dve.wait_ge(q_ul, n + 2)
                v.tensor_tensor(u_lim[:, k, :], u_lim[:, k, :], g_lim[:, k, :], ALU.mult)
                dve.wait_ge(q_s1, n + 1)
                v.reciprocal(sg[:, k, :], sg[:, k, :]).then_inc(q_s2, 1)
                dve.wait_ge(q_s2, n + 1)
                v.tensor_tensor(hid[:, k, :], u_lim[:, k, :], sg[:, k, :], ALU.mult).then_inc(q_hid, 1)

            with dve.Fori(0, E // 2) as i:
                for k in range(2):
                    hidden(i, k)

            def shared_hidden(i, wd):
                dve.wait_ge(q_se, i + 1)
                four = [P, 2, 2, wd]
                e4 = s_e[:, :, 0:wd].rearrange("p (a b) t -> p a b t", a=2)
                g4 = s_g[:, :, 0:wd].rearrange("p (a b) t -> p a b t", a=2)
                v.tensor_scalar(s_e[:, :, 0:wd], s_e[:, :, 0:wd], 1.0, None, ALU.add).then_inc(q_s3, 1)
                dve.wait_ge(q_s3, 3 * i + 1)
                v.reciprocal(s_e[:, :, 0:wd], s_e[:, :, 0:wd]).then_inc(q_s3, 1)
                dve.wait_ge(q_s3, 3 * i + 2)
                v.tensor_tensor(g4, tp[:, :, :].rearrange("p a (b t) -> p a b t", b=2)[:, :, :, 0:wd], e4,
                                ALU.mult).then_inc(q_s3, 1)
                dve.wait_ge(q_s3, 3 * i + 3)
                v.tensor_tensor(s_h[:, :, 0:wd].rearrange("p (a b) t -> p a b t", a=2),
                                gu[:, :, :].rearrange("p a (b t) -> p a b t", b=2)[:, :, :, 0:wd], g4,
                                ALU.mult).then_inc(q_sh, 1)

            def combine(i, k):
                dve.wait_ge(q_c[k], 16 * TOPK * (i + 1))
                dve.wait_ge(q_out[k], 16 * (i + 1))
                base = 18 * i + (9 * k + 1)
                wt = weight_of[:, bass.ds(2 * i + k, 1), :].rearrange("p n c -> p (n c)")
                v.tensor_scalar(acc[:, k], yg[k][0][:, :], wt[:, 0:1], None, ALU.mult).then_inc(q_acc, 1)
                for c in range(1, TOPK):
                    dve.wait_ge(q_acc, base + c)
                    v.scalar_tensor_tensor(acc[:, k], yg[k][c][:, :], wt[:, c:c + 1], acc[:, k], ALU.mult,
                                           ALU.add).then_inc(q_acc, 1)
                dve.wait_ge(q_acc, base + TOPK)
                dve.wait_ge(q_sy, 2 * i + (k + 1))
                v.tensor_tensor(acc[:, k], acc[:, k], yp[:, k, 0:D], ALU.add).then_inc(q_acc, 1)
                dve.wait_ge(q_acc, base + 9)
                v.tensor_tensor(acc[:, k], acc[:, k], h[:, bass.ds(2 * i + k, 1), :].rearrange("p n d -> p (n d)"),
                                ALU.add).then_inc(q_res, 1)
                dve.wait_ge(q_res, 2 * i + (k + 1))
                dve.sem_inc(q_cfree, 1)

            with dve.Fori(0, CHUNKS) as i:
                shared_hidden(i, NC2)
                combine(i, 0)
                combine(i, 1)
            shared_hidden(CHUNKS, P)
            combine(CHUNKS, 0)


def expert_inputs(router_weight, e_bias, gate_up, down, shared_gate, shared_up, shared_down):
    import numpy as np
    return {
        "router": router_weight.T.reshape(KC, P, E).transpose(1, 0, 2),
        "e_bias": np.broadcast_to(e_bias.reshape(1, E), (P, E)),
        "gate_up": gate_up.transpose(0, 2, 1).reshape(E, KC, P, 2 * INTER).transpose(0, 2, 1, 3),
        "down": down.transpose(0, 2, 1),
        "s_gu": np.concatenate([shared_gate, shared_up], 0).T.reshape(KC, P, 2 * SHARED).transpose(1, 0, 2),
        "s_down": shared_down.T.reshape(SHARED // P, P, D).transpose(1, 0, 2),
    }


def routing_constants():
    import numpy as np
    f, bf = np.float32, mybir.dt.np(BF16)
    i = np.arange(P)
    return {
        "before": (i[:, None] < i[None, :]).astype(bf),
        "ones_bf": np.ones((P, P), bf),
        "iota_e": np.broadcast_to(np.arange(E, dtype=f), (P, E)),
        "iota_bf": np.broadcast_to(np.arange(32, dtype=f).astype(bf), (P, 32)),
        "token": i.astype(f).reshape(P, 1),
    }


ATTENTION = ("wqk", "bqk", "wv", "bv", "wo", "bo")


def early_fusion(nc, a, out):
    def scratch(name, shape, dt):
        return nc.dram_tensor(name, shape, dt, kind="Internal").ap()

    h1 = scratch("h1", [T_ALL, D], F32)
    h2 = scratch("h2", [T_ALL, D], F32)
    xn1T = scratch("xn1T", [D, T_ALL], F32)
    xn2 = scratch("xn2", [T_ALL, D], F32)
    slots = scratch("slots", [E * CAP], F32)
    y = scratch("y", [E * CAP, D], F32)
    qk_t = scratch("qk_t", [2, NB, GROUPS, PARTS, GH * HD, S_IMG], BF16)
    qk_a = scratch("qk_a", [2, NB, GROUPS, PARTS, GH * HD, S_ALL], BF16)
    copy_text(nc, a["txt"], h1)
    attention_layer(nc, "t", False, a["xT"], *(a["t_" + n] for n in ATTENTION), a, qk_t, None, h1)
    layer_norm(nc, "n", h1, xn1T, a["ident_f"])
    attention_layer(nc, "a", True, xn1T, *(a["a_" + n] for n in ATTENTION), a, qk_a, h1, h2)
    experts_layer(nc, h2, xn2, slots, y, a, out)


def kernel(x, txt, L0_tok_w_qkv, L0_tok_b_qkv, L0_tok_w_out, L0_tok_b_out, L0_attn_W1, L0_attn_b1, L0_attn_W2,
           L0_attn_b2, L0_ffn_router_weight, L0_ffn_e_score_correction_bias, L0_ffn_gate_up_proj, L0_ffn_down_proj,
           L0_ffn_shared_gate, L0_ffn_shared_up, L0_ffn_shared_down):
    import numpy as np
    import concourse.bacc as bacc
    from concourse.bass_utils import run_bass_kernel_spmd

    n = np.asarray
    arrays = {"xT": n(x).reshape(NB * S_IMG, D).T, "txt": n(txt)}
    arrays.update({"t_" + k: v for k, v in attention_inputs(
        n(L0_tok_w_qkv).T, n(L0_tok_b_qkv), n(L0_tok_w_out).T, n(L0_tok_b_out)).items()})
    arrays.update({"a_" + k: v for k, v in attention_inputs(
        n(L0_attn_W1), n(L0_attn_b1), n(L0_attn_W2), n(L0_attn_b2)).items()})
    arrays.update(expert_inputs(n(L0_ffn_router_weight), n(L0_ffn_e_score_correction_bias), n(L0_ffn_gate_up_proj),
                                n(L0_ffn_down_proj), n(L0_ffn_shared_gate), n(L0_ffn_shared_up),
                                n(L0_ffn_shared_down)))
    arrays.update(constants())
    arrays.update(routing_constants())
    arrays = {k: np.ascontiguousarray(v) for k, v in arrays.items()}

    nc = bacc.Bacc("TRN2", target_bir_lowering=False, num_devices=1)
    aps = {k: nc.dram_tensor("in_" + k, v.shape, mybir.dt.from_np(v.dtype), kind="ExternalInput").ap()
           for k, v in arrays.items()}
    out = nc.dram_tensor("out", [T_ALL, D], F32, kind="ExternalOutput").ap()
    early_fusion(nc, aps, out)
    r = run_bass_kernel_spmd(nc, [{"in_" + k: v for k, v in arrays.items()}], core_ids=[0])
    return r.results[0]["out"].reshape(NB, S_ALL, D)
```

```python
from contextlib import ExitStack

import concourse.bass as bass
from concourse import mybir

ALU = mybir.AluOpType
ACT = mybir.ActivationFunctionType
AX = mybir.AxisListType
F32 = mybir.dt.float32
BF16 = mybir.dt.bfloat16
I32 = mybir.dt.int32
U32 = mybir.dt.uint32

P = 128
NB, S_IMG, S_TXT, D = 4, 512, 32, 256
S_ALL = S_IMG + S_TXT
T_ALL = NB * S_ALL
NT = T_ALL // P
HEADS, HD = 16, 16
GROUPS, GH = 4, 4
KC = D // P
PARTS = 3
STACK = 6 * HD
E, TOPK, INTER, SHARED, CAP = 32, 8, 128, 512, 512
LIMIT, ROUTE_SCALE, LN_EPS = 7.0, 2.5, 1e-5
CT = CAP // P
LATER = 12
SCALE = HD ** -0.5


class Turns:

    def __init__(self, banks, segments):
        self.place, self.per = {}, {}
        before = [0] * banks
        for segment, names in segments:
            count = [0] * banks
            for i, name in enumerate(names):
                bank = i % banks
                count[bank] += 1
                self.place[segment, name] = (bank, before[bank] + count[bank])
            self.per[segment] = count
            times = NB - 2 if segment == "middle" else 1
            before = [x + times * y for x, y in zip(before, count)]

    def of(self, segment, b, name):
        bank, n = self.place[segment, name]
        if segment == "middle":
            return bank, (b * self.per[segment][bank]) + (n - self.per[segment][bank])
        return bank, n


def attention_layer(nc, tag, causal, xT, w_qk, b_qk, w_v, b_v, w_o, b_o, consts, qk_dram, residual, txt, y_dram,
                    ynT_dram, yn_dram=None, router=None, odds_dram=None, following=None, projected=False):
    S = S_ALL if causal else S_IMG
    TAIL = S - S_IMG
    KT = S_IMG // P
    VT = KT + (1 if causal else 0)
    R = STACK + 2
    G = GROUPS
    ORDER = (0, 2, 1, 3)

    if causal:
        max_units = [(0, (0, 1, 2, 3)), (1, (0, 1)), (1, (2, 3))] + \
            [(i, (h,)) for i in (2, 3) for h in range(GH)] + [("tail", 0), ("tail", 1)]
    else:
        max_units = [(i, (h,)) for i in range(KT) for h in range(GH)]
    if causal:
        score_units = [(0, (h,)) for h in range(GH)] + [(1, (h,)) for h in range(GH)] + \
            [(2, (0, 1)), (2, (2, 3)), (3, (0, 1, 2, 3)), ("tail", 0), ("tail", 1)]
    else:
        score_units = [(j, (h,)) for j in range(KT) for h in range(GH)]
    MU, SU = len(max_units), len(score_units)
    AHEAD = MU // 2 + 2
    units_of = [[u for u, (j, _) in enumerate(score_units) if j == jj] for jj in range(KT)]
    NPROB = sum(len(us) for us in units_of)
    v_pairs = [(t, min(t + 2, VT)) for t in range(0, VT, 2)]

    def score_steps(g):
        out, at = [], 0
        for j in range(KT):
            ahead = min(SU, units_of[j][-1] + 5)
            out += [("s", g, u) for u in range(at, ahead)] + [("av", g, j)]
            at = max(at, ahead)
        out += [("s", g, u) for u in range(at, SU)]
        return out + ([("ot", g)] if TAIL else [])

    def output_steps():
        c = [("ct", i) for i in range(len(v_pairs))]
        p = [("cp", i) for i in range(len(v_pairs))]
        return [c[0], c[1], p[0]] + ([c[2], p[1], p[2]] if len(c) > 2 else [p[1]])

    def norm_steps():
        return [x for i in range(len(v_pairs)) for x in (("nm", i), ("nx", i))] + \
            ([("lg",)] if router is not None else []) + [("store_norm",)]

    def project_steps(tail=TAIL):
        return ([("qt",)] if tail else []) + [("qk", m) for m in range(4)]

    def projected_width(segment):
        return S_ALL if segment == "last" else S

    def turned(db, g):
        return [("on", db, g)] + ([("nt", db, g)] if TAIL else [])

    def body_steps(first, last):
        out = []
        for k in range(G):
            score = score_steps(k)
            at = [((i + 0.5) / len(score), x) for i, x in enumerate(score)]
            maxima = [("mx", k // 2, (k + 2) % G, u) for u in range(MU)] if k < 2 or not last else []
            if first and k == 0:
                second = [("mx", 0, 1, u) for u in range(AHEAD, MU)]
                at += [(0.5 * (i + 0.5) / len(second), x) for i, x in enumerate(second)]
                at += [(0.5 + 0.5 * (i + 0.5) / MU, x) for i, x in enumerate(maxima)]
            else:
                at += [((i + 0.5) / MU, x) for i, x in enumerate(maxima)]

            def put(lo, hi, steps):
                at.extend((lo + (hi - lo) * (i + 0.5) / len(steps), x) for i, x in enumerate(steps))

            if k == 0:
                put(0, 0.01, ([("load_x",)] if not last or following else []) + ([("load", 0, 3)] if not first else []) +
                    ([("load_res",)] if residual is not None and not first else []))
                put(*((-0.1, 0) if first else (0.01, 0.15)), [("v", i) for i in range(len(v_pairs))])
                put(0.5 if first else 0.1, 0.51 if first else 0.3,
                    [("tr", 0, 1)] + (turned(-1, 3) if not first else []))
                if not first:
                    put(0.3, 0.7, output_steps())
                if not last:
                    put(0.6, 1.0, project_steps())
                elif following:
                    put(0.6, 1.0, project_steps(S_TXT))
            else:
                if k < 3 or not last:
                    put(0.05, 0.15, [("tr", (k + 1) // G, (k + 1) % G)])
                put(0.15, 0.3, turned(0, k - 1))
                if k == 1 and not first:
                    put(0.1, 0.8, norm_steps())
                if not last:
                    put(0.3 if k == 1 else 0.0, 0.4 if k == 1 else 0.01, [("load", 1, k - 1)])
                    if k == 1:
                        put(0.0, 0.01, [("load_xv",)])
            out += [x for _, x in sorted(at, key=lambda y: y[0])]
        return out

    prologue = ([("load", 1, 0), ("load", 1, 1), ("load_xv",), ("load", 1, 2), ("load", 1, 3)] if projected else
                [("load_x",), ("load_xv",), ("norm_text",)] + project_steps() + [("load", 1, g) for g in range(G)]) + \
        [("mx", 1, 0, u) for u in range(MU)] + [("mx", 1, 1, u) for u in range(2)] + [("tr", 1, 0)] + \
        [("mx", 1, 1, u) for u in range(2, AHEAD)] + \
        ([("text",)] if residual is None else [])
    segments = [("prologue", prologue), ("first", body_steps(True, False)), ("middle", body_steps(False, False)),
                ("last", body_steps(False, True)),
                ("epilogue", ([("load_res",)] if residual is not None else []) + turned(-1, 3) + output_steps() +
                 norm_steps())]
    MISC_KINDS = ("tr", "ot", "on", "nt", "qt", "qk", "v", "ct", "cp", "nx", "lg", "text")
    misc = Turns(2, [(n, [x for x in xs if x[0] in MISC_KINDS]) for n, xs in segments])
    scores = Turns(3, [(n, [x for x in xs if x[0] == "s"]) for n, xs in segments])

    ctx = ExitStack()
    with ctx:
        def sb(name, shape, dt):
            return ctx.enter_context(nc.sbuf_tensor(f"{tag}_{name}", shape, dt))

        def ps(name, shape, dt):
            return ctx.enter_context(nc.psum_tensor(f"{tag}_{name}", shape, dt))

        def sem(name):
            return ctx.enter_context(nc.semaphore(f"{tag}_{name}"))

        wqk = sb("wqk", [P, KC, 2 * D], F32)
        bqk = sb("bqk", [P, 4], F32)
        wv = sb("wv", [P, KC, D], F32)
        bv = sb("bv", [P, D], F32)
        wo = sb("wo", [P, KC, D], F32)
        bo = sb("bo", [P, D], F32)
        ident_bf = sb("ident_bf", [P, P], BF16)
        ident_f = sb("ident_f", [P, P], F32)
        mask_q = sb("mask_q", [P, P], BF16)
        mask_k = sb("mask_k", [P, P], BF16)
        mask_qt = sb("mask_qt", [P, S_TXT], BF16)
        SX = S_ALL if following else S
        xb = sb("xb", [P, KC, SX], F32)
        xv = sb("xv", [P, KC, S], F32)
        q_stack = sb("q_stack", [P, G, GH, S], BF16)
        k_stack = sb("k_stack", [P, G, GH, S], BF16)
        qk_full = sb("qk_full", [P, 4, SX], F32)
        qk_rest = sb("qk_rest", [P, 4, SX], F32)
        qk_part = sb("qk_part", [P, 4, PARTS, SX], BF16)
        v_ones = sb("v_ones", [P, VT, G, GH, 32], F32)
        probs = sb("probs", [P, NPROB, S_IMG], F32)
        probs_t = sb("probs_t", [P, 5 * P], F32)
        neg_max = sb("neg_max", [P, 2, KT, GH], F32)
        max_part = sb("max_part", [P, 2, KT, 2, GH], BF16)
        neg_max_t = sb("neg_max_t", [P, 2, 3], F32)
        max_part_t = sb("max_part_t", [P, 2, 2], BF16)
        max_rows = sb("max_rows", [2 * GH, 2, S_IMG], BF16)
        max_rows_t = sb("max_rows_t", [2, 2, P], BF16)
        o_raw = sb("o_raw", [P, 2, S], F32)
        o_inv = sb("o_inv", [P, G, VT, GH], F32)
        o_rows = sb("o_rows", [P, VT, D], F32)
        oT = sb("oT", [P, VT, KC, P], F32)
        res = sb("res", [P, VT, D], F32)
        base = sb("base", [P, VT, D], F32)
        y_rows = sb("y_rows", [P, VT, D], F32)
        stats = sb("stats", [P, VT, 6], F32)
        mean_var = sb("mean_var", [P, VT, 2], F32)
        eps = sb("eps", [P, 2], F32)
        minus_half = sb("minus_half", [P, 2], F32)
        shifted = sb("shifted", [P, VT], F32)
        rstd = sb("rstd", [P, VT], F32)
        yn = sb("yn", [P, VT, D], F32)
        ynT = sb("ynT", [P, KC, VT * P], F32)
        w_router = sb("router", [P, KC, E], F32)
        odds = sb("odds", [P, VT, E], F32)

        mx = [ps(f"mx{i}", [P, 512], F32) for i in range(2)]
        sc = [ps(f"sc{i}", [P, 512], F32) for i in range(3)]
        ob = ps("ob", [P, 512], F32)
        ms = [ps(f"ms{i}", [P, 512], F32) for i in range(2)]

        s_first = sem("qk_weights_loaded")
        PRESETS = 2 + (1 if TAIL else 0)
        s_small = sem("maxima_constants_loaded")
        s_const = sem("constants_loaded")
        s_preset = sem("presets_done")
        s_xb = sem("x_loaded")
        s_xv = sem("x_for_v_loaded")
        s_stack = [sem(f"stack{g}_loaded") for g in range(G)]
        s_mrow = [sem(f"max_rows{g}_loaded") for g in range(G)]
        s_qk_stored = [sem(f"qk_of_groups{2 * i}{2 * i + 1}_stored") for i in range(2)]
        s_mx_ready = sem("max_scores_ready")
        s_mx_free = sem("max_banks_free")
        s_sc_ready = [sem(f"scores{i}_ready") for i in range(3)]
        s_exp = [sem(f"scores{i}_exp_done") for i in range(3)]
        s_av_done = sem("probs_used")
        s_o_read = sem("o_read")
        s_ms_ready = [sem(f"misc{i}_ready") for i in range(2)]
        s_ms_read = [sem(f"misc{i}_read") for i in range(2)]
        s_negt = sem("neg_max_tail_done")
        s_mhigh = sem("max_high_done")
        s_mpart = sem("max_parts_done")
        s_high = sem("qk_high_ready")
        s_rest = sem("qk_rest_ready")
        s_mid = sem("qk_mid_ready")
        s_low = sem("qk_low_ready")
        s_inv = sem("o_inverse_ready")
        s_res = sem("residual_loaded")
        s_base = sem("base_ready")
        s_out = sem("rows_stored")
        s_stats = sem("stats_done")
        s_dve = sem("vector_waited")
        s_sp = sem("sync_waited")
        s_set = sem("norm_constants_set")
        s_mv = sem("mean_var_done")
        s_shift = sem("variance_shifted")
        s_rstd = sem("inverse_deviation_ready")
        s_yn = sem("normalized_rows_ready")
        s_yn_out = sem("normalized_rows_stored")
        s_txt, s_txt_out = (sem("text_loaded"), sem("text_stored")) if txt is not None else (None, None)
        YN0 = 1 if txt is not None else 0
        YN = 16 * (1 + (4 if yn_dram is not None else 0))
        CONSTS = 16 * (6 + (1 if router is not None else 0))
        MROW = 16 * (4 if TAIL else 2)
        NP_ = len(v_pairs)

        block = ctx.enter_context(nc.Block())

        def run(eng, handle):
            for segment, steps in segments:
                if segment == "middle":
                    with eng.Fori(1, NB - 1) as b:
                        for x in steps:
                            handle(segment, b, x)
                else:
                    b = {"prologue": -1, "first": 0, "last": NB - 1, "epilogue": NB}[segment]
                    for x in steps:
                        handle(segment, b, x)

        def width(j):
            return S_IMG - (P * j if causal else 0)

        @block.sync
        def _(sp):
            def load_small():
                for dst, src in ((ident_bf, consts["ident_bf"]), (mask_q, consts["mask_q"]),
                                 (mask_qt, consts["mask_qt"])):
                    sp.dma_start(dst[:], src).then_inc(s_small, 16)

            def load_weights():
                for dst, src in ((wqk, w_qk), (bqk, b_qk)):
                    sp.dma_start(dst[:], src).then_inc(s_first, 16)

            if projected:
                load_small()
            else:
                load_weights()
            x_dram = xT.rearrange("(c p) t -> p c t", p=P)
            ynT_rows = ynT_dram.rearrange("(c p) t -> p c t", p=P)

            def handle(segment, b, x):
                if x[0] == "text":
                    bank, n = misc.of(segment, b, x)
                    sp.wait_ge(s_ms_read[bank], n + 1)
                    y_b = y_dram.rearrange("(b s) d -> b s d", b=NB)
                    sp.dma_start(y_b[:, S_IMG:S_ALL, :], txt).then_inc(s_txt_out, 16)
                    for c in range(KC):
                        sp.dma_start(ynT_rows[:, c, :].rearrange("p (b s) -> p b s", b=NB)[:, :, S_IMG:S_ALL],
                                     ynT[:, c, 0:P].rearrange("p (b s) -> p b s", b=NB)).then_inc(s_txt_out, 16)
                elif x[0] == "store_norm":
                    bank, n = misc.of(segment, b, ("nx", NP_ - 1) if router is None else ("lg",))
                    sp.wait_ge(s_ms_read[bank], n + 1)
                    sp.sem_inc(s_sp, 1)
                    sp.dma_start(ynT_rows[:, :, bass.ds(b * S_ALL - S_ALL, S)], ynT[:, :, 0:S]).then_inc(s_yn_out, 16)
                    if yn_dram is not None:
                        yn_b = yn_dram[bass.ds(b * S_ALL - S_ALL, S_ALL), :]
                        sp.dma_start(yn_b[0:S_IMG, 0:D].rearrange("(t p) d -> p t d", p=P), yn[:, 0:KT, :]
                                     ).then_inc(s_yn_out, 16)
                        sp.dma_start(yn_b[S_IMG:S, 0:D], yn[0:TAIL, KT, :]).then_inc(s_yn_out, 16)
                        odds_b = odds_dram[bass.ds(b * S_ALL - S_ALL, S_ALL), :]
                        sp.dma_start(odds_b[0:S_IMG, :].rearrange("(t p) e -> p t e", p=P), odds[:, 0:KT, :]
                                     ).then_inc(s_yn_out, 16)
                        sp.dma_start(odds_b[S_IMG:S, :], odds[0:TAIL, KT, :]).then_inc(s_yn_out, 16)
                elif x[0] == "load_x":
                    if segment != "prologue":
                        sp.wait_ge(s_high, b * 4 + 4)
                    if segment == "last":
                        sp.dma_start(wqk[:], following[0]).then_inc(s_first, 16)
                        sp.dma_start(bqk[:], following[1]).then_inc(s_first, 16)
                        sp.wait_ge(s_yn_out, 2 * YN)
                        sp.wait_ge(s_txt_out, 16 * (1 + KC))
                        sp.dma_start(xb[:], ynT_rows[:, :, 0:S_ALL]).then_inc(s_xb, 16)
                    else:
                        sp.dma_start(xb[:, :, 0:S], x_dram[:, :, bass.ds(b * S + S, S)]).then_inc(s_xb, 16)
                elif x[0] == "load_xv":
                    if segment != "prologue":
                        bank, n = misc.of(segment, b, ("v", NP_ - 1))
                        sp.wait_ge(s_ms_ready[bank], n)
                    sp.dma_start(xv[:], x_dram[:, :, bass.ds(b * S + S, S)]).then_inc(s_xv, 16)
                    if segment == "prologue":
                        if projected:
                            load_weights()
                        else:
                            load_small()
                        for dst, src in ((wv, w_v), (bv, b_v), (wo, w_o), (bo, b_o),
                                         (ident_f, consts["ident_f"]), (mask_k, consts["mask_k"])):
                            sp.dma_start(dst[:], src).then_inc(s_const, 16)
                        if router is not None:
                            sp.dma_start(w_router[:], router).then_inc(s_const, 16)
                elif x[0] == "load_res":
                    sp.wait_ge(s_base, b)
                    rows = residual[bass.ds(b * S_ALL - S_ALL, S_ALL), :]
                    sp.dma_start(res[:, 0:KT, :], rows[0:S_IMG, :].rearrange("(t p) d -> p t d", p=P)
                                 ).then_inc(s_res, 16)
                    sp.dma_start(res[0:TAIL, KT, :], rows[S_IMG:S, :]).then_inc(s_res, 16)
                elif x[0] == "qk":
                    m = ORDER[x[1]]
                    sp.wait_ge(s_low, b * 4 + (x[1] + 5))
                    if segment == "last":
                        dst = following[2][m // 2, 0:1, m % 2]
                    else:
                        dst = qk_dram[m // 2, bass.ds(b + 1, 1), m % 2]
                    sp.dma_start(dst.rearrange("b c p t -> p (b c) t"), qk_part[:, m, :, 0:projected_width(segment)]
                                 ).then_inc(s_qk_stored[m % 2], 16)
                elif x[0] == "load":
                    _, db, g = x
                    if segment != "prologue":
                        sp.wait_ge(s_av_done, b * (G * KT) + (KT + (g + 1) * KT * db))
                    if db == 1 and g % 2 == 0:
                        sp.wait_ge(s_qk_stored[g // 2], b * 32 + 64)
                    rows = slice(64 * (g % 2), 64 * (g % 2) + 64)
                    q, k = (qk_dram[a, bass.ds(b + db, 1), g // 2].rearrange("b c p t -> (b c) p t")[:, rows, :]
                            .rearrange("c (d h) t -> c d (h t)", h=GH) for a in range(2))
                    for at, n in ((0, 3), (3, 2), (5, 1)):
                        r = slice(HD * at, HD * (at + n))
                        sp.dma_start(q_stack[r, g].rearrange("p h t -> p (h t)"), q[0:n]
                                     ).then_inc(s_stack[g], 16)
                        sp.dma_start(k_stack[r, g].rearrange("p h t -> p (h t)"),
                                     k[3 - n:4 - n].to_broadcast([n, HD, GH * S])).then_inc(s_stack[g], 16)
                elif x[0] == "tr":
                    g = x[2]
                    bank, n = misc.of(segment, b, x)
                    sp.wait_ge(s_ms_read[bank], n + 1)
                    for part in range(2):
                        sp.dma_start(q_stack[STACK + part:STACK + part + 1, g, :, 0:S_IMG],
                                     max_rows[GH * part:GH * part + GH, g % 2, :]).then_inc(s_mrow[g], 16)
                        if TAIL:
                            sp.dma_start(q_stack[STACK + part:STACK + part + 1, g, :, S_IMG:S],
                                         max_rows_t[part:part + 1, g % 2, :].rearrange("p (h q) -> p h q", h=GH)
                                         ).then_inc(s_mrow[g], 16)
                elif x[0] == "cp":
                    lo, hi = v_pairs[x[1]]
                    bank, n = misc.of(segment, b, x)
                    sp.wait_ge(s_ms_read[bank], n + 1)
                    full = min(hi, KT)
                    y_b = y_dram[bass.ds(b * S_ALL - S_ALL, S_ALL), :]
                    if full > lo:
                        sp.dma_start(y_b[P * lo:P * full, :].rearrange("(t p) d -> p t d", p=P),
                                     y_rows[:, lo:full, :]).then_inc(s_out, 16)
                    else:
                        sp.dma_start(y_b[S_IMG:S, :], y_rows[0:TAIL, KT, :]).then_inc(s_out, 16)

            if txt is not None:
                sp.dma_start(y_rows[:, 0, :], txt.rearrange("b s d -> (b s) d")).then_inc(s_txt, 16)
            run(sp, handle)
            sp.wait_ge(s_out, 16 + 16 * NP_ * NB)
            sp.wait_ge(s_yn_out, YN * (NB + 1))
            if following:
                for stored in s_qk_stored:
                    sp.wait_ge(stored, 32 * (NB + 1))
            if txt is not None:
                sp.wait_ge(s_txt_out, 16 * (1 + KC))

        @block.tensor
        def _(pe):
            def handle(segment, b, x):
                kind = x[0]
                if kind in MISC_KINDS:
                    bank, n = misc.of(segment, b, x)
                    pe.wait_ge(s_ms_read[bank], n)
                    m_, done = ms[bank], s_ms_ready[bank]
                    m_bf = m_[:, :].bitcast(BF16)
                if kind == "mx":
                    _, db, g, u = x
                    i, hs = max_units[u]
                    if segment == "prologue" and u == 0:
                        pe.wait_ge(s_small, 16 * 3)
                    if u == 0:
                        pe.wait_ge(s_stack[g], b * (16 * 6) + (db + 1) * (16 * 6))
                    pe.wait_ge(s_mx_free, b * (G * MU) + ((db * G + g) * MU + u + 1))
                    out = mx[(g * MU + u) % 2]
                    if i == "tail":
                        lo, w = (0, S_IMG) if hs == 0 else (S_IMG, TAIL)
                        for h in range(GH):
                            r = slice(32 * h, 32 * h + 32)
                            mm = pe.matmul(out[r, 0:w], q_stack[0:STACK, g, h, S_IMG:S],
                                           k_stack[0:STACK, g, h, lo:lo + w], start=True, stop=(hs == 0))
                            if hs == 1:
                                mm = pe.matmul(out[r, 0:w], ident_bf[:, 0:32], mask_qt[:, :], start=False, stop=True)
                    else:
                        w = P * (i + 1) if causal else S_IMG
                        for n_, h in enumerate(hs):
                            mm = pe.matmul(out[:, n_ * w:n_ * w + w], q_stack[0:STACK, g, h, P * i:P * i + P],
                                           k_stack[0:STACK, g, h, 0:w], start=True, stop=not causal)
                            if causal:
                                mm = pe.matmul(out[:, n_ * w + w - P:n_ * w + w], ident_bf[:, :], mask_q[:, :],
                                               start=False, stop=True)
                    mm.then_inc(s_mx_ready, 1)
                elif kind == "tr":
                    _, db, g = x
                    pe.wait_ge(s_mpart, b * G + (db * G + g + 1))
                    for i in range(KT):
                        mm = pe.transpose(m_bf[0:2 * GH, P * i:P * i + P],
                                          max_part[:, g % 2, i, :, :].rearrange("p a h -> p (a h)"), ident_bf[:, :])
                    if TAIL:
                        mm = pe.transpose(m_bf[0:2, 512:640], max_part_t[:, g % 2, :], ident_bf[:, :])
                    mm.then_inc(done, 1)
                elif kind == "s":
                    _, g, u = x
                    j, hs = score_units[u]
                    if segment == "first" and (g, u) == (0, 0):
                        pe.wait_ge(s_const, CONSTS)
                        pe.wait_ge(s_set, 1)
                        pe.wait_ge(s_preset, PRESETS)
                    if u == 0:
                        pe.wait_ge(s_mrow[g], b * MROW + (16 + MROW))
                    bank, n = scores.of(segment, b, x)
                    pe.wait_ge(s_exp[bank], n)
                    out = sc[bank]
                    if (j, hs) == ("tail", 0):
                        for jj in range(KT):
                            for h in range(GH):
                                o = P * jj + 32 * h
                                mm = pe.matmul(out[:, o:o + 32], k_stack[0:R, g, h, P * jj:P * jj + P],
                                               q_stack[0:R, g, h, S_IMG:S], start=True, stop=True)
                    elif j == "tail":
                        for h in range(GH):
                            o = 32 * h
                            pe.matmul(out[0:32, o:o + 32], k_stack[0:R, g, h, S_IMG:S],
                                      q_stack[0:R, g, h, S_IMG:S], start=True, stop=False)
                            mm = pe.matmul(out[0:32, o:o + 32], ident_bf[:, 0:32], mask_k[:, 0:32],
                                           start=False, stop=True)
                    else:
                        w = width(j)
                        for n_, h in enumerate(hs):
                            o = n_ * w
                            mm = pe.matmul(out[:, o:o + w], k_stack[0:R, g, h, P * j:P * j + P],
                                           q_stack[0:R, g, h, S_IMG - w:S_IMG], start=True, stop=not causal)
                            if causal:
                                mm = pe.matmul(out[:, o:o + P], ident_bf[:, :], mask_k[:, :], start=False, stop=True)
                    mm.then_inc(s_sc_ready[bank], 1)
                elif kind == "av":
                    _, g, j = x
                    for u in units_of[j]:
                        bank, n = scores.of(segment, b, ("s", g, u))
                        pe.wait_ge(s_exp[bank], n + 1)
                    if j == 0:
                        pe.wait_ge(s_o_read, b * G + (g + 1))
                        if g == 0:
                            for i in range(NP_):
                                bank, n = misc.of(segment, b, ("v", i))
                                pe.wait_ge(s_ms_read[bank], n + 1)
                    w = width(j)
                    for u in units_of[j]:
                        for n_, h in enumerate(score_units[u][1]):
                            mm = pe.matmul(ob[32 * h:32 * h + 32, S_IMG - w:S_IMG], v_ones[:, j, g, h, :],
                                           probs[:, u, n_ * w:n_ * w + w], start=(j == 0), stop=(j == KT - 1),
                                           skip_group_check=True)
                    mm.then_inc(s_av_done, 1)
                elif kind == "ot":
                    g = x[1]
                    for u in (SU - 2, SU - 1):
                        bank, n = scores.of(segment, b, ("s", g, u))
                        pe.wait_ge(s_exp[bank], n + 1)
                    for jj in range(KT + 1):
                        for h in range(GH):
                            w = P if jj < KT else TAIL
                            mm = pe.matmul(m_[32 * h:32 * h + 32, 0:32], v_ones[0:w, jj, g, h, :],
                                           probs_t[0:w, P * jj + 32 * h:P * jj + 32 * h + 32], start=(jj == 0),
                                           stop=(jj == KT), skip_group_check=True)
                    mm.then_inc(done, 1)
                elif kind == "on":
                    _, db, g = x
                    pe.wait_ge(s_o_read, b * G + (db * G + g + 2))
                    for t in range(KT):
                        mm = pe.transpose(m_[:, P * t:P * t + P], o_raw[:, g % 2, P * t:P * t + P], ident_f[:, :])
                    mm.then_inc(done, 1)
                elif kind == "nt":
                    g = x[2]
                    pe.transpose(m_[0:TAIL, 0:P], o_raw[:, g % 2, S_IMG:S], ident_f[:, :]).then_inc(done, 1)
                elif kind in ("qt", "qk"):
                    if kind == "qt" or x[1] == 0:
                        pe.wait_ge(s_first, 64 if segment == "last" else 32)
                        pe.wait_ge(s_xb, b * 16 + 32)
                    for m in (range(4) if kind == "qt" else (ORDER[x[1]],)):
                        lo, w = (S_IMG, S_TXT) if kind == "qt" else (0, S_IMG)
                        o = S_TXT * m if kind == "qt" else 0
                        for c in range(KC):
                            mm = pe.matmul(m_[:, o:o + w], wqk[:, c, P * m:P * m + P], xb[:, c, lo:lo + w],
                                           start=(c == 0), stop=(c == KC - 1))
                    mm.then_inc(done, 1)
                elif kind == "v":
                    lo, hi = v_pairs[x[1]]
                    if segment == "first" and lo == 0:
                        pe.wait_ge(s_const, CONSTS)
                    if lo == 0:
                        pe.wait_ge(s_xv, b * 16 + 16)
                    for t in range(lo, hi):
                        w = P if t < KT else TAIL
                        o = D * (t - lo)
                        for c in range(KC):
                            mm = pe.matmul(m_[0:w, o:o + D], xv[:, c, P * t:P * t + w], wv[:, c, :],
                                           start=(c == 0), stop=(c == KC - 1))
                    mm.then_inc(done, 1)
                elif kind == "ct":
                    lo, hi = v_pairs[x[1]]
                    if lo == 0:
                        for y in turned(-1, 3):
                            bank2, n2 = misc.of(segment, b, y)
                            pe.wait_ge(s_ms_read[bank2], n2 + 1)
                    for t in range(lo, hi):
                        for c in range(KC):
                            o = D * (t - lo) + P * c
                            mm = pe.transpose(m_[:, o:o + P], o_rows[:, t, P * c:P * c + P], ident_f[:, :])
                    mm.then_inc(done, 1)
                elif kind == "lg":
                    bank2, n2 = misc.of(segment, b, ("nx", NP_ - 1))
                    pe.wait_ge(s_ms_read[bank2], n2 + 1)
                    for t in range(VT):
                        w = P if t < KT else TAIL
                        for c in range(KC):
                            mm = pe.matmul(m_[0:w, E * t:E * t + E], ynT[:, c, P * t:P * t + w], w_router[:, c, :],
                                           start=(c == 0), stop=(c == KC - 1))
                    mm.then_inc(done, 1)
                elif kind in ("nx", "text"):
                    if kind == "text":
                        lo, hi = 0, 1
                        pe.wait_ge(s_const, CONSTS)
                        pe.wait_ge(s_yn, 1)
                    else:
                        lo, hi = v_pairs[x[1]]
                        pe.wait_ge(s_yn, (b - 1) * VT + (hi + YN0))
                    for t in range(lo, hi):
                        for c in range(KC):
                            o = D * (t - lo) + P * c
                            mm = pe.transpose(m_[:, o:o + P], yn[:, t, P * c:P * c + P], ident_f[:, :])
                    mm.then_inc(done, 1)
                elif kind == "cp":
                    lo, hi = v_pairs[x[1]]
                    bank2, n2 = misc.of(segment, b, ("ct", x[1]))
                    pe.wait_ge(s_ms_read[bank2], n2 + 1)
                    for t in range(lo, hi):
                        w = P if t < KT else TAIL
                        o = D * (t - lo)
                        for c in range(KC):
                            mm = pe.matmul(m_[0:w, o:o + D], oT[:, t, c, 0:w], wo[:, c, :], start=(c == 0),
                                           stop=(c == KC - 1))
                    mm.then_inc(done, 1)

            run(pe, handle)

        @block.scalar
        def _(act):
            def handle(segment, b, x):
                kind = x[0]
                if kind in MISC_KINDS:
                    bank, n = misc.of(segment, b, x)
                    m_, read = ms[bank], s_ms_read[bank]
                if kind == "qt":
                    if segment != "prologue":
                        for stored in s_qk_stored:
                            act.wait_ge(stored, b * 32 + 32)
                    act.wait_ge(s_ms_ready[bank], n)
                    act.wait_ge(s_first, 64 if segment == "last" else 32)
                    for m in range(4):
                        i = nc.scalar.activation(qk_full[:, m, S_IMG:S_ALL], m_[:, S_TXT * m:S_TXT * m + S_TXT],
                                                 ACT.Identity, bias=bqk[:, m:m + 1])
                    i.then_inc(read, 1)
                elif kind == "qk":
                    step = x[1]
                    m = ORDER[step]
                    if segment == "prologue" or (projected and segment == "first"):
                        act.wait_ge(s_first, 32)
                    if segment != "prologue":
                        for stored in s_qk_stored:
                            act.wait_ge(stored, b * 32 + 32)
                    act.wait_ge(s_ms_ready[bank], n)
                    nc.scalar.activation(qk_full[:, m, 0:S_IMG], m_[:, :], ACT.Identity,
                                         bias=bqk[:, m:m + 1]).then_inc(read, 1)
                    act.wait_ge(read, n + 1)
                    wd = projected_width(segment)
                    nc.scalar.activation(qk_part[:, m, 0, 0:wd], qk_full[:, m, 0:wd], ACT.Copy).then_inc(s_high, 1)
                    for ss in ((step - 1,) if step < 3 else (2, 3)):
                        if ss >= 0:
                            act.wait_ge(s_rest, b * 4 + (ss + 5))
                            nc.scalar.activation(qk_part[:, ORDER[ss], 1, 0:wd], qk_rest[:, ORDER[ss], 0:wd],
                                                 ACT.Copy).then_inc(s_mid, 1)
                elif kind == "tr":
                    _, db, g = x
                    act.wait_ge(s_ms_ready[bank], n)
                    act.wait_ge(s_mrow[(g + 2) % G], b * MROW + (16 + MROW * (db + (1 if g >= 2 else 0))))
                    if TAIL:
                        nc.scalar.copy(max_rows_t[:, g % 2, :], m_[:, :].bitcast(BF16)[0:2, 512:640])
                    nc.scalar.copy(max_rows[:, g % 2, :], m_[:, :].bitcast(BF16)[0:2 * GH, 0:512]).then_inc(read, 1)
                elif kind == "s":
                    _, g, u = x
                    j, hs = score_units[u]
                    bank, n = scores.of(segment, b, x)
                    act.wait_ge(s_sc_ready[bank], n)
                    if (j, hs) == ("tail", 0):
                        nc.scalar.activation(probs_t[:, 0:512], sc[bank][:, :], ACT.Exp, scale=SCALE
                                             ).then_inc(s_exp[bank], 1)
                    elif j == "tail":
                        nc.scalar.activation(probs_t[0:32, 512:640], sc[bank][0:32, 0:P], ACT.Exp, scale=SCALE
                                             ).then_inc(s_exp[bank], 1)
                    else:
                        act.wait_ge(s_av_done, b * (G * KT) + (g * KT + j + 1))
                        w = width(j) * len(hs)
                        nc.scalar.activation(probs[:, u, 0:w], sc[bank][:, 0:w], ACT.Exp, scale=SCALE
                                             ).then_inc(s_exp[bank], 1)
                elif kind == "av" and x[2] == KT - 1:
                    g = x[1]
                    act.wait_ge(s_av_done, b * (G * KT) + ((g + 1) * KT + KT))
                    nc.scalar.copy(o_raw[:, g % 2, 0:S_IMG], ob[:, :]).then_inc(s_o_read, 1)
                elif kind == "ot":
                    g = x[1]
                    act.wait_ge(s_ms_ready[bank], n)
                    nc.scalar.copy(o_raw[:, g % 2, S_IMG:S], m_[:, 0:TAIL]).then_inc(read, 1)
                elif kind == "lg":
                    act.wait_ge(s_ms_ready[bank], n)
                    nc.scalar.activation(odds[:, 0:KT, :], m_[:, 0:E * KT].rearrange("p (t e) -> p t e", e=E),
                                         ACT.Exp, scale=-1.0)
                    nc.scalar.activation(odds[0:TAIL, KT, :], m_[0:TAIL, E * KT:E * VT], ACT.Exp, scale=-1.0
                                         ).then_inc(read, 1)
                elif kind in ("nx", "text"):
                    lo, hi = v_pairs[x[1]] if kind == "nx" else (0, 1)
                    act.wait_ge(s_ms_ready[bank], n)
                    if kind == "nx":
                        act.wait_ge(s_yn_out, (b - 1) * YN + YN)
                        if txt is not None:
                            act.wait_ge(s_txt_out, 16 * (1 + KC))
                    nc.scalar.copy(ynT[:, :, P * lo:P * hi].rearrange("p c (t q) -> p t c q", q=P),
                                   m_[:, 0:D * (hi - lo)].rearrange("p (t c q) -> p t c q", c=KC, q=P)
                                   ).then_inc(read, 1)
                elif kind == "ct":
                    lo, hi = v_pairs[x[1]]
                    act.wait_ge(s_ms_ready[bank], n)
                    w = P if hi <= KT else TAIL
                    nc.scalar.copy(oT[:, lo:hi, :, 0:w], m_[:, 0:D * (hi - lo)].rearrange(
                        "p (t c q) -> p t c q", c=KC, q=P)[:, :, :, 0:w]).then_inc(read, 1)

            run(act, handle)

        @block.gpsimd
        def _(pool):
            for q in (*s_exp, s_o_read, *s_ms_read, s_base):
                pool.sem_inc(q, 1)
            pool.sem_inc(s_mx_free, 2)
            if projected:
                for q in (s_high, s_rest, s_mid, s_low):
                    pool.sem_inc(q, 4)
                pool.sem_inc(s_xb, 16)
                for q in s_qk_stored:
                    pool.sem_inc(q, 32)
            pool.sem_inc(s_av_done, KT)
            for q in (*s_mrow, s_out):
                pool.sem_inc(q, 16)
            pool.sem_inc(s_yn_out, YN)
            pool.memset(k_stack[STACK:R], 1.0).then_inc(s_set, 1)
            pool.wait_ge(s_set, 1)
            pool.memset(v_ones[:], 1.0).then_inc(s_preset, 1)
            pool.memset(eps[:], LN_EPS).then_inc(s_set, 1)
            pool.memset(minus_half[:], -0.5).then_inc(s_set, 1)
            pool.wait_ge(s_const, CONSTS)
            pool.wait_ge(s_set, 3)

            def handle(segment, b, x):
                if x[0] in ("cp", "norm_text"):
                    lo, hi = v_pairs[x[1]] if x[0] == "cp" else (0, 1)
                    if x[0] == "cp":
                        pool.wait_ge(s_mv, (b - 1) * VT + (hi + YN0))
                    else:
                        pool.wait_ge(s_mv, 1)
                    nc.gpsimd.tensor_tensor(shifted[:, lo:hi], mean_var[:, lo:hi, 1], eps[:, 0:hi - lo], ALU.add
                                            ).then_inc(s_shift, 1)
                    if x[0] == "cp":
                        pool.wait_ge(s_shift, (b - 1) * NP_ + (x[1] + 1 + YN0))
                    else:
                        pool.wait_ge(s_shift, 1)
                    nc.gpsimd.tensor_tensor(rstd[:, lo:hi], shifted[:, lo:hi], minus_half[:, 0:hi - lo], ALU.pow
                                            ).then_inc(s_rstd, 1)
                elif x[0] == "qk":
                    step = x[1]
                    m = ORDER[step]
                    pool.wait_ge(s_high, b * 4 + (step + 5))
                    wd = projected_width(segment)
                    nc.gpsimd.tensor_tensor(qk_rest[:, m, 0:wd], qk_full[:, m, 0:wd], qk_part[:, m, 0, 0:wd],
                                            ALU.subtract).then_inc(s_rest, 1)
                    for ss in ((step - 1,) if step < 3 else (2, 3)):
                        if ss >= 0:
                            mm = ORDER[ss]
                            pool.wait_ge(s_mid, b * 4 + (ss + 5))
                            nc.gpsimd.tensor_tensor(qk_part[:, mm, 2, 0:wd], qk_rest[:, mm, 0:wd],
                                                    qk_part[:, mm, 1, 0:wd],
                                                    ALU.subtract).then_inc(s_low, 1)
                elif x[0] == "load_res":
                    pool.wait_ge(s_out, (b - 1) * (16 * NP_) + 16)
                    pool.wait_ge(s_res, b * 32)
                    nc.gpsimd.tensor_tensor(base[:, 0:KT, :], res[:, 0:KT, :],
                                            bo[:, None, :].to_broadcast([P, KT, D]), ALU.add)
                    nc.gpsimd.tensor_tensor(base[0:TAIL, KT, :], res[0:TAIL, KT, :], bo[0:TAIL, :],
                                            ALU.add).then_inc(s_base, 1)

            run(pool, handle)

        @block.vector
        def _(dve):
            nc.vector.memset(o_rows[:], 0.0).then_inc(s_preset, 1)
            if TAIL:
                nc.vector.memset(y_rows[:, KT, :], 0.0).then_inc(s_preset, 1)

            def statistics(lo, hi, before):
                for t in range(lo, hi):
                    nc.vector.bn_stats(stats[:, t, :], y_rows[:, t, :]).then_inc(s_stats, 1)
                dve.wait_ge(s_stats, before + (hi - lo))
                dve.sem_inc(s_dve, 1)
                for t in range(lo, hi):
                    nc.vector.bn_aggr(mean_var[:, t, :], stats[:, t, :]).then_inc(s_mv, 1)

            def normalize(lo, hi):
                for t in range(lo, hi):
                    nc.vector.tensor_scalar(yn[:, t, :], y_rows[:, t, :], mean_var[:, t, 0:1], rstd[:, t:t + 1],
                                            ALU.subtract, ALU.mult).then_inc(s_yn, 1)

            def handle(segment, b, x):
                kind = x[0]
                if kind in MISC_KINDS:
                    bank, n = misc.of(segment, b, x)
                    m_, read = ms[bank], s_ms_read[bank]
                if kind == "mx":
                    _, db, g, u = x
                    i, hs = max_units[u]
                    dve.wait_ge(s_mx_ready, b * (G * MU) + ((db * G + g) * MU + u + 1))
                    src = mx[(g * MU + u) % 2]
                    if i == "tail":
                        w = S_IMG if hs == 0 else TAIL
                        nc.vector.tensor_reduce(neg_max_t[:, g % 2, hs:hs + 1], src[:, 0:w], AX.X, ALU.max,
                                                negate=True).then_inc(s_mx_free, 1)
                    else:
                        w = P * (i + 1) if causal else S_IMG
                        nc.vector.tensor_reduce(
                            neg_max[:, g % 2, i, hs[0]:hs[0] + len(hs)],
                            src[:, 0:w * len(hs)].rearrange("p (h k) -> p h k", h=len(hs)), AX.X, ALU.max,
                            negate=True).then_inc(s_mx_free, 1)
                    if u == MU - 1:
                        dve.wait_ge(s_mx_free, b * (G * MU) + (2 + (db * G + g + 1) * MU))
                        nc.vector.tensor_copy(max_part[:, g % 2, :, 0, :], neg_max[:, g % 2]).then_inc(s_mhigh, 1)
                        k = 2 if TAIL else 1
                        if TAIL:
                            nc.vector.tensor_tensor(neg_max_t[:, g % 2, 2:3], neg_max_t[:, g % 2, 0:1],
                                                    neg_max_t[:, g % 2, 1:2], ALU.min).then_inc(s_negt, 1)
                            dve.wait_ge(s_negt, b * G + (db * G + g + 1))
                            nc.vector.tensor_copy(max_part_t[:, g % 2, 0:1], neg_max_t[:, g % 2, 2:3]
                                                  ).then_inc(s_mhigh, 1)
                        dve.wait_ge(s_mhigh, b * (G * k) + (db * G + g + 1) * k)
                        if TAIL:
                            nc.vector.tensor_tensor(max_part_t[:, g % 2, 1:2], neg_max_t[:, g % 2, 2:3],
                                                    max_part_t[:, g % 2, 0:1], ALU.subtract)
                        nc.vector.tensor_tensor(max_part[:, g % 2, :, 1, :], neg_max[:, g % 2],
                                                max_part[:, g % 2, :, 0, :], ALU.subtract).then_inc(s_mpart, 1)
                elif kind in ("on", "nt"):
                    _, db, g = x
                    k = 2 if TAIL else 1
                    count = (db * G + g) * k + (1 if kind == "on" else 2)
                    r, lo, hi = (slice(0, P), 0, KT) if kind == "on" else (slice(0, TAIL), KT, VT)
                    o = m_[r, 0:P * (hi - lo)].rearrange("p (t h d) -> p t h d", h=GH, d=32)
                    dve.wait_ge(s_ms_ready[bank], n)
                    nc.vector.reciprocal(o_inv[r, g, lo:hi, :], o[:, :, :, HD]).then_inc(s_inv, 1)
                    dve.wait_ge(s_inv, b * (G * k) + count)
                    nc.vector.tensor_tensor(
                        o_rows[r, lo:hi, 64 * g:64 * g + 64].rearrange("p t (h d) -> p t h d", h=GH), o[:, :, :, 0:HD],
                        o_inv[r, g, lo:hi, :, None].to_broadcast([r.stop, hi - lo, GH, HD]), ALU.mult).then_inc(read, 1)
                elif kind == "v":
                    lo, hi = v_pairs[x[1]]
                    if segment == "first" and lo == 0:
                        dve.wait_ge(s_const, CONSTS)
                        dve.wait_ge(s_preset, PRESETS)
                    dve.wait_ge(s_ms_ready[bank], n)
                    for t in range(lo, hi):
                        w = P if t < KT else TAIL
                        o = D * (t - lo)
                        i = nc.vector.tensor_tensor(
                            v_ones[0:w, t, :, :, 0:HD],
                            m_[0:w, o:o + D].rearrange("p (g h d) -> p g h d", g=G, h=GH),
                            bv[0:w, :].rearrange("p (g h d) -> p g h d", g=G, h=GH), ALU.add)
                    i.then_inc(read, 1)
                elif kind == "cp":
                    lo, hi = v_pairs[x[1]]
                    dve.wait_ge(s_ms_ready[bank], n)
                    if lo == 0:
                        dve.wait_ge(s_out, (b - 1) * (16 * NP_) + 16)
                        if residual is not None:
                            dve.wait_ge(s_base, b + 1)
                    for t in range(lo, hi):
                        w = P if t < KT else TAIL
                        o = D * (t - lo)
                        i = nc.vector.tensor_tensor(y_rows[0:w, t, :], m_[0:w, o:o + D],
                                                    bo[0:w, :] if residual is None else base[0:w, t, :], ALU.add)
                    i.then_inc(read, 1)
                    dve.wait_ge(read, n + 1)
                    statistics(lo, hi, (b - 1) * VT + (lo + YN0))
                elif kind == "norm_text":
                    dve.wait_ge(s_txt, 16)
                    statistics(0, 1, 0)
                    dve.wait_ge(s_rstd, 1)
                    normalize(0, 1)
                elif kind == "nm":
                    lo, hi = v_pairs[x[1]]
                    dve.wait_ge(s_rstd, (b - 1) * NP_ + (x[1] + 1 + YN0))
                    if lo == 0:
                        dve.wait_ge(s_yn_out, (b - 1) * YN + YN)
                    normalize(lo, hi)

            run(dve, handle)


def attention_inputs(w_cols, b_cols, w_rows, b_out):
    import numpy as np
    w = w_cols.reshape(D, HEADS, 3, HD)
    b = b_cols.reshape(HEADS, 3, HD)
    wqk = w[:, :, 0:2].reshape(D, GROUPS, GH, 2, HD).transpose(0, 3, 1, 4, 2)
    bqk = b[:, 0:2].reshape(GROUPS, GH, 2, HD).transpose(2, 0, 3, 1)
    out = {"wqk": wqk.reshape(KC, P, 2 * D).transpose(1, 0, 2),
           "bqk": bqk.reshape(4, P).T,
           "wv": w[:, :, 2].reshape(KC, P, D).transpose(1, 0, 2),
           "bv": np.broadcast_to(b[:, 2].reshape(1, D), (P, D))}
    out["wo"] = w_rows.reshape(KC, P, D).transpose(1, 0, 2)
    out["bo"] = np.broadcast_to(b_out.reshape(1, D), (P, D))
    return out


def constants():
    import numpy as np
    f, bf = np.float32, mybir.dt.np(BF16)
    i = np.arange(P)
    c = {"ident_f": np.eye(P, dtype=f), "ident_bf": np.eye(P, dtype=f).astype(bf)}
    later = np.where(i[None, :] > i[:, None], f(-1e30), f(0))
    c["mask_q"] = later.astype(bf)
    c["mask_k"] = later.T.astype(bf)
    qt = np.zeros((P, S_TXT), f)
    qt[0:S_TXT] = later[0:S_TXT, 0:S_TXT]
    c["mask_qt"] = qt.astype(bf)
    return c


def experts_layer(nc, h_dram, xnT_dram, xn_dram, odds_dram, slots_dram, w, out):
    ctx = ExitStack()
    with ctx:
        def sb(name, shape, dt, where=ctx):
            return where.enter_context(nc.sbuf_tensor(f"e_{name}", shape, dt))

        def sem(name):
            return ctx.enter_context(nc.semaphore(f"e_{name}"))

        idf = sb("ident", [P, P], F32)
        step_rows = sb("step_rows", [P, E + 1, 2, CT], F32)
        xT = sb("xT", [P, KC, T_ALL], F32)
        s_gu = sb("s_gu", [P, KC, 2 * SHARED], F32)
        s_down = sb("s_down", [P, SHARED // P, D], F32)
        FIRST = NT - LATER

        with ExitStack() as early:
            def se(name, shape, dt):
                return sb(name, shape, dt, early)

            h = se("h", [P, NT, D], F32)
            bias = se("bias", [P, E], F32)
            before = se("before", [P, P], BF16)
            ones = se("ones", [P, P], BF16)
            iota_bf = se("iota_bf", [P, 32], BF16)
            token = se("token", [P, 1], F32)
            spare = se("spare", [P, E * CT], F32)
            scores = se("scores", [P, NT, E], F32)
            ranked = se("ranked", [P, NT, E], F32)
            top = se("top", [P, NT, TOPK], F32)
            struck = se("struck", [P, NT, E], F32)
            chosen_bf = se("chosen_bf", [P, NT, E], BF16)
            left = se("left", [P, NT, E], F32)
            pos_i = se("pos_i", [P, NT, E], I32)
            total = se("total", [P, NT], F32)
            gain = se("gain", [P, NT, E], F32)
            hi_i = se("hi_i", [P, NT, E], I32)
            lo_i = se("lo_i", [P, NT, E], I32)
            hi = se("hi", [P, NT, E], BF16)
            lo = se("lo", [P, NT, E], BF16)
            one_hi = se("one_hi", [P, NT, E, 32], BF16)
            lo_token = se("lo_token", [P, NT, E, 2, 16], BF16)
            parts = se("parts", [P, 8, 4, 2, 16], F32)
            table = se("table", [P, 8, 16], F32)
            rows = se("rows", [P, P], F32)
            s_silu = se("s_silu", [P, 2, 512], F32)
            s_up = se("s_up", [P, 2, 512], F32)
            s_rows = se("s_rows", [P, 2, D], F32)
            s_h = se("s_h", [P, 2, SHARED // P, 512], F32)
            bank = [early.enter_context(nc.psum_tensor(f"e_t{i}", [P, 512], F32)) for i in range(4)]
            yb = [early.enter_context(nc.psum_tensor(f"e_y{i}", [P, 512], F32)) for i in range(2)]
            pr = early.enter_context(nc.psum_tensor("e_pr", [P, 512], F32))
            pt = early.enter_context(nc.psum_tensor("e_pt", [P, 512], F32))
            (s_in, s_x, s_xn_out, s_const, s_shared, s_down_in, s_odds, s_v, s_chosen, s_pos, s_onehot, s_table, s_table_read, s_rows_out, s_rows_in,
             s_rows_turned, s_tab, s_gain, s_sgu, s_silu_done, s_hid, s_y, s_y_read, s_added, s_past, s_out, s_zero) = [
                sem(n) for n in (
                    "h_loaded", "xT_loaded", "gains_stored", "router_constants", "shared_weights", "shared_down_loaded", "odds_loaded",
                    "vector_steps", "chosen_ready", "pos_ready", "onehot_ready", "table_ready", "table_read", "table_stored", "table_loaded",
                    "table_turned", "table_rows_ready", "gains_ready", "shared_gate_up", "shared_silu",
                    "shared_hidden", "shared_y", "shared_y_read", "shared_y_added", "rows_past_tokens_stored", "rows_stored", "step_rows_zeroed")]
            block = early.enter_context(nc.Block())
            F = SHARED // P
            chunks = [(512 * c, min(512, FIRST * P - 512 * c)) for c in range(-(-FIRST * P // 512))]
            chunk_of = [range(lo // P, (lo + wd) // P) for lo, wd in chunks]

            @block.sync
            def _(sp):
                sp.dma_start(scores[:], odds_dram.rearrange("(n p) e -> p n e", p=P)).then_inc(s_odds, 16)
                sp.dma_start(bias[:], w["e_bias"]).then_inc(s_odds, 16)
                features = xnT_dram.rearrange("(c p) t -> p c t", p=P)
                sp.dma_start(s_gu[:], w["s_gu"]).then_inc(s_shared, 16)
                sp.dma_start(xT[:, :, 0:FIRST * P], features[:, :, 0:FIRST * P]).then_inc(s_x, 16)
                for dst, src in ((idf, w["ident_f"]), (before, w["before"]), (ones, w["ones_bf"]),
                                 (iota_bf, w["iota_bf"]), (token, w["token"]), (spare, w["spare"])):
                    sp.dma_start(dst[:], src).then_inc(s_const, 16)
                sp.dma_start(xT[:, :, FIRST * P:], features[:, :, FIRST * P:]).then_inc(s_x, 16)
                sp.dma_start(s_down[:], w["s_down"]).then_inc(s_down_in, 16)
                rows_of = h_dram.rearrange("(n p) d -> p n d", p=P)
                sp.dma_start(h[:], rows_of).then_inc(s_in, 16)
                sp.wait_ge(s_in, 16)
                sp.dma_start(out[T_ALL:T_ALL + CAP, :].rearrange("(n p) d -> p n d", p=P), h[:, 0:CT]
                             ).then_inc(s_past, 16)
                by_row = xn_dram.rearrange("(n p) d -> p n d", p=P)
                sp.wait_ge(s_gain, 1)
                sp.dma_start(by_row[:, :, D:D + E], gain[:]).then_inc(s_xn_out, 16)
                out_rows = out[0:T_ALL, :].rearrange("(n p) d -> p n d", p=P)
                sp.dma_start(out_rows[:, FIRST:NT], h[:, FIRST:NT]).then_inc(s_out, 16)
                for c in range(len(chunks)):
                    sp.wait_ge(s_added, 2 + chunk_of[c].stop)
                    sp.dma_start(out_rows[:, chunk_of[c].start:chunk_of[c].stop],
                                 h[:, chunk_of[c].start:chunk_of[c].stop]).then_inc(s_out, 16)
                sp.wait_ge(s_tab, 4)
                sp.dma_start(slots_dram.rearrange("(g p l) -> p g l", p=P, l=16), table[:]).then_inc(s_rows_out, 16)
                sp.wait_ge(s_rows_out, 16)
                sp.dma_start(rows[:], slots_dram.rearrange("(r s) -> r s", s=P)).then_inc(s_rows_in, 16)
                sp.wait_ge(s_xn_out, 16)
                sp.wait_ge(s_x, 32)
                sp.wait_ge(s_out, 16 * (1 + len(chunks)))

            @block.gpsimd
            def _(pool):
                pool.sem_inc(s_hid, 2)
                pool.sem_inc(s_y_read, 2)
                pool.sem_inc(s_added, 2)
                pool.wait_ge(s_past, 16)
                def hidden(c):
                    wd = chunks[c][1]
                    for f in range(F):
                        n = F * c + f
                        if f == 1 and c > 0:
                            add(c - 1)
                        pool.wait_ge(s_silu_done, n + 1)
                        nc.gpsimd.tensor_tensor(s_h[:, c % 2, f, 0:wd], s_silu[:, n % 2, 0:wd],
                                                s_up[:, n % 2, 0:wd], ALU.mult).then_inc(s_hid, 1)

                def add(c):
                    for t in chunk_of[c]:
                        pool.wait_ge(s_y_read, t + 3)
                        nc.gpsimd.tensor_tensor(h[:, t, :], h[:, t, :], s_rows[:, t % 2], ALU.add
                                                ).then_inc(s_added, 1)

                for c in range(len(chunks)):
                    hidden(c)
                add(len(chunks) - 1)

            @block.scalar
            def _(act):
                def silu(c):
                    wd = chunks[c][1]
                    for f in range(F):
                        n = F * c + f
                        act.wait_ge(s_sgu, n + 1)
                        act.wait_ge(s_hid, n + 1)
                        nc.scalar.activation(s_silu[:, n % 2, 0:wd], bank[2 * (n % 2)][:, 0:wd], ACT.Silu)
                        nc.scalar.copy(s_up[:, n % 2, 0:wd], bank[2 * (n % 2) + 1][:, 0:wd]).then_inc(s_silu_done, 1)
                        if f == 0 and c > 0:
                            results(c - 1)

                def results(c):
                    for t in chunk_of[c]:
                        act.wait_ge(s_y, t + 1)
                        act.wait_ge(s_added, t + 1)
                        nc.scalar.copy(s_rows[:, t % 2], yb[t % 2][:, 0:D]).then_inc(s_y_read, 1)

                for c in range(len(chunks)):
                    silu(c)
                results(len(chunks) - 1)
            @block.tensor
            def _(pe):
                def gate_up(c):
                    at, wd = chunks[c]
                    for f in range(F):
                        n = F * c + f
                        pe.wait_ge(s_hid, n + 1)
                        for half in range(2):
                            for ch in range(KC):
                                mm = pe.matmul(bank[2 * (n % 2) + half][:, 0:wd],
                                               s_gu[:, ch, SHARED * half + P * f:SHARED * half + P * f + P],
                                               xT[:, ch, at:at + wd], start=(ch == 0), stop=(ch == KC - 1))
                        mm.then_inc(s_sgu, 1)
                        if f == 0 and c > 0:
                            down(c - 1)

                def down(c):
                    if c == 0:
                        pe.wait_ge(s_down_in, 16)
                    pe.wait_ge(s_hid, F * (c + 1) + 2)
                    for t in chunk_of[c]:
                        pe.wait_ge(s_y_read, t + 1)
                        o = P * t - chunks[c][0]
                        for f in range(F):
                            mm = pe.matmul(yb[t % 2][:, 0:D], s_h[:, c % 2, f, o:o + P], s_down[:, f, :],
                                           start=(f == 0), stop=(f == F - 1))
                        mm.then_inc(s_y, 1)

                pe.wait_ge(s_chosen, 1)
                pe.wait_ge(s_const, 16 * 6)
                pe.matmul(pt[:, 0:E], before[:, :], chosen_bf[:, 0, :], start=True, stop=True)
                pe.matmul(pr[:, :], before[:, :], chosen_bf[:, 1:NT, :].rearrange("p t e -> p (t e)"), start=True,
                          stop=False)
                for t in reversed(range(NT - 1)):
                    mm = pe.matmul(pr[:, E * t:].rearrange("p (t e) -> p t e", e=E), ones[:, :],
                                   chosen_bf[:, t, None, :].to_broadcast([P, NT - 1 - t, E]), start=False,
                                   stop=(t == 0), skip_group_check=(t > 0))
                mm.then_inc(s_pos, 1)
                pe.wait_ge(s_shared, 16)
                pe.wait_ge(s_x, 32)
                for c in range(len(chunks)):
                    gate_up(c)
                down(len(chunks) - 1)
                for part in range(2):
                    pe.wait_ge(s_onehot, part + 1)
                    if part == 1:
                        pe.wait_ge(s_table_read, 1)
                    for g in range(4 * part, 4 * part + 4):
                        for t in range(NT):
                            mm = pe.matmul(pt[:, P * (g % 4):P * (g % 4) + P],
                                           one_hi[:, t, 4 * g:4 * g + 4, :].rearrange("p e a -> p (e a)"),
                                           lo_token[:, t, 4 * g:4 * g + 4, :, :].rearrange("p e k b -> p (e k b)"),
                                           start=(t == 0), stop=(t == NT - 1))
                    mm.then_inc(s_table, 1)
                pe.wait_ge(s_rows_in, 16)
                pe.transpose(bank[0][:, 0:P], rows[:, :], idf[:, :]).then_inc(s_rows_turned, 1)

            @block.vector
            def _(dve):
                nc.vector.memset(step_rows[:], 0.0).then_inc(s_zero, 1)
                steps = [0]

                def then(i):
                    steps[0] += 1
                    i.then_inc(s_v, 1)
                    dve.wait_ge(s_v, steps[0])

                v = nc.vector
                dve.wait_ge(s_odds, 32)
                then(v.tensor_scalar(scores[:], scores[:], 1.0, None, ALU.add))
                then(v.reciprocal(scores[:], scores[:]))
                then(v.tensor_tensor(ranked[:], scores[:], bias[:, None, :].to_broadcast([P, NT, E]), ALU.add))
                for t in range(NT):
                    i = v.max(top[:, t, :], ranked[:, t, :])
                then(i)
                for t in range(NT):
                    i = v.match_replace(struck[:, t, :], top[:, t, :], ranked[:, t, :], -3e38)
                then(i)
                v.tensor_tensor(chosen_bf[:], struck[:], ranked[:], ALU.not_equal).then_inc(s_chosen, 1)
                then(v.tensor_tensor(left[:], struck[:], ranked[:], ALU.is_equal))
                dve.wait_ge(s_chosen, 1)
                then(v.tensor_tensor(gain[:], scores[:], chosen_bf[:], ALU.mult))
                then(v.tensor_reduce(total[:], gain[:], AX.X, ALU.add))
                then(v.tensor_scalar(total[:], total[:], 1e-20, None, ALU.add))
                then(v.reciprocal(total[:], total[:]))
                then(v.tensor_scalar(total[:], total[:], ROUTE_SCALE, None, ALU.mult))
                v.tensor_tensor(gain[:], gain[:], total[:, :, None].to_broadcast([P, NT, E]), ALU.mult
                                ).then_inc(s_gain, 1)
                dve.wait_ge(s_const, 16 * 6)
                dve.wait_ge(s_pos, 1)
                v.scalar_tensor_tensor(pos_i[:, 0, :], left[:, 0, :], 4096.0, pt[:, 0:E], ALU.mult, ALU.add)
                then(v.scalar_tensor_tensor(pos_i[:, 1:NT, :], left[:, 1:NT, :], 4096.0,
                                            pr[:, :].rearrange("p (t e) -> p t e", e=E), ALU.mult, ALU.add))
                v.tensor_scalar(lo_i[:], pos_i[:], 15, None, ALU.bitwise_and)
                then(v.tensor_scalar(hi_i[:], pos_i[:], 4, None, ALU.logical_shift_right))
                v.tensor_copy(hi[:], hi_i[:])
                then(v.tensor_copy(lo[:], lo_i[:]))
                then(v.tensor_tensor(lo_token[:, :, :, 0, :], lo[:, :, :, None].to_broadcast([P, NT, E, 16]),
                                     iota_bf[:, None, None, 0:16].to_broadcast([P, NT, E, 16]), ALU.is_equal))
                for t in range(NT):
                    i = v.tensor_scalar(lo_token[:, t, :, 1, :], lo_token[:, t, :, 0, :], float(t), None, ALU.mult)
                then(i)
                v.tensor_scalar(lo_token[:, :, :, 0, :], lo_token[:, :, :, 0, :], token[:, 0:1], None, ALU.mult)
                for part in range(2):
                    es = slice(E // 2 * part, E // 2 * part + E // 2)
                    v.tensor_tensor(one_hi[:, :, es], hi[:, :, es, None].to_broadcast([P, NT, E // 2, 32]),
                                    iota_bf[:, None, None, :].to_broadcast([P, NT, E // 2, 32]), ALU.is_equal
                                    ).then_inc(s_onehot, 1)
                for part in range(2):
                    dve.wait_ge(s_table, part + 1)
                    then(v.tensor_copy(parts[:, 4 * part:4 * part + 4],
                                       pt[:, :].rearrange("p (g e k b) -> p g e k b", g=4, e=4, k=2)))
                    dve.sem_inc(s_table_read, 1)
                for e in range(4):
                    r = slice(32 * e, 32 * e + 32)
                    v.scalar_tensor_tensor(table[r], parts[r, :, e, 1, :], float(P), parts[r, :, e, 0, :], ALU.mult,
                                           ALU.add).then_inc(s_tab, 1)
                dve.wait_ge(s_rows_turned, 1)
                dve.wait_ge(s_zero, 1)
                of_slot = bank[0][:, 0:P]
                by_expert = of_slot.rearrange("p (n c) -> p n c", c=CT)
                then(v.tensor_scalar(step_rows[:, 0:E - 2, 0, :], by_expert[:, 2:E, :], -1.0, 0.0, ALU.add, ALU.max))
                v.tensor_scalar(step_rows[:, E - 2:E, 0, :], by_expert[:, 0:2, :], -1.0, 0.0, ALU.add, ALU.max)
                then(v.scalar_tensor_tensor(spare[:], of_slot, 0.0, spare[:], ALU.is_equal, ALU.mult))
                then(v.tensor_tensor(spare[:], spare[:], of_slot, ALU.add))
                then(v.tensor_scalar(step_rows[:, 1:E + 1, 1, :], spare[:, :].rearrange("p (n c) -> p n c", c=CT),
                                     -1.0, None, ALU.add))

        ROW = D + E
        gate_up = sb("gate_up", [P, 2, KC, 2 * INTER], F32)
        down = sb("down", [P, 2, D], F32)
        now = sb("now", [P, 2, 2, CT], U32)
        xg = sb("xg", [P, 2, CT, ROW], F32)
        gains = sb("gains", [P, 2, CT], F32)
        xgT = sb("xgT", [P, 2, KC, CAP], F32)
        g_lim = sb("g_lim", [P, 2, CAP], F32)
        u_lim = sb("u_lim", [P, 2, CAP], F32)
        silu = sb("silu", [P, 2, CAP], F32)
        hid = sb("hid", [P, 2, CAP], F32)
        y = sb("y", [P, 2, CT, D], F32)
        s_silu = sb("s_silu2", [P, 512], F32)
        s_h = sb("s_h2", [P, SHARED], F32)
        s_rows = sb("s_rows2", [P, D], F32)
        tp = ctx.enter_context(nc.psum_tensor("e_tp", [P, KC, 512], F32))
        gu = [ctx.enter_context(nc.psum_tensor(f"e_gu{i}", [P, 2, 512], F32)) for i in range(2)]
        yp = ctx.enter_context(nc.psum_tensor("e_yp", [P, 2, 512], F32))
        q_w = [sem(f"gate_up{k}_loaded") for k in range(2)]
        q_wd = [sem(f"down{k}_loaded") for k in range(2)]
        q_g = [sem(f"rows{k}_gathered") for k in range(2)]
        q_sc = sem("results_added")
        (q_sgu, q_ssilu, q_shid, q_sy, q_srows, q_sadd) = [
            sem(n) for n in ("later_shared_gate_up", "later_shared_silu", "later_shared_hidden", "later_shared_y",
                             "later_shared_rows", "later_shared_added")]
        (q_now, q_pool, q_turned, q_xT, q_gain, q_gu, q_gl, q_ul, q_silu, q_hid, q_y, q_yr) = [
            sem(n) for n in ("step_rows_ready", "pool_waited", "rows_turned", "xT_taken",
                             "gains_taken", "gate_up_ready",
                             "gate_limited", "up_limited", "silu_ready", "hidden_ready", "y_ready", "y_weighed")]
        block = ctx.enter_context(nc.Block())
        HALF = E // 2


        @block.sync
        def _(sp):
            def load_gate_up(n, k):
                sp.dma_start(gate_up[:, k], w["gate_up"][bass.ds(n, 1)].rearrange("e p c o -> p (e c) o")
                             ).then_inc(q_w[k], 16)

            def load_down(n, k):
                sp.dma_start(down[:, k], w["down"][bass.ds(n, 1)].rearrange("e p o -> p (e o)")
                             ).then_inc(q_wd[k], 16)

            for k in range(2):
                load_gate_up(k, k)
                load_down(k, k)
            sp.wait_ge(q_gu, 2)
            load_gate_up(2, 0)
            with sp.Fori(0, HALF - 2) as i:
                sp.wait_ge(q_gu, 4 * i + 4)
                load_gate_up(2 * i + 3, 1)
                sp.wait_ge(q_y, 2 * i + 1)
                load_down(2 * i + 2, 0)
                sp.wait_ge(q_gu, 4 * i + 6)
                load_gate_up(2 * i + 4, 0)
                sp.wait_ge(q_y, 2 * i + 2)
                load_down(2 * i + 3, 1)
            sp.wait_ge(q_gu, 2 * (E - 2))
            load_gate_up(E - 1, 1)
            sp.wait_ge(q_y, E - 3)
            load_down(E - 2, 0)
            sp.wait_ge(q_y, E - 2)
            load_down(E - 1, 1)

        @block.gpsimd
        def _(pool):
            pool.sem_inc(q_xT, 1)
            pool.sem_inc(q_ul, 2)
            pool.sem_inc(q_yr, 1)
            pool.sem_inc(q_srows, 1)

            def gather(k, cs=range(CT)):
                for c in cs:
                    pool.indirect_dma_start(xg[:, k, c, :], None, xn_dram,
                                            bass.IndirectOffsetOnAxis(now[:, k, 0, c:c + 1], 0)
                                            ).then_inc(q_g[k], 16)

            def add(k):
                for c in range(CT):
                    pool.indirect_dma_start(out, bass.IndirectOffsetOnAxis(now[:, k, 1, c:c + 1], 0),
                                            y[:, 1 - k, c, :], None, compute_op=ALU.add).then_inc(q_sc, 16)

            def ready():
                pool.sem_inc(q_pool, 1)

            for k in range(2):
                pool.wait_ge(q_now, k + 1)
                gather(k)

            def add_shared(i):
                pool.wait_ge(q_sc, (16 * CT) * (2 * i + 2))
                pool.wait_ge(q_srows, i + 2)
                ready()
                pool.dma_start(out[bass.ds(i * P + FIRST * P, P), :], s_rows[:, :], accum_op=ALU.add
                               ).then_inc(q_sadd, 16)

            def step(i, k, rows=True, results=True, first=False, shared=False):
                n = 2 * i + k
                pool.wait_ge(q_now, n + 3)
                if rows:
                    pool.wait_ge(q_gain, n + 1)
                    pool.wait_ge(q_turned, n + 1)
                    ready()
                    if shared:
                        gather(k, range(CT // 2))
                        add_shared(i - 1)
                        gather(k, range(CT // 2, CT))
                        pool.wait_ge(q_sadd, 16 * i)
                    else:
                        gather(k)
                if results:
                    pool.wait_ge(q_yr, n + 1)
                    if not first:
                        pool.wait_ge(q_sc, (16 * CT) * n - 16 * CT)
                    ready()
                    add(k)

            step(0, 0, results=False)
            step(0, 1, first=True)
            with pool.Fori(1, LATER + 1) as i:
                for k in range(2):
                    step(i, k, shared=(k == 1))
            with pool.Fori(LATER + 1, HALF - 1) as i:
                for k in range(2):
                    step(i, k)
            for k in range(2):
                step(HALF - 1, k, rows=False)
            step(HALF, 0, rows=False)
            pool.wait_ge(q_sc, 16 * CT * E)

        @block.tensor
        def _(pe):
            def turn(n, i, k):
                pe.wait_ge(q_g[k], 16 * CT * (i + 1))
                pe.wait_ge(q_xT, 2 * n + 1)
                for ch in range(KC):
                    for c in range(CT):
                        mm = pe.transpose(tp[:, ch, P * c:P * c + P], xg[:, k, c, P * ch:P * ch + P], idf[:, :])
                mm.then_inc(q_turned, 1)

            def compute(n, i, k):
                pe.wait_ge(q_w[k], 16 * (i + 1))
                pe.wait_ge(q_xT, 2 * n + 3)
                pe.wait_ge(q_ul, n + 1)
                for half in range(2):
                    for ch in range(KC):
                        mm = pe.matmul(gu[k][:, half, :], gate_up[:, k, ch, INTER * half:INTER * half + INTER],
                                       xgT[:, k, ch, :], start=(ch == 0), stop=(ch == KC - 1))
                    mm.then_inc(q_gu, 1)

            def finish(n, i, k):
                pe.wait_ge(q_wd[k], 16 * (i + 1))
                pe.wait_ge(q_hid, n + 1)
                pe.wait_ge(q_yr, n + 1)
                for c in range(CT):
                    mm = pe.matmul(yp[:, c // 2, D * (c % 2):D * (c % 2) + D], hid[:, k, P * c:P * c + P], down[:, k, :],
                                   start=True, stop=True)
                mm.then_inc(q_y, 1)

            turn(0, 0, 0)
            compute(0, 0, 0)
            turn(1, 0, 1)

            def shared_gate_up(i):
                pe.wait_ge(q_ul, 2 * i + 4)
                for half in range(2):
                    for f in range(SHARED // P):
                        for ch in range(KC):
                            mm = pe.matmul(gu[1][:, half, P * f:P * f + P],
                                           s_gu[:, ch, SHARED * half + P * f:SHARED * half + P * f + P],
                                           xT[:, ch, bass.ds(i * P + FIRST * P, P)], start=(ch == 0),
                                           stop=(ch == KC - 1))
                mm.then_inc(q_sgu, 1)

            def shared_down(i):
                pe.wait_ge(q_xT, 4 * i + 9)
                pe.wait_ge(q_shid, i + 1)
                for f in range(SHARED // P):
                    mm = pe.matmul(tp[:, 0, 0:D], s_h[:, P * f:P * f + P], s_down[:, f, :], start=(f == 0),
                                   stop=(f == SHARED // P - 1))
                mm.then_inc(q_sy, 1)

            def two_steps(i, shared):
                n = 2 * i
                compute(n + 1, i, 1)
                if shared:
                    pe.wait_ge(q_srows, i + 1)
                turn(n + 2, i + 1, 0)
                finish(n, i, 0)
                compute(n + 2, i + 1, 0)
                if shared:
                    shared_gate_up(i)
                turn(n + 3, i + 1, 1)
                finish(n + 1, i, 1)
                if shared:
                    shared_down(i)

            with pe.Fori(0, LATER) as i:
                two_steps(i, True)
            pe.wait_ge(q_srows, LATER + 1)
            with pe.Fori(LATER, HALF - 1) as i:
                two_steps(i, False)
            compute(E - 1, HALF - 1, 1)
            finish(E - 2, HALF - 1, 0)
            finish(E - 1, HALF - 1, 1)

        @block.scalar
        def _(act):
            def take(n, k):
                act.wait_ge(q_turned, n + 1)
                for ch in range(KC):
                    nc.scalar.copy(xgT[:, k, ch, :], tp[:, ch, :]).then_inc(q_xT, 1)

            def gate(n, k):
                act.wait_ge(q_gl, n + 1)
                nc.scalar.activation(silu[:, k, :], g_lim[:, k, :], ACT.Silu).then_inc(q_silu, 1)

            def result(n, k, first=False):
                act.wait_ge(q_y, n + 1)
                act.wait_ge(q_gain, n + 1)
                if not first:
                    act.wait_ge(q_sc, (16 * CT) * n - 16 * CT)
                for c in range(CT):
                    a = nc.scalar.activation(y[:, k, c, :], yp[:, c // 2, D * (c % 2):D * (c % 2) + D], ACT.Copy,
                                             scale=gains[:, k, c:c + 1])
                a.then_inc(q_yr, 1)

            take(0, 0)
            gate(0, 0)
            take(1, 1)

            def two_steps(i, shared, first=False):
                for k in range(2):
                    n = 2 * i + k
                    gate(n + 1, 1 - k)
                    if shared and k == 1:
                        act.wait_ge(q_sgu, i + 1)
                        nc.scalar.activation(s_silu[:, :], gu[1][:, 0, :], ACT.Silu).then_inc(q_ssilu, 1)
                    take(n + 2, k)
                    result(n, k, first)

            two_steps(0, True, first=True)
            with act.Fori(1, LATER) as i:
                two_steps(i, True)
            with act.Fori(LATER, HALF - 1) as i:
                two_steps(i, False)
            gate(E - 1, 1)
            result(E - 2, 0)
            result(E - 1, 1)

        @block.vector
        def _(dve):
            v = nc.vector

            def stage(m, k, added=True):
                if added:
                    dve.wait_ge(q_sc, (16 * CT) * m - 2 * (16 * CT))
                v.tensor_scalar(now[:, k], step_rows[:, bass.ds(m, 1)].rearrange("p m a c -> p (m a) c"), 1.0, None,
                                ALU.mult).then_inc(q_now, 1)

            def take_gains(n, i, k):
                dve.wait_ge(q_g[k], 16 * CT * (i + 1))
                dve.wait_ge(q_yr, n)
                v.tensor_scalar(gains[:, k, :], xg[:, k, :, bass.ds(n + D, 1)].rearrange("p c g -> p (c g)"), 1.0,
                                None, ALU.mult).then_inc(q_gain, 1)

            def limit(n, k):
                dve.wait_ge(q_gu, 2 * n + 1)
                v.tensor_scalar(g_lim[:, k, :], gu[k][:, 0, :], LIMIT, None, ALU.min).then_inc(q_gl, 1)
                dve.wait_ge(q_gu, 2 * n + 2)
                v.tensor_scalar(u_lim[:, k, :], gu[k][:, 1, :], LIMIT, -LIMIT, ALU.min, ALU.max).then_inc(q_ul, 1)

            def hidden(n, k):
                dve.wait_ge(q_ul, n + 3)
                dve.wait_ge(q_silu, n + 1)
                v.tensor_tensor(hid[:, k, :], silu[:, k, :], u_lim[:, k, :], ALU.mult).then_inc(q_hid, 1)

            for k in range(2):
                v.tensor_scalar(now[:, k, 0, :], step_rows[:, E - 2 + k, 0, :], 1.0, None, ALU.mult
                                ).then_inc(q_now, 1)
            for k in range(2):
                dve.wait_ge(q_g[k], 16 * CT)
                v.tensor_scalar(gains[:, k, :], xg[:, k, :, D + k], 1.0, None, ALU.mult).then_inc(q_gain, 1)
                if k == 0:
                    stage(0, 0, added=False)
            limit(0, 0)
            hidden(0, 0)

            def two_steps(i, shared, first=False):
                for k in range(2):
                    n = 2 * i + k
                    limit(n + 1, 1 - k)
                    stage(n + 1, 1 - k, added=not first)
                    hidden(n + 1, 1 - k)
                    if shared and k == 1:
                        dve.wait_ge(q_ssilu, i + 1)
                        v.tensor_tensor(s_h[:, :], s_silu[:, :], gu[1][:, 1, :], ALU.mult).then_inc(q_shid, 1)
                    take_gains(n + 2, i + 1, k)
                if shared:
                    dve.wait_ge(q_sy, i + 1)
                    if not first:
                        dve.wait_ge(q_sadd, 16 * i)
                    v.tensor_scalar(s_rows[:, :], tp[:, 0, 0:D], 1.0, None, ALU.mult).then_inc(q_srows, 1)

            two_steps(0, True, first=True)
            with dve.Fori(1, LATER) as i:
                two_steps(i, True)
            with dve.Fori(LATER, HALF - 1) as i:
                two_steps(i, False)
            limit(E - 1, 1)
            stage(E - 1, 1)
            hidden(E - 1, 1)
            stage(E, 0)


def expert_inputs(router_weight, e_bias, gate_up, down, shared_gate, shared_up, shared_down):
    import numpy as np
    return {
        "router": router_weight.T.reshape(KC, P, E).transpose(1, 0, 2),
        "e_bias": np.broadcast_to(e_bias.reshape(1, E), (P, E)),
        "gate_up": gate_up.transpose(0, 2, 1).reshape(E, KC, P, 2 * INTER).transpose(0, 2, 1, 3),
        "down": down.transpose(0, 2, 1),
        "s_gu": np.concatenate([shared_gate, shared_up], 0).T.reshape(KC, P, 2 * SHARED).transpose(1, 0, 2),
        "s_down": shared_down.T.reshape(SHARED // P, P, D).transpose(1, 0, 2),
    }


def routing_constants():
    import numpy as np
    f, bf = np.float32, mybir.dt.np(BF16)
    i = np.arange(P)
    return {
        "before": (i[:, None] < i[None, :]).astype(bf),
        "ones_bf": np.ones((P, P), bf),
        "iota_bf": np.broadcast_to(np.arange(32, dtype=f).astype(bf), (P, 32)),
        "token": (i + 1).astype(f).reshape(P, 1),
        "spare": np.broadcast_to(T_ALL + 1 + P * np.arange(CT)[None, None, :] + i[:, None, None],
                                 (P, E, CT)).reshape(P, E * CT).astype(f),
    }


ATTENTION = ("wqk", "bqk", "wv", "bv", "wo", "bo")


def early_fusion(nc, a, out):
    def scratch(name, shape, dt):
        return nc.dram_tensor(name, shape, dt, kind="Internal").ap()

    h1 = scratch("h1", [T_ALL, D], F32)
    h2 = scratch("h2", [T_ALL, D], F32)
    xn1T = scratch("xn1T", [D, T_ALL], F32)
    xn2T = scratch("xn2T", [D, T_ALL], F32)
    xn2 = scratch("xn2", [T_ALL, D + E], F32)
    odds = scratch("odds", [T_ALL, E], F32)
    slots = scratch("slots", [E * CAP], F32)
    qk_t = scratch("qk_t", [2, NB, GROUPS // 2, PARTS, P, S_IMG], BF16)
    qk_a = scratch("qk_a", [2, NB, GROUPS // 2, PARTS, P, S_ALL], BF16)
    attention_layer(nc, "t", False, a["xT"], *(a["t_" + n] for n in ATTENTION), a, qk_t, None, a["txt"], h1,
                    xn1T, following=(a["a_wqk"], a["a_bqk"], qk_a))
    attention_layer(nc, "a", True, xn1T, *(a["a_" + n] for n in ATTENTION), a, qk_a, h1, None, h2, xn2T, xn2,
                    a["router"], odds, projected=True)
    experts_layer(nc, h2, xn2T, xn2, odds, slots, a, out)


def kernel(x, txt, L0_tok_w_qkv, L0_tok_b_qkv, L0_tok_w_out, L0_tok_b_out, L0_attn_W1, L0_attn_b1, L0_attn_W2,
           L0_attn_b2, L0_ffn_router_weight, L0_ffn_e_score_correction_bias, L0_ffn_gate_up_proj, L0_ffn_down_proj,
           L0_ffn_shared_gate, L0_ffn_shared_up, L0_ffn_shared_down):
    import numpy as np
    import concourse.bacc as bacc
    from concourse.bass_utils import run_bass_kernel_spmd

    n = np.asarray
    arrays = {"xT": n(x).reshape(NB * S_IMG, D).T, "txt": n(txt)}
    arrays.update({"t_" + k: v for k, v in attention_inputs(
        n(L0_tok_w_qkv).T, n(L0_tok_b_qkv), n(L0_tok_w_out).T, n(L0_tok_b_out)).items()})
    arrays.update({"a_" + k: v for k, v in attention_inputs(
        n(L0_attn_W1), n(L0_attn_b1), n(L0_attn_W2), n(L0_attn_b2)).items()})
    arrays.update(expert_inputs(n(L0_ffn_router_weight), n(L0_ffn_e_score_correction_bias), n(L0_ffn_gate_up_proj),
                                n(L0_ffn_down_proj), n(L0_ffn_shared_gate), n(L0_ffn_shared_up),
                                n(L0_ffn_shared_down)))
    arrays.update(constants())
    arrays.update(routing_constants())
    arrays = {k: np.ascontiguousarray(v) for k, v in arrays.items()}

    nc = bacc.Bacc("TRN2", target_bir_lowering=False, num_devices=1)
    aps = {k: nc.dram_tensor("in_" + k, v.shape, mybir.dt.from_np(v.dtype), kind="ExternalInput").ap()
           for k, v in arrays.items()}
    out = nc.dram_tensor("out", [T_ALL + CAP, D], F32, kind="ExternalOutput").ap()
    early_fusion(nc, aps, out)
    r = run_bass_kernel_spmd(nc, [{"in_" + k: v for k, v in arrays.items()}], core_ids=[0])
    return r.results[0]["out"][0:T_ALL].reshape(NB, S_ALL, D)
```
